# Optimizing a Trainium2 kernel written in Bass

```python
import numpy as np
import jax
import jax.numpy as jnp

def _softmax(x, axis=-1):
    return jax.nn.softmax(x, axis=axis)

def _gelu(x):
    return jax.nn.gelu(x, approximate=True)

def _silu(x):
    return jax.nn.silu(x)

def _sigmoid(x):
    return jax.nn.sigmoid(x)

def _layernorm(x, axis=-1, eps=1e-05):
    m = jnp.mean(x, axis=axis, keepdims=True)
    v = jnp.var(x, axis=axis, keepdims=True)
    return (x - m) / jnp.sqrt(v + eps)

def _scatter_add(tgt, idx, src, axis=0):
    return tgt.at[idx].add(src)

def _segment_sum(src, seg, n):
    return jax.ops.segment_sum(src, seg, n)
kernel_name = 'mk_early_fusion_d1_tok_img768_r4_a9341c'

def setup_inputs(seed: int=0):
    np.random.seed(seed)
    _w = jnp.asarray

    def _rec_inputs():
        import jax
        import jax.numpy as jnp
        _rk = jax.random.key(seed)
        x = -0.00016672 + 0.999947 * jax.random.normal(jax.random.fold_in(_rk, 1), (32, 3, 96, 96), jnp.float32)
        txt = -0.000218476 + 0.553769 * jax.random.normal(jax.random.fold_in(_rk, 2), (32, 77, 192), jnp.float32)
        return (x, txt)
    x, txt = _rec_inputs()

    def _L0_tok_setup():
        import jax, jax.numpy as jnp
        import numpy as np
        IMAGE_SIZE = 96
        PATCH = 16
        EMBED = 192
        NUM_PATCHES = (IMAGE_SIZE // PATCH) ** 2
        PATCH_DIM = PATCH * PATCH * 3

        def _patchify(x, patch):
            b, c, h, w = x.shape
            nh, nw = (h // patch, w // patch)
            x = x.reshape(b, c, nh, patch, nw, patch)
            x = x.transpose(0, 2, 4, 1, 3, 5)
            return x.reshape(b, nh * nw, c * patch * patch)
        key = jax.random.key(seed)
        k1, k2, k3, k4, k5 = jax.random.split(key, 5)
        x = jax.random.normal(k1, (64, 3, IMAGE_SIZE, IMAGE_SIZE), dtype=jnp.float32)
        W_emb = jax.random.normal(k2, (PATCH_DIM, EMBED), dtype=jnp.float32) * 0.02
        b_emb = jnp.zeros((EMBED,), dtype=jnp.float32)
        pos_embedding = jax.random.normal(k3, (1, NUM_PATCHES + 1, EMBED), dtype=jnp.float32) * 0.02
        cls_token = jax.random.normal(k4, (1, 1, EMBED), dtype=jnp.float32) * 0.02
        return {'x': x, 'W_emb': W_emb, 'b_emb': b_emb, 'pos_embedding': pos_embedding, 'cls_token': cls_token}
    _L0_tok_all = _L0_tok_setup()
    _L0_tok_in = {k: v for k, v in _L0_tok_all.items() if k in ('W_emb', 'b_emb', 'pos_embedding', 'cls_token')}
    del _L0_tok_all

    def _L0_attn_setup():
        import math
        import jax, jax.numpy as jnp
        import numpy as np
        B, N, D_IN, D_OUT = (8, 512, 192, 192)
        key = jax.random.key(seed)
        k1, k2, k3 = jax.random.split(key, 3)
        x = jax.random.normal(k1, (B, N, D_IN), dtype=jnp.float32)
        W_qkv = jax.random.normal(k2, (D_IN, 3 * D_OUT), dtype=jnp.float32) * (1.0 / math.sqrt(D_IN))
        b_qkv = jax.random.normal(k3, (3 * D_OUT,), dtype=jnp.float32) * 0.02
        return {'x': x, 'W_qkv': W_qkv, 'b_qkv': b_qkv}
    _L0_attn_all = _L0_attn_setup()
    _L0_attn_in = {k: v for k, v in _L0_attn_all.items() if k in ('W_qkv', 'b_qkv')}
    del _L0_attn_all

    def _L0_ffn_setup():
        import jax, jax.numpy as jnp
        import numpy as np
        D = 192
        I = 768
        E = 8
        K = 2
        LIMIT = 10.0
        VOCAB = 8192

        def _expert(xf, W1, W2, W3):
            gate = jnp.minimum(xf @ W1, LIMIT)
            up = jnp.clip(xf @ W3, -LIMIT, LIMIT)
            return jax.nn.silu(gate) * up @ W2
        key = jax.random.key(seed)
        ks = jax.random.split(key, 10)
        s = 0.02
        return {'x': jax.random.normal(ks[0], (1, 512, D), dtype=jnp.float32), 'input_ids': jax.random.randint(ks[1], (1, 512), 0, VOCAB, dtype=jnp.int64), 'gate_w': jax.random.normal(ks[2], (D, E), dtype=jnp.float32) * s, 'gate_bias': jnp.zeros((E,), dtype=jnp.float32), 'w1': jax.random.normal(ks[3], (E, D, I), dtype=jnp.float32) * s, 'w2': jax.random.normal(ks[4], (E, I, D), dtype=jnp.float32) * s, 'w3': jax.random.normal(ks[5], (E, D, I), dtype=jnp.float32) * s, 'w1s': jax.random.normal(ks[6], (D, I), dtype=jnp.float32) * s, 'w2s': jax.random.normal(ks[7], (I, D), dtype=jnp.float32) * s, 'w3s': jax.random.normal(ks[8], (D, I), dtype=jnp.float32) * s}
    _L0_ffn_all = _L0_ffn_setup()
    _L0_ffn_in = {k: v for k, v in _L0_ffn_all.items() if k in ('input_ids', 'gate_w', 'gate_bias', 'w1', 'w2', 'w3', 'w1s', 'w2s', 'w3s')}
    del _L0_ffn_all
    return {'x': x, 'txt': txt, 'L0_tok_W_emb': _L0_tok_in['W_emb'], 'L0_tok_b_emb': _L0_tok_in['b_emb'], 'L0_tok_pos_embedding': _L0_tok_in['pos_embedding'], 'L0_tok_cls_token': _L0_tok_in['cls_token'], 'L0_attn_W_qkv': _L0_attn_in['W_qkv'], 'L0_attn_b_qkv': _L0_attn_in['b_qkv'], 'L0_ffn_input_ids': _L0_ffn_in['input_ids'], 'L0_ffn_gate_w': _L0_ffn_in['gate_w'], 'L0_ffn_gate_bias': _L0_ffn_in['gate_bias'], 'L0_ffn_w1': _L0_ffn_in['w1'], 'L0_ffn_w2': _L0_ffn_in['w2'], 'L0_ffn_w3': _L0_ffn_in['w3'], 'L0_ffn_w1s': _L0_ffn_in['w1s'], 'L0_ffn_w2s': _L0_ffn_in['w2s'], 'L0_ffn_w3s': _L0_ffn_in['w3s']}

def reference(x, txt, L0_tok_W_emb, L0_tok_b_emb, L0_tok_pos_embedding, L0_tok_cls_token, L0_attn_W_qkv, L0_attn_b_qkv, L0_ffn_input_ids, L0_ffn_gate_w, L0_ffn_gate_bias, L0_ffn_w1, L0_ffn_w2, L0_ffn_w3, L0_ffn_w1s, L0_ffn_w2s, L0_ffn_w3s):
    import jax
    import jax.numpy as jnp

    def _L0_tok_ref(x, W_emb, b_emb, pos_embedding, cls_token):
        import jax, jax.numpy as jnp
        import numpy as np
        IMAGE_SIZE = 96
        PATCH = 16
        EMBED = 192
        NUM_PATCHES = (IMAGE_SIZE // PATCH) ** 2
        PATCH_DIM = PATCH * PATCH * 3

        def _patchify(x, patch):
            b, c, h, w = x.shape
            nh, nw = (h // patch, w // patch)
            x = x.reshape(b, c, nh, patch, nw, patch)
            x = x.transpose(0, 2, 4, 1, 3, 5)
            return x.reshape(b, nh * nw, c * patch * patch)
        b = x.shape[0]
        patches = _patchify(x, PATCH)
        tok = jnp.einsum('bnd,de->bne', patches, W_emb) + b_emb
        cls = jnp.broadcast_to(cls_token, (b, 1, EMBED))
        tok = jnp.concatenate([cls, tok], axis=1)
        return tok + pos_embedding[:, :tok.shape[1], :]

    def _L0_attn_ref(x, W_qkv, b_qkv):
        import math
        import jax, jax.numpy as jnp
        import numpy as np
        B, N, D_IN, D_OUT = (8, 512, 192, 192)
        d_out = D_OUT
        qkv = jnp.einsum('bnd,de->bne', x, W_qkv) + b_qkv
        q = qkv[:, :, :d_out]
        k = qkv[:, :, d_out:2 * d_out]
        v = qkv[:, :, 2 * d_out:3 * d_out]
        scale = 1.0 / math.sqrt(d_out)
        scores = jnp.einsum('bqd,bkd->bqk', q, k) * scale
        attn = jax.nn.softmax(scores, axis=-1)
        context = jnp.einsum('bqk,bkd->bqd', attn, v)
        return context

    def _L0_ffn_ref(x, input_ids, gate_w, gate_bias, w1, w2, w3, w1s, w2s, w3s):
        import jax, jax.numpy as jnp
        import numpy as np
        D = 192
        I = 768
        E = 8
        K = 2
        LIMIT = 10.0
        VOCAB = 8192

        def _expert(xf, W1, W2, W3):
            gate = jnp.minimum(xf @ W1, LIMIT)
            up = jnp.clip(xf @ W3, -LIMIT, LIMIT)
            return jax.nn.silu(gate) * up @ W2
        B, T, _ = x.shape
        flat = x.reshape(-1, D)
        N = flat.shape[0]
        scores = jnp.sqrt(jax.nn.softplus(flat @ gate_w))
        routed_scores = scores + gate_bias
        _, indices = jax.lax.top_k(routed_scores, K)
        weights = jnp.take_along_axis(scores, indices, axis=1)
        weights = weights / jnp.clip(weights.sum(axis=-1, keepdims=True), 1e-06)
        combine = jnp.zeros((N, E), dtype=weights.dtype)
        combine = combine.at[jnp.arange(N)[:, None], indices].add(weights)
        y = _expert(flat, w1s, w2s, w3s)
        gate_h = jnp.minimum(jnp.einsum('td,edi->eti', flat, w1), LIMIT)
        up_h = jnp.clip(jnp.einsum('td,edi->eti', flat, w3), -LIMIT, LIMIT)
        h = jax.nn.silu(gate_h) * up_h
        out_e = jnp.einsum('eti,eid->etd', h, w2)
        routed = jnp.einsum('etd,te->td', out_e, combine)
        return (y + routed).reshape(B, T, D)
    h = _L0_tok_ref(x, L0_tok_W_emb, L0_tok_b_emb, L0_tok_pos_embedding, L0_tok_cls_token)
    h = jnp.concatenate([h, txt], axis=1)
    h = h + _L0_attn_ref(_layernorm(h, axis=-1), L0_attn_W_qkv, L0_attn_b_qkv)
    h = h + _L0_ffn_ref(_layernorm(h, axis=-1), L0_ffn_input_ids, L0_ffn_gate_w, L0_ffn_gate_bias, L0_ffn_w1, L0_ffn_w2, L0_ffn_w3, L0_ffn_w1s, L0_ffn_w2s, L0_ffn_w3s)
    return h

_drawn_inputs = setup_inputs


def setup_inputs(seed=0):
    import zlib

    import numpy as np

    out = dict(_drawn_inputs(seed))
    spreads = {'L0_tok_b_emb': (0.0, 0.1), 'L0_ffn_gate_bias': (0.0, 2.0)}
    factors = {'L0_tok_cls_token': 2.803, 'L0_ffn_gate_w': 26.45}
    for name, (base, spread) in spreads.items():
        noise = np.random.default_rng([zlib.crc32(name.encode()), seed]).standard_normal(out[name].shape)
        drawn = base * np.exp(spread * noise) if base else spread * noise
        out[name] = jnp.asarray(drawn.astype(out[name].dtype))
    for name, factor in factors.items():
        out[name] = (out[name] * factor).astype(out[name].dtype)
    return out
```

```python
import numpy as np
import concourse.bass as bass
from concourse import mybir
from concourse.bass import ds
from contextlib import ExitStack

F32 = mybir.dt.float32
F16 = mybir.dt.float16
I32 = mybir.dt.int32
U32 = mybir.dt.uint32
ALU = mybir.AluOpType
ACT = mybir.ActivationFunctionType
AX = mybir.AxisListType


def early_fusion_layer(nc: bass.Bass, x, txt, w_emb, b_emb, pos, cls, w_qkv, b_qkv, gate_w, gate_bias,
                       w1, w2, w3, w1s, w2s, w3s, out):
    NS, CH, IMG, _ = x.shape
    NW, D = txt.shape[1], txt.shape[2]
    PATCH = 16
    SIDE = IMG // PATCH
    NP = SIDE * SIDE
    T = NP + 1 + NW
    NE, _, FI = w1.shape
    TOPK = 2
    DM, DT = 128, D - 128
    KC = CH * PATCH * PATCH // 128
    IC = FI // 128
    EPS = 1e-5
    SCALE = float(D) ** -0.5
    LIMIT = 10.0
    SILU_LIMIT = float(LIMIT / (1.0 + np.exp(-LIMIT)))
    G = 4
    NG = NS // G
    XSC = 2.0 ** 11
    HSC = 2.0 ** 9

    HALF = NS // 2
    PA = -(-HALF * T // 128)
    PR = (NS * T * TOPK + NE * 127) // 128
    NPOS = PA + PR + PA
    GAP = PA * 128 - HALF * T

    xrows = nc.dram_tensor("xrows", [2 * PA * 128, 2 * D], F16).ap()
    yshared = nc.dram_tensor("yshared", [2 * PA * 128, D], F32).ap()
    yrouted = nc.dram_tensor("yrouted", [PR * 128, D], F32).ap()
    slot_token = nc.dram_tensor("slot_token", [128 * PR, 1], I32).ap()

    ctx = ExitStack()
    with ctx:
        def sb(name, shape, dt=F32):
            return ctx.enter_context(nc.sbuf_tensor(name, shape, dt))

        def sem(name):
            return ctx.enter_context(nc.semaphore(name))

        WU = 3 * FI
        WE = 2 * WU + 2 * IC * D
        W16 = sb("W16", [128, (NE + 1) * WE], F16)
        h = sb("h", [128, NS, D])
        identf = sb("identf", [128, 128])
        ident16 = sb("ident16", [128, 128], F16)
        before = sb("before", [128, 128], F16)
        ones16 = sb("ones16", [128, 128], F16)
        wscale = sb("wscale", [128, 3 * (NE + 1)])
        winv = sb("winv", [128, 3 * (NE + 1)])
        logits = sb("logits", [128, NS * NE])
        mhalf = sb("mhalf", [128, G])
        gbias = sb("gbias", [128, NE])
        btab = sb("btab", [128, NPOS + 2], I32)
        bscale = sb("bscale", [128, 5, NPOS + 2])
        token_slot = sb("token_slot", [128, NS], I32)

        ARENA = 13200
        arena = sb("arena", [128, ARENA])

        def carve(at, cols, dt=F32):
            words = cols if dt != F16 else (cols + 1) // 2
            ap = arena[:, at:at + words]
            assert at + words <= ARENA, (at, words, ARENA)
            return (ap if dt == F32 else ap.bitcast(dt)), at + words

        o = 0
        wq_m, o = carve(o, 3 * D)
        wq_t, o = carve(o, 3 * D)
        bv, o = carve(o, D)
        gw_m, o = carve(o, NE)
        gw_t, o = carve(o, NE)
        bq, o = carve(o, 4)
        bqs, o = carve(o, 2)
        stats, o = carve(o, 6 * G)
        mv1, o = carve(o, 2 * G)
        rstd1, o = carve(o, G)
        mv2, o = carve(o, 2 * G)
        rstd2, o = carve(o, G)
        negmax, o = carve(o, G)
        rowsum, o = carve(o, 2 * G)
        rinv, o = carve(o, G)
        amax, o = carve(o, 2)
        amaxall, o = carve(o, 2)
        bits, o = carve(o, 2)
        xn, o = carve(o, G * D)
        xnT, o = carve(o, 2 * G * T)
        qk, o = carve(o, 4 * G * T)
        v, o = carve(o, 2 * G * D)
        prob, o = carve(o, G * T)
        probT, o = carve(o, G * T)
        xs, o = carve(o, 2 * G * D)
        rows, o = carve(o, G * 2 * D, F16)
        stage, o = carve(o, 2 * 2 * FI)
        xn = xn.rearrange("p (g d) -> p g d", g=G)
        xnT = xnT.rearrange("p (m c) -> p m c", m=2)
        qk = qk.rearrange("p (m c) -> p m c", m=4)
        v = v.rearrange("p (r g d) -> p r g d", r=2, g=G)
        xs = xs.rearrange("p (r g d) -> p r g d", r=2, g=G)
        rows = rows.rearrange("p (g d) -> p g d", g=G)
        stage = stage.rearrange("p (r c) -> p r c", r=2)
        xsT = sb("xsT", [128, 2, G * T])

        EMB = WE
        emb = W16[:, EMB:NE * WE].bitcast(F32)
        xin = emb[:, 0:2 * CH * PATCH * IMG].rearrange("p (f c w) -> p f c w", f=2, c=CH)
        e0 = 2 * CH * PATCH * IMG
        patchT = emb[:, e0:e0 + KC * NS * NP].rearrange("p (k c) -> p k c", k=KC)
        e0 += KC * NS * NP
        wemb = emb[:, e0:e0 + KC * D].rearrange("p (k d) -> p k d", k=KC)
        e0 += KC * D
        EQ = 8
        NQ = NS // EQ
        tokT = emb[:, e0:e0 + 2 * 2 * EQ * NP].rearrange("p (r m c) -> p r m c", r=2, m=2)
        e0 += 2 * 2 * EQ * NP
        posb = emb[:, e0:e0 + D]
        bembb = emb[:, e0 + D:e0 + 2 * D]
        row0 = emb[:, e0 + 2 * D:e0 + 5 * D]
        zrow = emb[:, e0 + 5 * D:e0 + 6 * D].bitcast(F16)
        e0 += 6 * D
        xpatch = emb[:, e0:e0 + CH * PATCH * IMG].rearrange("p (c w v) -> p c w v", c=CH, w=SIDE)
        assert e0 + CH * PATCH * IMG <= (NE * WE - EMB) // 2

        o = 0
        xrow, o = carve(o, 2 * 2 * D, F16)
        xT, o = carve(o, 2 * 4 * 128, F16)
        HC = IC // 2
        HW_ = HC * 128
        act_s, o = carve(o, 2 * HW_)
        act_t, o = carve(o, 2 * HW_)
        act_h, o = carve(o, 2 * HW_)
        hhi, o = carve(o, 4 * HW_, F16)
        hlo, o = carve(o, 4 * HW_, F16)
        ysb, o = carve(o, 2 * D)
        yin, o = carve(o, 4 * 3 * D)
        gidx, o = carve(o, 2)
        tidx, o = carve(o, 8)
        xrow = xrow.rearrange("p (r c) -> p r c", r=2)
        xT = xT.rearrange("p (r k c) -> p r k c", r=2, k=4)
        act_s = act_s.rearrange("p (r c) -> p r c", r=2)
        act_t = act_t.rearrange("p (r c) -> p r c", r=2)
        act_h = act_h.rearrange("p (r c) -> p r c", r=2)
        hhi = hhi.rearrange("p (q r c) -> p q r c", q=2, r=2)
        hlo = hlo.rearrange("p (q r c) -> p q r c", q=2, r=2)
        ysb = ysb.rearrange("p (r c) -> p r c", r=2)
        yin = yin.rearrange("p (t k d) -> p t k d", t=4, k=3)
        gidx = gidx.bitcast(U32)
        tidx = tidx.bitcast(U32)
        NR = NS * NE
        rt = []
        for _ in range(7):
            a, o = carve(o, NR)
            rt.append(a)
        best, o = carve(o, 8 * NS)
        best = best.rearrange("p (k t) -> p k t", k=8)
        mask16, o = carve(o, NR, F16)
        small, o = carve(o, 6 * NE)
        small = small.rearrange("p (k e) -> p k e", k=6)
        blk, o = carve(o, 2 * PR)
        blk = blk.rearrange("p (k b) -> p k b", k=2)
        ids, o = carve(o, PR)
        ids = ids.bitcast(I32)
        slots, o = carve(o, 2 * NS)
        slots = slots.bitcast(I32).rearrange("p (k t) -> p k t", k=2)
        pidx, o = carve(o, 2 * NS)
        pidx = pidx.bitcast(I32).rearrange("p (k t) -> p k t", k=2)
        tmpi, o = carve(o, 2 * NS)
        tmpi = tmpi.bitcast(I32).rearrange("p (k t) -> p k t", k=2)
        wts = sb("wts", [128, 2, NS])
        rankof = sb("rankof", [128, NE])
        iotab = sb("iotab", [128, PR])

        banks = ctx.enter_context(nc.psum_tensor("banks", [128, 8, 512], F32))

        const_ready = sem("const_ready")
        wemb_in, x_in0, x_in1, pos_in, txt_in, wq_in, gate_in = map(
            sem, ("wemb_in", "x_in0", "x_in1", "pos_in", "txt_in", "wq_in", "gate_in"))
        cls_sum, cls_row, pos_sum = sem("cls_sum"), sem("cls_row"), sem("pos_sum")
        x_patch = sem("x_patch")
        patch_t, patch_a, patch_v = sem("patch_t"), sem("patch_a"), sem("patch_v")
        emb_done, tok_a, tok_v = sem("emb_done"), sem("tok_a"), sem("tok_v")
        tok_t, tok_h = sem("tok_t"), sem("tok_h")
        stage_in = [sem("stage_in0"), sem("stage_in1")]
        w_amax, w_all, w_scale, w_hi, w_lo = map(sem, ("w_amax", "w_all", "w_scale", "w_hi", "w_lo"))
        dve_link, act_link = sem("dve_link"), sem("act_link")
        mv1_ready, rstd1_ready, xn_ready = sem("mv1_ready"), sem("rstd1_ready"), sem("xn_ready")
        mv2_ready, rstd2_ready, xs_ready = sem("mv2_ready"), sem("rstd2_ready"), sem("xs_ready")
        pool_link = sem("pool_link")
        tr_full, tr_free = sem("tr_full"), sem("tr_free")
        qk_full, qk_free = sem("qk_full"), sem("qk_free")
        vc_full, vc_free = sem("vc_full"), sem("vc_free")
        s_full, max_ready, exp_done = sem("s_full"), sem("max_ready"), sem("exp_done")
        hi_ready, lo_ready, rows_out = sem("hi_ready"), sem("lo_ready"), [sem("rows_out0"), sem("rows_out1")]
        zero_out, idz_out = sem("zero_out"), sem("idz_out")
        e_abs, e_exp, mask_ready, rank_done, slots_ready, btab_ready = map(
            sem, ("e_abs", "e_exp", "mask_ready", "rank_done", "slots_ready", "btab_ready"))
        btab_shared = sem("btab_shared")
        ids_out, ids_in = sem("ids_out"), sem("ids_in")
        xrow_in = [sem("xrow_in0"), sem("xrow_in1")]
        xrow_got = [sem("xrow_got0"), sem("xrow_got1")]
        xt_full, xt_ready = sem("xt_full"), sem("xt_ready")
        gu_full, g_used, u_used = sem("gu_full"), sem("g_used"), sem("u_used")
        silu_ready, clamp_ready, hid_ready = sem("silu_ready"), sem("clamp_ready"), sem("hid_ready")
        hhi_ready, hlo_ready = sem("hhi_ready"), sem("hlo_ready")
        y_full, y_ready = sem("y_full"), sem("y_ready")
        y_out = [sem("y_out0"), sem("y_out1")]
        gidx_ready, tidx_ready = sem("gidx_ready"), sem("tidx_ready")
        yin_in = [sem(f"yin_in{k}") for k in range(4)]
        yin_got = [sem(f"yin_got{k}") for k in range(4)]
        ysum1, ysum2, tile_done = sem("ysum1"), sem("ysum2"), sem("tile_done")
        out_done = sem("out_done")

        UNITS = [(e, m) for e in [NE] + list(range(NE)) for m in range(3)]
        NU = len(UNITS)
        UCOLS = [2 * FI, 2 * FI, IC * D]
        SHARED_W = [w1s, w3s, w2s]
        ROUTED_W = [w1, w3, w2]
        UNITS_EMB = 6

        def units_at(g):
            left = NU - UNITS_EMB
            return range(UNITS_EMB + left * g // NG, UNITS_EMB + left * (g + 1) // NG)

        def w_at(e, m):
            return e * WE + m * WU

        def stage_full(u):
            return sum(16 if UNITS[k][1] == 2 else 48 for k in range(u % 2, u + 1, 2))

        TR = [("xm", 0), ("xt", 0)]
        for g in range(NG + 2):
            if g + 1 < NG:
                TR += [("xm", g + 1), ("xt", g + 1)]
            if 0 <= g - 1 < NG:
                TR += [("p", g - 1)]
            if 0 <= g - 2 < NG:
                TR += [("sm", g - 2), ("st", g - 2), ("gate", g - 2)]
        TRNO = {u: n for n, u in enumerate(TR)}
        VC = []
        for g in range(NG + 1):
            if g < NG:
                VC += [("v", g, 0), ("v", g, 1)]
            if g >= 1:
                VC += [("c", g - 1, 0), ("c", g - 1, 1)]
        VCNO = {u: n for n, u in enumerate(VC)}

        NPT = 2 * KC * 2
        block = ctx.enter_context(nc.Block())

        @block.sync
        def _(sp):
            def load_unit(u):
                e, m = UNITS[u]
                if u >= 2:
                    sp.wait_ge(w_lo, u - 1)
                src = SHARED_W[m] if e == NE else ROUTED_W[m][e]
                done = stage_in[u % 2]
                if m < 2:
                    sp.dma_start(stage[:, u % 2, 0:FI], src[0:DM, :]).then_inc(done, 16)
                    for part in range(2):
                        sp.dma_start(stage[64 * part:64 * part + 64, u % 2, FI:2 * FI], src[DM:D, :]).then_inc(done, 16)
                else:
                    sp.dma_start(stage[:, u % 2, 0:IC * D].rearrange("p (c d) -> p c d", c=IC),
                                 src.rearrange("(c p) d -> p c d", p=128)).then_inc(done, 16)

            sp.dma_start(row0[0:1, 0:D], pos[0, 0:1, :]).then_inc(pos_in, 16)
            sp.dma_start(row0[0:1, D:2 * D], cls[0, :, :]).then_inc(pos_in, 16)
            sp.dma_start(posb[0:NP, :], pos[0, 1:NP + 1, :]).then_inc(pos_in, 16)
            sp.dma_start(bembb[0:NP, :], b_emb.partition_broadcast(NP)).then_inc(pos_in, 16)
            for f in range(2):
                for b in range(NS // 2):
                    eng = sp
                    eng.dma_start(xin[SIDE * b:SIDE * b + SIDE, f, :, :],
                                  x[f * (NS // 2) + b].rearrange("c (n y) w -> n c (y w)", n=SIDE)
                                  ).then_inc(x_in0 if f == 0 else x_in1, 16)
                if f == 0:
                    sp.dma_start(wemb, w_emb.rearrange("(k p) d -> p k d", p=128)).then_inc(wemb_in, 16)
                    load_unit(0)
                    load_unit(1)
            sp.dma_start(h[NP + 1:T, :, :], txt.rearrange("b t d -> t b d")).then_inc(txt_in, 16)
            sp.dma_start(wq_m, w_qkv[0:DM, :]).then_inc(wq_in, 16)
            sp.dma_start(wq_t[0:DT, :], w_qkv[DM:D, :]).then_inc(wq_in, 16)
            sp.dma_start(bv[0:T, :], b_qkv[2 * D:3 * D].partition_broadcast(T)).then_inc(wq_in, 16)
            for k in range(2):
                b1 = b_qkv[k * D:(k + 1) * D].rearrange("(p a) -> p a", a=1)
                sp.dma_start(bq[:, 2 * k:2 * k + 1], b1[0:DM, :]).then_inc(wq_in, 16)
                sp.dma_start(bq[0:DT, 2 * k + 1:2 * k + 2], b1[DM:D, :]).then_inc(wq_in, 16)
            sp.dma_start(gw_m, gate_w[0:DM, :]).then_inc(gate_in, 16)
            sp.dma_start(gw_t[0:DT, :], gate_w[DM:D, :]).then_inc(gate_in, 16)
            sp.dma_start(gbias[0:T, :], gate_bias.partition_broadcast(T)).then_inc(gate_in, 16)
            sp.wait_ge(cls_sum, 1)
            sp.dma_start(h[NP:NP + 1, :, :], row0[0:1, 2 * D:3 * D].unsqueeze(1).to_broadcast([1, NS, D])
                         ).then_inc(cls_row, 16)
            sp.wait_ge(const_ready, 3)
            sp.dma_start(xrows[HALF * T:PA * 128, :], zrow[0:GAP, :]).then_inc(zero_out, 16)
            sp.dma_start(xrows[PA * 128 + HALF * T:2 * PA * 128, :], zrow[0:GAP, :]).then_inc(zero_out, 16)
            sp.dma_start(slot_token.rearrange("(p b) a -> p (b a)", p=128), zrow[:, 0:2 * PR].bitcast(I32)
                         ).then_inc(idz_out, 16)
            for u in range(2, UNITS_EMB + 1):
                load_unit(u)

            def store_rows(g):
                sp.wait_ge(hi_ready, g + 1)
                sp.wait_ge(lo_ready, g + 1)
                at = g * G * T + (GAP if g >= NG // 2 else 0)
                sp.dma_start(xrows[at:at + G * T, :].rearrange("(g t) d -> t g d", g=G), rows[0:T, :, :]
                             ).then_inc(rows_out[g % 2], 16)

            for g in range(NG + 2):
                if g < NG:
                    for u in units_at(g):
                        if u + 1 < NU:
                            load_unit(u + 1)
                if g >= 2:
                    store_rows(g - 2)

            for k in range(2):
                sp.wait_ge(rows_out[k], 16 * (NG // 2))
            sp.wait_ge(zero_out, 32)

            def load_rows(c, i=0):
                if c >= 2:
                    sp.wait_ge(xt_full, c - 1 + 2 * i)
                sp.dma_start(xrow[:, c % 2, :], xrows[ds((c + 2 * i) * 128, 128), :]).then_inc(xrow_in[c % 2], 16)

            def store_y(c, i=0):
                sp.wait_ge(y_ready, c + 1 + 2 * i)
                if PA <= c < PA + PR:
                    rows_of_y = yrouted[ds((c - PA + 2 * i) * 128, 128), :]
                else:
                    rows_of_y = yshared[ds((c - (PR if c >= PA else 0) + 2 * i) * 128, 128), :]
                sp.dma_start(rows_of_y, ysb[:, c % 2, :]).then_inc(y_out[c % 2], 16)

            for c in range(4):
                load_rows(c)
            with sp.Fori(0, (PA - 5) // 2) as i:
                for s in range(2):
                    load_rows(4 + s, i)
                    store_y(s, i)
            load_rows(PA - 1)
            store_y(PA - 5)
            for c in range(PA - 4, PA):
                store_y(c)
            with sp.Fori(0, (PR - 2) // 2) as i:
                for s in range(2):
                    store_y(PA + s, i)

            def load_y(t, k, gap):
                sp.wait_ge(tile_done, t - 3)
                sp.dma_start(yin[0:T, k, 0, :], yshared[ds(t * T + gap, T), :]).then_inc(yin_in[k], 16)

            def store_out(t):
                sp.wait_ge(tile_done, t + 4)
                src = h[:, ds(t, 4), :]
                dst = out[ds(t, 4), :, :]
                sp.dma_start(dst[:, 1:NP + 1, :].rearrange("b t d -> t b d"), src[0:NP, :, :]).then_inc(out_done, 16)
                sp.dma_start(dst[:, 0:1, :].rearrange("b t d -> t b d"), src[NP:NP + 1, :, :]).then_inc(out_done, 16)
                sp.dma_start(dst[:, NP + 1:T, :].rearrange("b t d -> t b d"), src[NP + 1:T, :, :]).then_inc(out_done, 16)

            def y_stored(c, i=0):
                sp.wait_ge(y_out[0], 16 * (c // 2 + 1 + i))
                sp.wait_ge(y_out[1], 16 * ((c - 1) // 2 + 1 + i))

            L0 = PA + PR - 2
            store_y(L0)
            store_y(L0 + 1)
            y_stored(L0 + 1)
            for k in range(4):
                sp.dma_start(yin[0:T, k, 0, :], yshared[k * T:(k + 1) * T, :]).then_inc(yin_in[k], 16)
            NJ = (PA - 1) // 2
            with sp.Fori(1, NJ) as j:
                for s in range(2):
                    store_y(L0 + 2 + s, j - 1)
                y_stored(L0 + 1, j)
                for k in range(4):
                    load_y(4 * j + k, k, (j // 4) * GAP)
                store_out(4 * (j - 1))
            for c in range(L0 + 2 * NJ, NPOS):
                store_y(c)
            sp.wait_ge(y_out[0], 16 * ((NPOS + 1) // 2))
            sp.wait_ge(y_out[1], 16 * (NPOS // 2))
            for t in range(4 * NJ, NS):
                load_y(t, t % 4, GAP)
            for t in range(4 * (NJ - 1), NS, 4):
                store_out(t)
            sp.wait_ge(out_done, 48 * NS // 4)

        def patches_apart(eng, copy, f, c):
            eng.wait_ge(x_in0 if f == 0 else x_in1, 16 * HALF)
            if f == 1:
                eng.wait_ge(patch_t, NPT // 2)
            P = SIDE * HALF
            copy(xpatch[0:P, c, :, :].rearrange("p w (y v) -> p w y v", v=PATCH),
                 xin[0:P, f, c, :].rearrange("p (y w v) -> p w y v", w=SIDE, v=PATCH)).then_inc(x_patch, 1)

        @block.gpsimd
        def _(pool):
            IO = bass.IndirectOffsetOnAxis
            links = [0]

            def link(ins):
                links[0] += 1
                ins.then_inc(pool_link, 1)
                pool.wait_ge(pool_link, links[0])

            pool.memset(identf[:, :], 0.0).then_inc(pool_link, 1)
            pool.memset(ident16[:, :], 0.0).then_inc(pool_link, 1)
            links[0] = 2
            link(pool.memset(ones16[:, :], 1.0))
            for m in (identf, ident16):
                pool.affine_select(out=m[:, :], in_=m[:, :], compare_op=ALU.not_equal, fill=1.0, base=0,
                                   pattern=[[-1, 128]], channel_multiplier=1).then_inc(const_ready, 1)
            pool.memset(zrow[:, :], 0.0).then_inc(const_ready, 1)
            pool.affine_select(out=before[:, :], in_=ones16[:, :], compare_op=ALU.is_gt, fill=0.0, base=0,
                               pattern=[[1, 128]], channel_multiplier=-1).then_inc(const_ready, 1)
            pool.memset(mhalf[:, :], -0.5).then_inc(const_ready, 1)
            pool.iota(rankof[:, :], pattern=[[-1, NE]], base=NE, channel_multiplier=0,
                      allow_small_or_imprecise_dtypes=True).then_inc(const_ready, 1)
            pool.iota(iotab[:, :], pattern=[[1, PR]], base=0, channel_multiplier=0,
                      allow_small_or_imprecise_dtypes=True).then_inc(const_ready, 1)
            pool.iota(token_slot[:, :], pattern=[[HALF * T + GAP, 2], [T, HALF]], base=0,
                      channel_multiplier=1).then_inc(const_ready, 1)
            pool.iota(btab[:, :], pattern=[[0, NPOS + 2]], base=NE, channel_multiplier=0).then_inc(const_ready, 1)
            pool.wait_ge(const_ready, 9)

            def unit_max(u):
                pool.wait_ge(w_amax, u + 1)
                pool.partition_all_reduce(amaxall[:, u % 2:u % 2 + 1], amax[:, u % 2:u % 2 + 1], 128,
                                          bass.bass_isa.ReduceOp.max).then_inc(w_all, 1)

            def rstd(mv, r, ready, done, g):
                pool.wait_ge(ready, g + 1)
                link(pool.tensor_scalar(r[0:T, :], mv[0:T, :].rearrange("p (g k) -> p g k", k=2)[:, :, 1],
                                        1.0, EPS, ALU.mult, ALU.add))
                pool.tensor_tensor(r[0:T, :], r[0:T, :], mhalf[0:T, :], ALU.pow).then_inc(done, 1)

            patches_apart(pool, pool.tensor_copy, 0, 2)
            unit_max(0)
            unit_max(1)
            patches_apart(pool, pool.tensor_copy, 1, 2)
            unit_max(2)
            unit_max(3)
            for g in range(2):
                rstd(mv1, rstd1, mv1_ready, rstd1_ready, g)
                unit_max(4 + g)
            for g in range(NG + 2):
                units = list(units_at(g)) if g < NG else []
                if units:
                    unit_max(units[0])
                if 1 <= g <= NG:
                    rstd(mv2, rstd2, mv2_ready, rstd2_ready, g - 1)
                if units[1:]:
                    unit_max(units[1])
                if g + 2 < NG:
                    rstd(mv1, rstd1, mv1_ready, rstd1_ready, g + 2)
                if units[2:]:
                    unit_max(units[2])
                if g >= 2:
                    pool.wait_ge(hi_ready, g - 1)
                    pool.tensor_tensor(rows[0:T, :, D:2 * D], xs[0:T, g % 2, :, :], rows[0:T, :, 0:D],
                                       ALU.subtract).then_inc(lo_ready, 1)

            pool.wait_ge(slots_ready, 1)
            pool.wait_ge(idz_out, 16)
            for t in range(NS):
                for k in range(TOPK):
                    pool.indirect_dma_start(out=slot_token, out_offset=IO(pidx.bitcast(U32)[0:T, k, t:t + 1], 0),
                                            in_=token_slot[0:T, t:t + 1], in_offset=None).then_inc(ids_out, 16)
            pool.wait_ge(ids_out, 16 * NS * TOPK)
            pool.dma_start(ids, slot_token.rearrange("(p b) a -> p (b a)", p=128)).then_inc(ids_in, 16)
            pool.wait_ge(ids_in, 16)
            for k in range(2):
                pool.wait_ge(rows_out[k], 16 * (NG // 2))
            pool.wait_ge(zero_out, 32)

            def gather_rows(c, i=0):
                q = c % 2
                pool.wait_ge(xt_full, c - 1 + 2 * i)
                pool.tensor_copy(gidx[:, q:q + 1], ids.bitcast(U32)[:, ds(c - PA + 2 * i, 1)]).then_inc(gidx_ready, 1)
                pool.compute_val(c - PA + 1 + 2 * i)
                pool.wait_ge(ids_in, 16)
                pool.wait_ge(gidx_ready, c - PA + 1 + 2 * i)
                pool.indirect_dma_start(out=xrow[:, q, :], out_offset=None, in_=xrows,
                                        in_offset=IO(gidx[:, q:q + 1], 0)).then_inc(xrow_got[q], 16)

            def load_rows(c, i=0):
                pool.wait_ge(xt_full, c - 1 + 2 * i)
                pool.dma_start(xrow[:, c % 2, :], xrows[ds((c - PR + 2 * i) * 128, 128), :]
                               ).then_inc(xrow_got[c % 2], 16)

            def gather_y(t, k):
                pool.tensor_copy(tidx[0:T, 2 * k:2 * k + 2], slots.bitcast(U32)[0:T, :, ds(t, 1)]
                                 .rearrange("p k a -> p (k a)")).then_inc(tidx_ready, 1)
                pool.compute_val(t + 1)
                pool.wait_ge(slots_ready, 1)
                pool.wait_ge(tidx_ready, t + 1)
                for n in range(TOPK):
                    pool.indirect_dma_start(out=yin[0:T, k, 1 + n, :], out_offset=None, in_=yrouted,
                                            in_offset=IO(tidx[0:T, 2 * k + n:2 * k + n + 1], 0)).then_inc(yin_got[k], 16)

            with pool.Fori(0, PR // 2) as i:
                for s in range(2):
                    gather_rows(PA + s, i)
            load_rows(PA + PR)
            for s in range(2):
                load_rows(PA + PR + 1 + s)
            pool.wait_ge(y_out[0], 16 * ((PA + PR + 1) // 2))
            pool.wait_ge(y_out[1], 16 * ((PA + PR) // 2))
            for k in range(4):
                gather_y(k, k)
            NJ = (PA - 1) // 2
            with pool.Fori(1, NJ) as j:
                for s in range(2):
                    load_rows(PA + PR + 1 + s, j)
                for k in range(4):
                    pool.wait_ge(tile_done, 4 * j + k - 3)
                    gather_y(4 * j + k, k)
            for t in range(4 * NJ, NS):
                pool.wait_ge(tile_done, t - 3)
                gather_y(t, t % 4)

        def use_ready(eng, kind, g):
            eng.wait_ge(tr_full, TRNO[kind, g] + 1)
            return 5 + TRNO[kind, g] % 3

        @block.scalar
        def _(act):
            def unit_hi(u):
                e, m = UNITS[u]
                act.wait_ge(w_scale, u + 1)
                n = UCOLS[m]
                at = w_at(e, m)
                act.activation(W16[:, at:at + n], stage[:, u % 2, 0:n], ACT.Copy,
                               scale=wscale[:, 3 * e + m:3 * e + m + 1]).then_inc(w_hi, 1)

            def patch_evac(n):
                f, k, w3 = n // (2 * KC), n % (2 * KC) // 2, n % 2
                act.wait_ge(patch_t, n + 1)
                dst = patchT[:, k, f * HALF * NP:(f + 1) * HALF * NP].rearrange("p (r w) -> p w r", w=SIDE)
                act.activation(dst[:, 3 * w3:3 * w3 + 3, :],
                               banks[:, 0, 0:3 * SIDE * HALF].rearrange("p (w r) -> p w r", w=3),
                               ACT.Copy).then_inc(patch_a, 1)

            def tok_evac(q):
                act.wait_ge(emb_done, 2 * q + 1)
                if q >= 2:
                    act.wait_ge(tok_t, 4 * (q - 1))
                act.activation(tokT[:, q % 2, 0, :], banks[:, 3 + 2 * (q % 2), 0:EQ * NP], ACT.Copy).then_inc(tok_a, 1)

            act.preload_act_table(ACT.Exp)
            patches_apart(act, act.copy, 0, 1)
            for n in range(0, NPT // 2, 2):
                patch_evac(n)
            unit_hi(0)
            unit_hi(1)
            tok_evac(0)
            tok_evac(1)
            patches_apart(act, act.copy, 1, 1)
            for n in range(NPT // 2, NPT, 2):
                patch_evac(n)
            unit_hi(2)
            unit_hi(3)
            tok_evac(2)
            tok_evac(3)
            act.wait_ge(wq_in, 16 * 7)
            act.mul(bqs[:, 0:1], bq[:, 0:1], SCALE).then_inc(act_link, 1)
            act.mul(bqs[0:DT, 1:2], bq[0:DT, 1:2], SCALE).then_inc(act_link, 1)
            act.wait_ge(act_link, 2)
            unit_hi(4)
            unit_hi(5)

            def xn_evac(g):
                if g >= 1:
                    act.wait_ge(vc_full, VCNO["v", g - 1, 1] + 1)
                bank = use_ready(act, "xm", g)
                act.activation(xnT[:, 0, :], banks[:, bank, 0:G * T], ACT.Copy).then_inc(tr_free, 1)
                bank = use_ready(act, "xt", g)
                act.activation(xnT[0:DT, 1, :], banks[0:DT, bank, 0:G * T], ACT.Copy).then_inc(tr_free, 1)

            xn_evac(0)
            for g in range(NG + 2):
                units = list(units_at(g)) if g < NG else []
                if g < NG:
                    if g >= 1:
                        act.wait_ge(s_full, g)
                    for m in range(4):
                        act.wait_ge(qk_full, 4 * g + m + 1)
                        n = DT if m % 2 else DM
                        if m < 2:
                            act.activation(qk[0:n, m, :], banks[0:n, m % 2, 0:G * T], ACT.Identity, scale=SCALE,
                                           bias=bqs[0:n, m:m + 1]).then_inc(qk_free, 1)
                        else:
                            act.activation(qk[0:n, m, :], banks[0:n, m % 2, 0:G * T], ACT.Identity,
                                           bias=bq[0:n, m:m + 1]).then_inc(qk_free, 1)
                if units:
                    unit_hi(units[0])
                if g + 1 < NG:
                    xn_evac(g + 1)
                if 1 <= g <= NG:
                    bank = use_ready(act, "p", g - 1)
                    if g >= 2:
                        act.wait_ge(vc_full, VCNO["c", g - 2, 1] + 1)
                    act.activation(probT[0:T, :], banks[0:T, bank, 0:G * T], ACT.Copy).then_inc(tr_free, 1)
                if units[1:]:
                    unit_hi(units[1])
                if g >= 2:
                    act.wait_ge(xs_ready, g - 1)
                    if g >= 3:
                        act.wait_ge(rows_out[(g - 3) % 2], 16 * ((g - 3) // 2 + 1))
                    act.activation(rows[0:T, :, 0:D], xs[0:T, g % 2, :, :], ACT.Copy).then_inc(hi_ready, 1)
                if g < NG:
                    act.wait_ge(max_ready, g + 1)
                    for s in range(G):
                        act.activation(prob[0:T, s * T:(s + 1) * T], banks[0:T, 4, s * T:(s + 1) * T], ACT.Exp,
                                       bias=negmax[0:T, s:s + 1],
                                       accum_out=rowsum[0:T, G * (g % 2) + s:G * (g % 2) + s + 1]).then_inc(exp_done, 1)
                if units[2:]:
                    unit_hi(units[2])
                if g >= 2:
                    bank = use_ready(act, "sm", g - 2)
                    act.activation(xsT[:, 0, :], banks[:, bank, 0:G * T], ACT.Copy).then_inc(tr_free, 1)
                    bank = use_ready(act, "st", g - 2)
                    act.activation(xsT[0:DT, 1, :], banks[0:DT, bank, 0:G * T], ACT.Copy).then_inc(tr_free, 1)
                    bank = use_ready(act, "gate", g - 2)
                    act.activation(logits[0:T, (g - 2) * G * NE:(g - 1) * G * NE], banks[0:T, bank, 0:G * NE],
                                   ACT.Copy, scale=1.0 / XSC).then_inc(tr_free, 1)

            act.wait_ge(e_abs, 1)
            act.activation(rt[1][0:T, :], rt[0][0:T, :], ACT.Exp).then_inc(e_exp, 1)
            act.preload_act_table(ACT.Silu)

            def xt_evac(c, i=0):
                act.wait_ge(xt_full, c + 1 + 2 * i)
                act.activation(xT[:, c % 2, :, :], banks[:, 6 + c % 2, 0:256].bitcast(F16)
                               .rearrange("p (k c) -> p k c", k=4), ACT.Copy).then_inc(xt_ready, 1)

            def y_evac(c, i=0):
                act.wait_ge(y_full, c + 1 + 2 * i)
                if c >= 2:
                    act.wait_ge(y_out[c % 2], 16 * (c // 2 + i))
                act.activation(ysb[:, c % 2, :], banks[:, 4 + c % 2, 0:D], ACT.Copy,
                               scale=bscale[:, 4, ds(c + 2 * i, 1)]).then_inc(y_ready, 1)

            def step(c, i=0):
                for r in range(2):
                    n = 2 * c + r + 4 * i if type(i) is not int else 2 * c + r
                    if r and type(i) is not int:
                        act.compute_val(n + 1)
                        act.wait_ge(e_exp, 1)
                    act.wait_ge(gu_full, n + 1)
                    act.activation(act_s[:, r, :], banks[:, r, 0:HW_], ACT.Silu,
                                   scale=bscale[:, 0, ds(c + 2 * i, 1)]).then_inc(silu_ready, 1)
                    if r == 0:
                        if c + 1 < NPOS:
                            xt_evac(c + 1, i)
                        if c >= 2:
                            y_evac(c - 2, i)
                    if r:
                        act.wait_ge(e_exp, 1)
                    act.wait_ge(hid_ready, n + 1)
                    act.activation(hhi[:, c % 2, r, :], act_h[:, r, :], ACT.Copy,
                                   scale=bscale[:, 3, ds(c + 2 * i, 1)]).then_inc(hhi_ready, 1)

            act.wait_ge(btab_shared, 1)
            xt_evac(0)
            step(0)
            step(1)
            with act.Fori(0, (PA - 3) // 2) as i:
                for s in range(2):
                    step(2 + s, i)
            step(PA - 1)
            act.wait_ge(btab_ready, 1)
            with act.Fori(0, PR // 2) as i:
                for s in range(2):
                    step(PA + s, i)
            with act.Fori(0, (PA - 1) // 2) as i:
                for s in range(2):
                    step(PA + PR + s, i)
            step(NPOS - 1)
            y_evac(NPOS - 2)
            y_evac(NPOS - 1)

        @block.tensor
        def _(pe):
            pe.wait_ge(const_ready, 1)

            def patch_transposes(f):
                pe.wait_ge(x_patch, CH * (f + 1))
                for n in range(f * 2 * KC, (f + 1) * 2 * KC):
                    k, w3 = n % (2 * KC) // 2, n % 2
                    if n >= 2:
                        pe.wait_ge(patch_v if n % 2 else patch_a, n // 2)
                    for w in range(3):
                        mm = pe.transpose(banks[:, n % 2, w * SIDE * HALF:(w + 1) * SIDE * HALF],
                                          xpatch[0:SIDE * HALF, k // 2, 3 * w3 + w, k % 2 * 128:k % 2 * 128 + 128],
                                          identf[0:SIDE * HALF, 0:SIDE * HALF])
                    mm.then_inc(patch_t, 1)

            def embed(q):
                if q >= 2:
                    pe.wait_ge(tok_a, q - 1)
                    pe.wait_ge(tok_v, q - 1)
                f = q // (NQ // 2)
                pe.wait_ge(patch_a, (f + 1) * KC)
                pe.wait_ge(patch_v, (f + 1) * KC)
                for part, (n, at) in enumerate(((DM, 0), (DT, DM))):
                    for k in range(KC):
                        mm = pe.matmul(banks[0:n, 3 + 2 * (q % 2) + part, 0:EQ * NP], wemb[:, k, at:at + n],
                                       patchT[:, k, q * EQ * NP:(q + 1) * EQ * NP], start=(k == 0), stop=(k == KC - 1))
                    mm.then_inc(emb_done, 1)

            def token_transposes(q):
                pe.wait_ge(tok_a, q + 1)
                pe.wait_ge(tok_v, q + 1)
                for m in range(4 * q, 4 * q + 4):
                    if m >= 2:
                        pe.wait_ge(tok_h, m - 1)
                    bank = 2 if m % 2 else 7
                    for s in range(2):
                        col = (2 * (m % 4) + s) * NP
                        pe.transpose(banks[0:NP, bank, s * D:s * D + DM], tokT[:, q % 2, 0, col:col + NP],
                                     identf[:, :])
                        mm = pe.transpose(banks[0:NP, bank, s * D + DM:(s + 1) * D],
                                          tokT[0:DT, q % 2, 1, col:col + NP], identf[0:DT, 0:DT])
                    mm.then_inc(tok_t, 1)

            patch_transposes(0)
            pe.wait_ge(wemb_in, 16)
            embed(0)
            embed(1)
            patch_transposes(1)
            token_transposes(0)
            token_transposes(1)
            embed(2)
            embed(3)
            token_transposes(2)
            token_transposes(3)

            def use_bank(kind, g):
                n = TRNO[kind, g]
                if n >= 3:
                    pe.wait_ge(tr_free, n - 2)
                return 5 + n % 3

            def vc_bank(*use):
                n = VCNO[use]
                if n >= 2:
                    pe.wait_ge(vc_free, n - 1)
                return 2 + n % 2

            def transposes(kind, g, src, n):
                bank = use_bank(kind, g)
                for s in range(G):
                    mm = pe.transpose(banks[0:n, bank, s * T:(s + 1) * T], src(s), identf[0:T, 0:T])
                mm.then_inc(tr_full, 1)

            def xn_transposes(g):
                pe.wait_ge(xn_ready, g + 1)
                transposes("xm", g, lambda s: xn[0:T, s, 0:DM], DM)
                transposes("xt", g, lambda s: xn[0:T, s, DM:D], DT)

            pe.wait_ge(tok_h, 4 * NQ)
            xn_transposes(0)
            pe.wait_ge(wq_in, 16 * 7)
            pe.wait_ge(gate_in, 16 * 3)
            for g in range(NG + 2):
                if g < NG:
                    pe.wait_ge(tr_free, TRNO["xt", g] + 1)
                    for m in range(4):
                        n = DT if m % 2 else DM
                        at = (m // 2) * D + (DM if m % 2 else 0)
                        if 4 * g + m >= 2:
                            pe.wait_ge(qk_free, 4 * g + m - 1)
                        dst = banks[0:n, m % 2, 0:G * T]
                        pe.matmul(dst, wq_m[:, at:at + n], xnT[:, 0, :], start=True, stop=False)
                        pe.matmul(dst, wq_t[0:DT, at:at + n], xnT[0:DT, 1, :], start=False, stop=True
                                  ).then_inc(qk_full, 1)
                    for a in range(2):
                        bank = vc_bank("v", g, a)
                        for s in range(2):
                            c0 = (2 * a + s) * T
                            dst = banks[0:T, bank, s * D:(s + 1) * D]
                            pe.matmul(dst, xnT[:, 0, c0:c0 + T], wq_m[:, 2 * D:3 * D], start=True, stop=False)
                            mm = pe.matmul(dst, xnT[0:DT, 1, c0:c0 + T], wq_t[0:DT, 2 * D:3 * D], start=False, stop=True)
                        mm.then_inc(vc_full, 1)
                if g + 1 < NG:
                    xn_transposes(g + 1)
                if 1 <= g <= NG:
                    pe.wait_ge(exp_done, G * g)
                    transposes("p", g - 1, lambda s: prob[0:T, s * T:(s + 1) * T], T)
                    pe.wait_ge(tr_free, TRNO["p", g - 1] + 1)
                    for a in range(2):
                        bank = vc_bank("c", g - 1, a)
                        for s in range(2):
                            b = 2 * a + s
                            mm = pe.matmul(banks[0:T, bank, s * D:(s + 1) * D], probT[0:T, b * T:(b + 1) * T],
                                           v[0:T, (g - 1) % 2, b, :], start=True, stop=True)
                        mm.then_inc(vc_full, 1)
                if g < NG:
                    pe.wait_ge(qk_free, 4 * g + 4)
                    if g >= 1:
                        pe.wait_ge(exp_done, G * g)
                    for s in range(G):
                        cols = slice(s * T, (s + 1) * T)
                        pe.matmul(banks[0:T, 4, cols], qk[:, 0, cols], qk[:, 2, cols], start=True, stop=False)
                        mm = pe.matmul(banks[0:T, 4, cols], qk[0:DT, 1, cols], qk[0:DT, 3, cols], start=False, stop=True)
                    mm.then_inc(s_full, 1)
                if g >= 2:
                    pe.wait_ge(xs_ready, g - 1)
                    transposes("sm", g - 2, lambda s: xs[0:T, g % 2, s, 0:DM], DM)
                    transposes("st", g - 2, lambda s: xs[0:T, g % 2, s, DM:D], DT)
                    pe.wait_ge(tr_free, TRNO["st", g - 2] + 1)
                    bank = use_bank("gate", g - 2)
                    for s in range(G):
                        cols = slice(s * T, (s + 1) * T)
                        dst = banks[0:T, bank, s * NE:(s + 1) * NE]
                        pe.matmul(dst, xsT[:, 0, cols], gw_m, start=True, stop=False)
                        mm = pe.matmul(dst, xsT[0:DT, 1, cols], gw_t[0:DT, :], start=False, stop=True)
                    mm.then_inc(tr_full, 1)

            pe.wait_ge(mask_ready, 1)
            pe.matmul(banks[0:T, 4, 0:NR], before[0:T, 0:T], mask16[0:T, :], start=True, stop=True)
            pe.matmul(banks[:, 5, 0:NR], ones16[0:T, :], mask16[0:T, :], start=True, stop=True).then_inc(rank_done, 1)

            def row_transposes(c, i=0):
                q = c % 2
                if c < PA:
                    pe.wait_ge(xrow_in[q], 16 * (c // 2 + 1 + i))
                else:
                    pe.wait_ge(xrow_got[q], 16 * (c // 2 - (PA + 1 - q) // 2 + 1 + i))
                if c >= 2:
                    pe.wait_ge(xt_ready, c - 1 + 2 * i)
                dst = banks[:, 6 + q, 0:256].bitcast(F16)
                for k in range(2):
                    pe.transpose(dst[:, k * 128:(k + 1) * 128], xrow[:, q, k * D:k * D + DM], ident16[:, :])
                    for part in range(2):
                        mm = pe.transpose(dst[64 * part:64 * part + 64, (2 + k) * 128:(3 + k) * 128],
                                          xrow[:, q, k * D + DM:(k + 1) * D], ident16[:, :])
                mm.then_inc(xt_full, 1)

            def up_half(c, i, r, base):
                q = c % 2
                n = 2 * c + r + 4 * i
                pe.wait_ge(xt_ready, c + 1 + 2 * i)
                if c >= 1:
                    pe.wait_ge(silu_ready, n - 1)
                    pe.wait_ge(clamp_ready, n - 1)
                for k in range(HC):
                    for m in range(2):
                        dst = banks[:, 2 * m + r, k * 128:(k + 1) * 128]
                        at = base + m * WU + (HC * r + k) * 128
                        hi = W16[:, ds(at, 128)]
                        tails = W16[:, ds(at + FI, 128)]
                        lo = W16[:, ds(at + 2 * FI, 128)]
                        pe.matmul(dst, hi, xT[:, q, 0, :], start=True, stop=False)
                        pe.matmul(dst, hi, xT[:, q, 1, :], start=False, stop=False)
                        pe.matmul(dst, lo, xT[:, q, 0, :], start=False, stop=False)
                        pe.matmul(dst, tails, xT[:, q, 2, :], start=False, stop=False)
                        mm = pe.matmul(dst, tails, xT[:, q, 3, :], start=False, stop=True)
                mm.then_inc(gu_full, 1)

            def down_half(c, i, r, base):
                q = c % 2
                n = 2 * c + r + 4 * i
                pe.wait_ge(hlo_ready, n + 1)
                if r == 0 and c >= 2:
                    pe.wait_ge(y_ready, c - 1 + 2 * i)
                for k in range(HC):
                    at = base + 2 * WU + (HC * r + k) * D
                    hi = W16[:, ds(at, D)]
                    lo = W16[:, ds(at + IC * D, D)]
                    dst = banks[:, 4 + q, 0:D]
                    cols = slice(k * 128, (k + 1) * 128)
                    first, last = r == 0 and k == 0, r == 1 and k == HC - 1
                    pe.matmul(dst, hhi[:, q, r, cols], hi, start=first, stop=False)
                    pe.matmul(dst, hhi[:, q, r, cols], lo, start=False, stop=False)
                    mm = pe.matmul(dst, hlo[:, q, r, cols], hi, start=False, stop=last)
                if r == 1:
                    mm.then_inc(y_full, 1)

            def step(c, i, up, down):
                up_half(c, i, 0, up)
                if c + 1 < NPOS:
                    row_transposes(c + 1, i)
                if down is not None:
                    down_half(c - 1, i, 0, down)
                up_half(c, i, 1, up)
                if down is not None:
                    down_half(c - 1, i, 1, down)

            def expert_at(p):
                return pe.value_load(btab[0:1, ds(p, 1)], min_val=0, max_val=NE) * WE

            shared = NE * WE
            pe.wait_ge(w_lo, NU)
            row_transposes(0)
            step(0, 0, shared, None)
            step(1, 0, shared, shared)
            with pe.Fori(0, (PA - 3) // 2) as i:
                for s in range(2):
                    step(2 + s, i, shared, shared)
            step(PA - 1, 0, shared, shared)
            pe.wait_ge(btab_ready, 1)
            with pe.Fori(0, PR // 2) as i:
                for s in range(2):
                    step(PA + s, i, expert_at(PA + s + 2 * i), expert_at(PA + s - 1 + 2 * i))
            step(PA + PR, 0, shared, expert_at(PA + PR - 1))
            with pe.Fori(0, (PA - 3) // 2) as i:
                for s in range(2):
                    step(PA + PR + 1 + s, i, shared, shared)
            step(NPOS - 2, 0, shared, shared)
            step(NPOS - 1, 0, shared, shared)
            down_half(NPOS - 1, 0, 0, shared)
            down_half(NPOS - 1, 0, 1, shared)

        @block.vector
        def _(dve):
            links = [0]

            def link(ins):
                links[0] += 1
                ins.then_inc(dve_link, 1)
                dve.wait_ge(dve_link, links[0])

            def unit_amax(u):
                e, m = UNITS[u]
                dve.wait_ge(stage_in[u % 2], stage_full(u))
                dve.tensor_reduce(amax[:, u % 2:u % 2 + 1], stage[:, u % 2, 0:UCOLS[m]], axis=AX.X, op=ALU.max,
                                  apply_absolute_value=True).then_inc(w_amax, 1)

            def unit_scale(u):
                e, m = UNITS[u]
                at = slice(3 * e + m, 3 * e + m + 1)
                dve.wait_ge(w_all, u + 1)
                link(dve.tensor_scalar(bits.bitcast(I32)[:, 0:1], amaxall.bitcast(I32)[:, u % 2:u % 2 + 1],
                                       0x7F800000, None, ALU.bitwise_and))
                link(dve.tensor_scalar(bits.bitcast(I32)[:, 1:2], bits.bitcast(I32)[:, 0:1],
                                       float(40 << 23), -1.0, ALU.max, ALU.mult))
                dve.tensor_scalar(wscale[:, at].bitcast(I32), bits.bitcast(I32)[:, 1:2], float(268 << 23), None,
                                  ALU.add).then_inc(w_scale, 1)
                dve.wait_ge(w_scale, u + 1)
                dve.tensor_scalar(winv[:, at].bitcast(I32), wscale[:, at].bitcast(I32), -1.0, float(254 << 23),
                                  ALU.mult, ALU.add)

            def unit_lo(u):
                e, m = UNITS[u]
                at = w_at(e, m)
                scale = wscale[:, 3 * e + m:3 * e + m + 1]
                dve.wait_ge(w_hi, u + 1)
                if m < 2:
                    dve.scalar_tensor_tensor(W16[:, at + 2 * FI:at + 3 * FI], stage[:, u % 2, 0:FI], scale,
                                             W16[:, at:at + FI], ALU.mult, ALU.subtract)
                    tail = W16[64:128, at + FI:at + 2 * FI]
                    dve.scalar_tensor_tensor(tail, stage[64:128, u % 2, FI:2 * FI], scale[64:128, :], tail,
                                             ALU.mult, ALU.subtract).then_inc(w_lo, 1)
                else:
                    n = IC * D
                    dve.scalar_tensor_tensor(W16[:, at + n:at + 2 * n], stage[:, u % 2, 0:n], scale,
                                             W16[:, at:at + n], ALU.mult, ALU.subtract).then_inc(w_lo, 1)

            def unit(u):
                unit_amax(u)
                if u >= 1:
                    unit_lo(u - 1)
                unit_scale(u)

            def patch_evac(n):
                f, k, w3 = n // (2 * KC), n % (2 * KC) // 2, n % 2
                dve.wait_ge(patch_t, n + 1)
                dst = patchT[:, k, f * HALF * NP:(f + 1) * HALF * NP].rearrange("p (r w) -> p w r", w=SIDE)
                dve.tensor_copy(dst[:, 3 * w3:3 * w3 + 3, :],
                                banks[:, 1, 0:3 * SIDE * HALF].rearrange("p (w r) -> p w r", w=3)).then_inc(patch_v, 1)

            def tok_evac(q):
                dve.wait_ge(emb_done, 2 * q + 2)
                if q >= 2:
                    dve.wait_ge(tok_t, 4 * (q - 1))
                dve.tensor_copy(tokT[0:DT, q % 2, 1, :], banks[0:DT, 4 + 2 * (q % 2), 0:EQ * NP]).then_inc(tok_v, 1)

            def tok_add(q):
                for m in range(4 * q, 4 * q + 4):
                    dve.wait_ge(tok_t, m + 1)
                    dve.tensor_tensor(h[0:NP, 2 * m:2 * m + 2, :],
                                      banks[0:NP, 2 if m % 2 else 7, 0:2 * D].rearrange("p (s d) -> p s d", s=2),
                                      posb[0:NP, :].unsqueeze(1).to_broadcast([NP, 2, D]), ALU.add).then_inc(tok_h, 1)

            dve.wait_ge(pos_in, 64)
            dve.tensor_tensor(row0[0:1, 2 * D:3 * D], row0[0:1, 0:D], row0[0:1, D:2 * D], ALU.add).then_inc(cls_sum, 1)
            dve.tensor_tensor(posb[0:NP, :], posb[0:NP, :], bembb[0:NP, :], ALU.add).then_inc(pos_sum, 1)
            patches_apart(dve, dve.tensor_copy, 0, 0)
            for n in range(1, NPT // 2, 2):
                patch_evac(n)
            unit(0)
            unit(1)
            tok_evac(0)
            tok_evac(1)
            patches_apart(dve, dve.tensor_copy, 1, 0)
            for n in range(NPT // 2 + 1, NPT, 2):
                patch_evac(n)
            unit(2)
            dve.wait_ge(pos_sum, 1)
            tok_add(0)
            tok_add(1)
            unit(3)
            tok_evac(2)
            tok_evac(3)
            tok_add(2)
            tok_add(3)
            dve.wait_ge(tok_h, 4 * NQ)

            def group_stats(g, mv, ready):
                for s in range(G):
                    dve.bn_stats(stats[0:T, 6 * s:6 * s + 6], h[0:T, G * g + s, :]).then_inc(dve_link, 1)
                links[0] += G
                dve.wait_ge(dve_link, links[0])
                for s in range(G):
                    dve.bn_aggr(mv[0:T, 2 * s:2 * s + 2], stats[0:T, 6 * s:6 * s + 6]).then_inc(ready, 1) if s == G - 1 \
                        else dve.bn_aggr(mv[0:T, 2 * s:2 * s + 2], stats[0:T, 6 * s:6 * s + 6])

            def normalise(g, dst, mv, rstd):
                for s in range(G):
                    last = dve.tensor_scalar(dst(s), h[0:T, G * g + s, :], mv[0:T, 2 * s:2 * s + 1],
                                             rstd[0:T, s:s + 1], ALU.subtract, ALU.mult)
                return last

            def xn_group(g):
                dve.wait_ge(rstd1_ready, g + 1)
                if g >= 1:
                    dve.wait_ge(tr_full, TRNO["xt", g - 1] + 1)
                normalise(g, lambda s: xn[0:T, s, :], mv1, rstd1).then_inc(xn_ready, 1)

            dve.wait_ge(txt_in, 16)
            dve.wait_ge(cls_row, 16)
            group_stats(0, mv1, mv1_ready)
            unit(4)
            xn_group(0)
            group_stats(1, mv1, mv1_ready)
            unit(5)
            xn_group(1)

            dve.wait_ge(wq_in, 16 * 7)
            for g in range(NG + 2):
                units = list(units_at(g)) if g < NG else []
                if g < NG:
                    for a in range(2):
                        n = VCNO["v", g, a]
                        dve.wait_ge(vc_full, n + 1)
                        dve.tensor_tensor(v[0:T, g % 2, 2 * a:2 * a + 2, :],
                                          banks[0:T, 2 + n % 2, 0:2 * D].rearrange("p (s d) -> p s d", s=2),
                                          bv[0:T, :].unsqueeze(1).to_broadcast([T, 2, D]), ALU.add).then_inc(vc_free, 1)
                if units:
                    unit(units[0])
                if 1 <= g <= NG:
                    dve.wait_ge(exp_done, G * g)
                    r = G * ((g - 1) % 2)
                    link(dve.reciprocal(rinv[0:T, :], rowsum[0:T, r:r + G]))
                    for a in range(2):
                        n = VCNO["c", g - 1, a]
                        dve.wait_ge(vc_full, n + 1)
                        for s in range(2):
                            b = 2 * a + s
                            row = h[0:T, G * (g - 1) + b, :]
                            last = dve.scalar_tensor_tensor(row, banks[0:T, 2 + n % 2, s * D:(s + 1) * D],
                                                            rinv[0:T, b:b + 1], row, ALU.mult, ALU.add)
                        last.then_inc(vc_free, 1)
                    dve.wait_ge(vc_free, n + 1)
                    group_stats(g - 1, mv2, mv2_ready)
                if g < NG:
                    dve.wait_ge(s_full, g + 1)
                    dve.tensor_reduce(negmax[0:T, :], banks[0:T, 4, 0:G * T].rearrange("p (s k) -> p s k", s=G),
                                      axis=AX.X, op=ALU.max, negate=True).then_inc(max_ready, 1)
                if units[1:]:
                    unit(units[1])
                if 1 <= g <= NG:
                    dve.wait_ge(rstd2_ready, g)
                    link(dve.tensor_scalar(rinv[0:T, :], rstd2[0:T, :], XSC, None, ALU.mult))
                    if g >= 3:
                        dve.wait_ge(lo_ready, g - 2)
                        dve.wait_ge(tr_full, TRNO["st", g - 3] + 1)
                    normalise(g - 1, lambda s: xs[0:T, (g - 1) % 2, s, :], mv2, rinv).then_inc(xs_ready, 1)
                if g + 2 < NG:
                    group_stats(g + 2, mv1, mv1_ready)
                if units[2:]:
                    unit(units[2])
                if g + 2 < NG:
                    xn_group(g + 2)
            unit_lo(NU - 1)

            all_e = [slice(m, 3 * (NE + 1), 3) for m in range(3)]
            d5 = rt[6][:, 0:5 * (NE + 1)].rearrange("p (k e) -> p k e", k=5)
            dve.wait_ge(w_lo, NU)
            dve.wait_ge(lo_ready, NG)
            for k in range(2):
                dve.wait_ge(rows_out[k], 16 * (NG // 2))
            dve.tensor_scalar(d5[:, 0, :], winv[:, all_e[0]], 1.0 / XSC, None, ALU.mult)
            dve.tensor_scalar(d5[:, 1, :], wscale[:, all_e[1]], LIMIT * XSC, None, ALU.mult)
            dve.tensor_scalar(d5[:, 2, :], wscale[:, all_e[1]], -LIMIT * XSC, None, ALU.mult)
            dve.tensor_scalar(d5[:, 3, :], winv[:, all_e[1]], HSC / XSC, None, ALU.mult)
            link(dve.tensor_scalar(d5[:, 4, :], winv[:, all_e[2]], 1.0 / HSC, None, ALU.mult))
            link(dve.tensor_copy(bscale[:, :, :], d5[:, :, NE:NE + 1].to_broadcast([128, 5, NPOS + 2])))

            R = slice(0, T)
            dve.wait_ge(tr_free, len(TR))
            link(dve.tensor_scalar(rt[0][R, :], logits[R, :], -1.0, None, ALU.mult))
            dve.tensor_tensor(rt[0][R, :], rt[0][R, :], logits[R, :], ALU.min).then_inc(e_abs, 1)
            dve.wait_ge(e_exp, 1)
            link(dve.tensor_scalar(rt[2][R, :], rt[1][R, :], 2.0, None, ALU.add))
            link(dve.reciprocal(rt[2][R, :], rt[2][R, :]))
            link(dve.tensor_tensor(rt[1][R, :], rt[1][R, :], rt[2][R, :], ALU.mult))
            link(dve.tensor_tensor(rt[2][R, :], rt[1][R, :], rt[1][R, :], ALU.mult))
            link(dve.tensor_scalar(rt[3][R, :], rt[2][R, :], 1.0 / 15, None, ALU.mult))
            for k in range(6, 0, -1):
                link(dve.scalar_tensor_tensor(rt[3][R, :], rt[3][R, :], 1.0 / (2 * k + 1), rt[2][R, :],
                                              ALU.add, ALU.mult))
            link(dve.scalar_tensor_tensor(rt[3][R, :], rt[3][R, :], 1.0, rt[1][R, :], ALU.add, ALU.mult))
            link(dve.tensor_scalar(rt[0][R, :], logits[R, :], 0.0, None, ALU.max))
            link(dve.scalar_tensor_tensor(rt[0][R, :], rt[3][R, :], 2.0, rt[0][R, :], ALU.mult, ALU.add))
            link(dve.tensor_scalar(rt[1][R, :], rt[0][R, :], 1e-30, None, ALU.max))
            link(dve.tensor_scalar(rt[2].bitcast(I32)[R, :], rt[1].bitcast(I32)[R, :], -0.5, float(0x5F3759DF),
                                   ALU.mult, ALU.add))
            for _ in range(4):
                link(dve.tensor_tensor(rt[3][R, :], rt[2][R, :], rt[2][R, :], ALU.mult))
                link(dve.scalar_tensor_tensor(rt[3][R, :], rt[3][R, :], -0.5, rt[1][R, :], ALU.mult, ALU.mult))
                link(dve.scalar_tensor_tensor(rt[2][R, :], rt[3][R, :], 1.5, rt[2][R, :], ALU.add, ALU.mult))
            link(dve.tensor_tensor(rt[0][R, :], rt[0][R, :], rt[2][R, :], ALU.mult))

            def by_tile(a, n=T):
                return a[0:n, :].rearrange("p (t e) -> p t e", e=NE)

            def over_e(a):
                return a[R, :].unsqueeze(2).to_broadcast([T, NS, NE])

            def over_t(a, n=T):
                return a[0:n, :].unsqueeze(1).to_broadcast([n, NS, NE])

            scores = by_tile(rt[0])
            biased, first, second, tmp = by_tile(rt[1]), by_tile(rt[2]), by_tile(rt[3]), by_tile(rt[4])
            dve.wait_ge(gate_in, 48)
            link(dve.tensor_tensor(biased, scores, over_t(gbias), ALU.add))
            for k, pick in enumerate((first, second)):
                link(dve.tensor_reduce(best[R, 0, :], biased, axis=AX.X, op=ALU.max))
                link(dve.tensor_tensor(tmp, biased, over_e(best[:, 0, :]), ALU.is_equal))
                link(dve.tensor_tensor(tmp, tmp, over_t(rankof), ALU.mult))
                link(dve.tensor_reduce(best[R, 1, :], tmp, axis=AX.X, op=ALU.max))
                link(dve.tensor_tensor(pick, tmp, over_e(best[:, 1, :]), ALU.is_equal))
                link(dve.tensor_tensor(tmp, pick, scores, ALU.mult))
                link(dve.tensor_reduce(best[R, 2 + k, :], tmp, axis=AX.X, op=ALU.add))
                if k == 0:
                    link(dve.scalar_tensor_tensor(biased, pick, -3e38, biased, ALU.mult, ALU.add))
            link(dve.tensor_tensor(best[R, 4, :], best[R, 2, :], best[R, 3, :], ALU.add))
            link(dve.tensor_scalar(best[R, 4, :], best[R, 4, :], 1e-6, None, ALU.max))
            link(dve.reciprocal(best[R, 4, :], best[R, 4, :]))
            for k in range(2):
                dve.tensor_tensor(wts[R, k, :], best[R, 2 + k, :], best[R, 4, :], ALU.mult)
            dve.tensor_tensor(mask16[R, :], rt[2][R, :], rt[3][R, :], ALU.add).then_inc(mask_ready, 1)
            dve.wait_ge(rank_done, 1)
            a, b = rt[4], rt[5]
            link(dve.tensor_copy(a, banks[:, 5, 0:NR]))
            n = 1
            while n < NS:
                dve.tensor_copy(b[:, 0:n * NE], a[:, 0:n * NE])
                link(dve.tensor_tensor(b[:, n * NE:], a[:, n * NE:], a[:, 0:(NS - n) * NE], ALU.add))
                a, b = b, a
                n *= 2
            total, nblk, end, start = small[:, 0, :], small[:, 1, :], small[:, 2, :], small[:, 3, :]
            link(dve.tensor_tensor(b, a, banks[:, 5, 0:NR], ALU.subtract))
            link(dve.tensor_scalar(total.bitcast(I32), a[:, (NS - 1) * NE:], 127.0, None, ALU.add))
            link(dve.tensor_scalar(total.bitcast(I32), total.bitcast(I32), 7, None, ALU.logical_shift_right))
            link(dve.tensor_copy(nblk, total.bitcast(I32)))
            c0, c1 = nblk, end
            n = 1
            while n < NE:
                dve.tensor_copy(c1[:, 0:n], c0[:, 0:n])
                link(dve.tensor_tensor(c1[:, n:], c0[:, n:], c0[:, 0:NE - n], ALU.add))
                c0, c1 = c1, (small[:, 4, :] if n == 1 else small[:, 5, :])
                n *= 2
            link(dve.tensor_tensor(start, c0, nblk, ALU.subtract))
            link(dve.tensor_scalar(total, start, 128.0, None, ALU.mult))
            link(dve.tensor_tensor(a[R, :], b[R, :], banks[R, 4, 0:NR], ALU.add))
            link(dve.tensor_tensor(by_tile(a), by_tile(a), over_t(total), ALU.add))
            for k, pick in enumerate((first, second)):
                link(dve.tensor_tensor(by_tile(b), by_tile(a), pick, ALU.mult))
                link(dve.tensor_reduce(best[R, 5 + k, :], by_tile(b), axis=AX.X, op=ALU.add))
            link(dve.tensor_copy(slots[R, :, :], best[R, 5:7, :]))
            shift = PR.bit_length() - 1
            assert PR == 1 << shift
            link(dve.tensor_scalar(pidx[R, :, :], slots[R, :, :], 127, shift, ALU.bitwise_and, ALU.logical_shift_left))
            link(dve.tensor_scalar(tmpi[R, :, :], slots[R, :, :], 7, None, ALU.logical_shift_right))
            dve.tensor_tensor(pidx[R, :, :], pidx[R, :, :], tmpi[R, :, :], ALU.bitwise_or).then_inc(slots_ready, 1)
            link(dve.tensor_scalar(blk[:, 0, :], iotab[:, :], start[:, 1:2], None, ALU.is_ge))
            for e in range(2, NE):
                link(dve.scalar_tensor_tensor(blk[:, 0, :], iotab[:, :], start[:, e:e + 1], blk[:, 0, :],
                                              ALU.is_ge, ALU.add))
            dve.tensor_copy(btab[:, PA:PA + PR], blk[:, 0, :])
            link(dve.memset(bscale[:, :, PA:PA + PR], 0.0))
            for e in range(NE):
                link(dve.tensor_scalar(blk[:, 1, :], blk[:, 0, :], float(e), None, ALU.is_equal))
                for k in range(5):
                    row = bscale[:, k, PA:PA + PR]
                    ins = dve.scalar_tensor_tensor(row, blk[:, 1, :], d5[:, k, e:e + 1], row, ALU.mult, ALU.add)
                    if k == 4:
                        link(ins)
            dve.memset(best[:, 7, 0:1], 0.0).then_inc(btab_shared, 1)
            dve.memset(best[:, 7, 1:2], 0.0).then_inc(btab_ready, 1)

            def step(c, i=0):
                for r in range(2):
                    n = 2 * c + r + 4 * i
                    p = ds(c + 2 * i, 1)
                    dve.wait_ge(gu_full, n + 1)
                    dve.tensor_scalar(act_t[:, r, :], banks[:, 2 + r, 0:HW_], bscale[:, 1, p], bscale[:, 2, p],
                                      ALU.min, ALU.max).then_inc(clamp_ready, 1)
                    dve.wait_ge(silu_ready, n + 1)
                    dve.wait_ge(clamp_ready, n + 1)
                    if c >= 1:
                        dve.wait_ge(hhi_ready, n - 1)
                    dve.scalar_tensor_tensor(act_h[:, r, :], act_s[:, r, :], SILU_LIMIT, act_t[:, r, :],
                                             ALU.min, ALU.mult).then_inc(hid_ready, 1)
                    dve.wait_ge(hid_ready, n + 1)
                    dve.wait_ge(hhi_ready, n + 1)
                    if c >= 2:
                        dve.wait_ge(y_full, c - 1 + 2 * i)
                    dve.scalar_tensor_tensor(hlo[:, c % 2, r, :], act_h[:, r, :], bscale[:, 3, p],
                                             hhi[:, c % 2, r, :], ALU.mult, ALU.subtract).then_inc(hlo_ready, 1)

            def combine(t, k):
                dve.wait_ge(yin_in[k], 4 * (t - k) + 16)
                dve.wait_ge(yin_got[k], 8 * (t - k) + 32)
                dve.scalar_tensor_tensor(yin[R, k, 0, :], yin[R, k, 1, :], wts[R, 0, ds(t, 1)], yin[R, k, 0, :],
                                         ALU.mult, ALU.add).then_inc(ysum1, 1)
                dve.wait_ge(ysum1, t + 1)
                dve.scalar_tensor_tensor(yin[R, k, 0, :], yin[R, k, 2, :], wts[R, 1, ds(t, 1)], yin[R, k, 0, :],
                                         ALU.mult, ALU.add).then_inc(ysum2, 1)
                dve.wait_ge(ysum2, t + 1)
                row = h[R, ds(t, 1), :].rearrange("p a d -> p (a d)")
                dve.tensor_tensor(row, row, yin[R, k, 0, :], ALU.add).then_inc(tile_done, 1)

            step(0)
            step(1)
            with dve.Fori(0, (PA - 3) // 2) as i:
                for s in range(2):
                    step(2 + s, i)
            step(PA - 1)
            with dve.Fori(0, PR // 2) as i:
                for s in range(2):
                    step(PA + s, i)
            step(PA + PR)
            step(PA + PR + 1)
            NJ = (PA - 1) // 2
            with dve.Fori(1, NJ) as j:
                for s in range(2):
                    step(PA + PR + s, j)
                    for k in range(2):
                        combine(4 * (j - 1) + 2 * s + k, 2 * s + k)
            step(NPOS - 1)
            for t in range(4 * (NJ - 1), NS):
                combine(t, t % 4)
    return nc


_INS = ['x', 'txt', 'L0_tok_W_emb', 'L0_tok_b_emb', 'L0_tok_pos_embedding', 'L0_tok_cls_token', 'L0_attn_W_qkv',
        'L0_attn_b_qkv', 'L0_ffn_gate_w', 'L0_ffn_gate_bias', 'L0_ffn_w1', 'L0_ffn_w2', 'L0_ffn_w3',
        'L0_ffn_w1s', 'L0_ffn_w2s', 'L0_ffn_w3s']


def kernel(**inputs):
    import numpy as _np
    import concourse.bacc as _bacc
    from concourse import mybir as _mybir
    from concourse.bass_utils import run_bass_kernel_spmd as _run

    nc = _bacc.Bacc("TRN2", target_bir_lowering=False, num_devices=1)
    arrays, args = {}, []
    for name in _INS:
        a = _np.ascontiguousarray(inputs[name])
        arrays[f"in_{name}"] = a
        args.append(nc.dram_tensor(f"in_{name}", a.shape, _mybir.dt.from_np(a.dtype), kind="ExternalInput").ap())
    b = inputs['x'].shape[0]
    tokens = inputs['L0_tok_pos_embedding'].shape[1] + inputs['txt'].shape[1]
    d = inputs['txt'].shape[2]
    args.append(nc.dram_tensor("out", (b, tokens, d), _mybir.dt.float32, kind="ExternalOutput").ap())
    early_fusion_layer(nc, *args)
    r = _run(nc, [arrays], core_ids=[0])
    return r.results[0]["out"]
```

```python
import numpy as np
import concourse.bass as bass
from concourse import mybir
from concourse.bass import ds
from contextlib import ExitStack

F32 = mybir.dt.float32
F16 = mybir.dt.float16
I32 = mybir.dt.int32
U32 = mybir.dt.uint32
ALU = mybir.AluOpType
ACT = mybir.ActivationFunctionType
AX = mybir.AxisListType


def early_fusion_layer(nc: bass.Bass, x, txt, w_emb, b_emb, pos, cls, w_qkv, b_qkv, gate_w, gate_bias,
                       w1, w2, w3, w1s, w2s, w3s, out):
    NS, CH, IMG, _ = x.shape
    NW, D = txt.shape[1], txt.shape[2]
    PATCH = 16
    SIDE = IMG // PATCH
    NP = SIDE * SIDE
    T = NP + 1 + NW
    NE, _, FI = w1.shape
    TOPK = 2
    DM, DT = 128, D - 128
    KC = CH * PATCH * PATCH // 128
    IC = FI // 128
    EPS = 1e-5
    SCALE = float(D) ** -0.5
    LIMIT = 10.0
    SILU_LIMIT = float(LIMIT / (1.0 + np.exp(-LIMIT)))
    G = 4
    NG = NS // G
    XSC = 2.0 ** 11
    HSC = 2.0 ** 9

    BW, SUB = 256, 2
    HALF = NS // 2
    NTOK = NS * T
    PS = -(-NTOK // BW)
    PA = 8
    PB = PS - PA
    PR = (NTOK * TOPK + NE * (BW - 1)) // BW
    NPOS = PS + PR
    NSUB = PR * SUB

    xrows = nc.dram_tensor("xrows", [PS * BW, 2 * D], F16).ap()
    yshared = nc.dram_tensor("yshared", [PS * BW, D], F32).ap()
    yrouted = nc.dram_tensor("yrouted", [PR * BW, D], F32).ap()
    slot_table = nc.dram_tensor("slot_table", [128 * NSUB, 2], I32).ap()

    ctx = ExitStack()
    with ctx:
        def sb(name, shape, dt=F32):
            return ctx.enter_context(nc.sbuf_tensor(name, shape, dt))

        def sem(name):
            return ctx.enter_context(nc.semaphore(name))

        WU = 3 * FI
        WE = 2 * WU + 2 * IC * D
        W16 = sb("W16", [128, (NE + 1) * WE], F16)
        h = sb("h", [128, NS, D])
        identf = sb("identf", [128, 128])
        ident16 = sb("ident16", [128, 128], F16)
        before = sb("before", [128, 128], F16)
        ones16 = sb("ones16", [128, 128], F16)
        wscale = sb("wscale", [128, 3 * (NE + 1)])
        winv = sb("winv", [128, 3 * (NE + 1)])
        logits = sb("logits", [128, NS * NE])
        mhalf = sb("mhalf", [128, G])
        gbias = sb("gbias", [128, NE])
        btab = sb("btab", [128, NPOS + 2], I32)
        bscale = sb("bscale", [128, 5, NPOS + 2])
        yscale = sb("yscale", [128, NPOS, SUB])
        pairs = sb("pairs", [128, NS, TOPK, 2])

        ARENA = 13600
        arena = sb("arena", [128, ARENA])

        def carve(at, cols, dt=F32):
            words = cols if dt != F16 else (cols + 1) // 2
            ap = arena[:, at:at + words]
            assert at + words <= ARENA, (at, words, ARENA)
            return (ap if dt == F32 else ap.bitcast(dt)), at + words

        o = 0
        wq_m, o = carve(o, 3 * D)
        wq_t, o = carve(o, 3 * D)
        bv, o = carve(o, D)
        gw_m, o = carve(o, NE)
        gw_t, o = carve(o, NE)
        bq, o = carve(o, 4)
        bqs, o = carve(o, 2)
        stats, o = carve(o, 2 * 6 * G)
        mv1, o = carve(o, 2 * G)
        rstd1, o = carve(o, G)
        mv2, o = carve(o, 2 * G)
        rstd2, o = carve(o, G)
        negmax, o = carve(o, G)
        rowsum, o = carve(o, 2 * G)
        rinv, o = carve(o, G)
        rstdx, o = carve(o, G)
        amax, o = carve(o, 4)
        amaxall, o = carve(o, 4)
        bits, o = carve(o, 4)
        xnT, o = carve(o, 2 * G * T)
        qk, o = carve(o, 4 * G * T)
        v, o = carve(o, 2 * G * D)
        prob, o = carve(o, G * T)
        probT, o = carve(o, G * T)
        xs, o = carve(o, 2 * G * D)
        rows, o = carve(o, G * 2 * D, F16)
        NST = 3
        stage, o = carve(o, NST * 2 * FI)
        xnT = xnT.rearrange("p (m c) -> p m c", m=2)
        qk = qk.rearrange("p (m c) -> p m c", m=4)
        v = v.rearrange("p (r g d) -> p r g d", r=2, g=G)
        xs = xs.rearrange("p (r g d) -> p r g d", r=2, g=G)
        rows = rows.rearrange("p (g d) -> p g d", g=G)
        stage = stage.rearrange("p (r c) -> p r c", r=NST)
        xsT = sb("xsT", [128, 2, G * T])

        EMB = WE
        emb = W16[:, EMB:NE * WE].bitcast(F32)
        xin = emb[:, 0:2 * CH * PATCH * IMG].rearrange("p (f c w) -> p f c w", f=2, c=CH)
        e0 = 2 * CH * PATCH * IMG
        patchT = emb[:, e0:e0 + KC * NS * NP].rearrange("p (k c) -> p k c", k=KC)
        e0 += KC * NS * NP
        wemb = emb[:, e0:e0 + KC * D].rearrange("p (k d) -> p k d", k=KC)
        e0 += KC * D
        EQ = 8
        NQ = NS // EQ
        tokT = emb[:, e0:e0 + 2 * 2 * EQ * NP].rearrange("p (r m c) -> p r m c", r=2, m=2)
        e0 += 2 * 2 * EQ * NP
        posb = emb[:, e0:e0 + D]
        bembb = emb[:, e0 + D:e0 + 2 * D]
        row0 = emb[:, e0 + 2 * D:e0 + 5 * D]
        zrow = emb[:, e0 + 5 * D:e0 + 6 * D].bitcast(F16)
        e0 += 6 * D
        xpatch = emb[:, e0:e0 + CH * PATCH * IMG].rearrange("p (c w v) -> p c w v", c=CH, w=SIDE)
        assert e0 + CH * PATCH * IMG <= (NE * WE - EMB) // 2
        xn = emb[:, (NE * WE - EMB) // 2 - G * D:(NE * WE - EMB) // 2].rearrange("p (g d) -> p g d", g=G)

        o = 0
        xrow, o = carve(o, 2 * SUB * 2 * D, F16)
        xT, o = carve(o, 2 * 4 * BW, F16)
        ND = 3
        HC = IC // ND
        HW_ = HC * BW
        act_s, o = carve(o, 2 * HW_)
        act_h, o = carve(o, 2 * HW_)
        hhi, o = carve(o, ND * HW_, F16)
        hlo, o = carve(o, ND * HW_, F16)
        ysb, o = carve(o, 2 * SUB * D)
        yin, o = carve(o, 2 * G * D)
        gidx, o = carve(o, 2 * SUB)
        xrow = xrow.rearrange("p (r s c) -> p r s c", r=2, s=SUB)
        xT = xT.rearrange("p (r k c) -> p r k c", r=2, k=4)
        act_s = act_s.rearrange("p (r c) -> p r c", r=2)
        act_h = act_h.rearrange("p (r c) -> p r c", r=2)
        hhi = hhi.rearrange("p (r c) -> p r c", r=ND)
        hlo = hlo.rearrange("p (r c) -> p r c", r=ND)
        ysb = ysb.rearrange("p (r s d) -> p r s d", r=2, s=SUB)
        yin = yin.rearrange("p (r g d) -> p r g d", r=2, g=G)
        gidx = gidx.bitcast(U32)
        NR = NS * NE
        rt = []
        for _ in range(7):
            a, o = carve(o, NR)
            rt.append(a)
        best, o = carve(o, 8 * NS)
        best = best.rearrange("p (k t) -> p k t", k=8)
        mask16, o = carve(o, NR, F16)
        small, o = carve(o, 6 * NE)
        small = small.rearrange("p (k e) -> p k e", k=6)
        blk, o = carve(o, 2 * PR)
        blk = blk.rearrange("p (k b) -> p k b", k=2)
        ids, o = carve(o, 2 * NSUB)
        ids = ids.rearrange("p (b k) -> p b k", k=2)
        slots, o = carve(o, 2 * NS)
        slots = slots.bitcast(I32).rearrange("p (k t) -> p k t", k=2)
        pidx, o = carve(o, 2 * NS)
        pidx = pidx.bitcast(I32).rearrange("p (k t) -> p k t", k=2)
        tmpi, o = carve(o, 2 * NS)
        tmpi = tmpi.bitcast(I32).rearrange("p (k t) -> p k t", k=2)
        rankof = sb("rankof", [128, NE])
        iotab = sb("iotab", [128, PR])

        banks = ctx.enter_context(nc.psum_tensor("banks", [128, 8, 512], F32))

        const_ready = sem("const_ready")
        wemb_in, x_in0, x_in1, pos_in, txt_in, wq_in, gate_in = map(
            sem, ("wemb_in", "x_in0", "x_in1", "pos_in", "txt_in", "wq_in", "gate_in"))
        cls_sum, cls_row, pos_sum = sem("cls_sum"), sem("cls_row"), sem("pos_sum")
        x_patch = sem("x_patch")
        patch_t, patch_a, patch_v = sem("patch_t"), sem("patch_a"), sem("patch_v")
        emb_done, tok_a, tok_v = sem("emb_done"), sem("tok_a"), sem("tok_v")
        tok_t, tok_h = sem("tok_t"), sem("tok_h")
        stage_in = [sem(f"stage_in{k}") for k in range(3)]
        w_amax, w_scale, w_inv, w_hi, w_lo, w32_lo = map(sem, ("w_amax", "w_scale", "w_inv", "w_hi", "w_lo", "w32_lo"))
        dve_link, act_link = sem("dve_link"), sem("act_link")
        mv1_ready, rstd1_ready, xn_ready = sem("mv1_ready"), sem("rstd1_ready"), sem("xn_ready")
        mv2_ready, rstd2_ready, xs_ready = sem("mv2_ready"), sem("rstd2_ready"), sem("xs_ready")
        pool_link = sem("pool_link")
        tr_full, tr_free = sem("tr_full"), sem("tr_free")
        qk_full, qk_free = sem("qk_full"), sem("qk_free")
        vc_full, vc_free = sem("vc_full"), sem("vc_free")
        s_full, max_ready, exp_done = sem("s_full"), sem("max_ready"), sem("exp_done")
        hi_ready, lo_ready, rows_out = sem("hi_ready"), sem("lo_ready"), [sem("rows_out0"), sem("rows_out1")]
        zero_out, idz_out = sem("zero_out"), sem("idz_out")
        e_abs, e_exp, mask_ready, rank_done, slots_ready, btab_ready = map(
            sem, ("e_abs", "e_exp", "mask_ready", "rank_done", "slots_ready", "btab_ready"))
        btab_shared = sem("btab_shared")
        ids_out, ids_in = sem("ids_out"), sem("ids_in")
        xrow_in = [sem("xrow_in0"), sem("xrow_in1")]
        xrow_got = [sem("xrow_got0"), sem("xrow_got1")]
        xt_full, xt_ready = sem("xt_full"), sem("xt_ready")
        gu_full = sem("gu_full")
        silu_ready, clamp_ready, hid_ready = sem("silu_ready"), sem("clamp_ready"), sem("hid_ready")
        hhi_ready, hlo_ready = sem("hhi_ready"), sem("hlo_ready")
        y_full, y_ready = sem("y_full"), sem("y_ready")
        y_out = [sem("y_out0"), sem("y_out1")]
        gidx_ready, yscale_ready = sem("gidx_ready"), sem("yscale_ready")
        yin_in = [sem("yin_in0"), sem("yin_in1")]
        shared_added, first_added = sem("shared_added"), sem("first_added")
        second_added = [sem(f"second_added{j}") for j in range(NS // G)]
        out_done = sem("out_done")

        UNITS = [(e, m) for e in [NE] + list(range(NE)) for m in range(3)]
        NU = len(UNITS)
        UCOLS = [2 * FI, 2 * FI, IC * D]
        SHARED_W = [w1s, w3s, w2s]
        ROUTED_W = [w1, w3, w2]
        UNITS_EMB = 6

        def units_at(g):
            left = NU - UNITS_EMB
            return range(UNITS_EMB + left * g // NG, UNITS_EMB + left * (g + 1) // NG)

        def w_at(e, m):
            return e * WE + m * WU

        def stage_full(u):
            return sum(16 if UNITS[k][1] == 2 else 48 for k in range(u % NST, u + 1, NST))

        TR = [("xm", 0), ("xt", 0)]
        for g in range(NG + 3):
            if 0 <= g - 3 < NG:
                TR += [("gate", g - 3)]
            if g + 1 < NG:
                TR += [("xm", g + 1), ("xt", g + 1)]
            if 0 <= g - 1 < NG:
                TR += [("p", g - 1)]
            if 0 <= g - 2 < NG:
                TR += [("sm", g - 2), ("st", g - 2)]
        TRNO = {u: n for n, u in enumerate(TR)}
        def n_of(c, r):
            return ND * c + r

        VC = []
        for g in range(NG + 1):
            if g < NG:
                VC += [("v", g, 0), ("v", g, 1)]
            if g >= 1:
                VC += [("c", g - 1, 0), ("c", g - 1, 1)]
        VCNO = {u: n for n, u in enumerate(VC)}

        LOADS_AT = {}
        for j in range(2, NG):
            last = -(-(j + 1) * G * T // BW) - 1
            LOADS_AT.setdefault(max(last, PA - 1) + PR if last >= PA else PA + PR - 2, []).append(j)
        ADD_AT = {j: c + 2 for c, js in LOADS_AT.items() for j in js}
        ZERO_DMAS = -(-(PS * BW - NTOK) // 128)
        NPT = 2 * KC * 2
        block = ctx.enter_context(nc.Block())

        @block.sync
        def _(sp):
            def load_unit(u):
                e, m = UNITS[u]
                if u >= NST:
                    sp.wait_ge(w32_lo if m else w_lo, 2 * (u // 3) - 2 + m if m else u // 3)
                src = SHARED_W[m] if e == NE else ROUTED_W[m][e]
                done = stage_in[u % NST]
                if m < 2:
                    sp.dma_start(stage[:, u % NST, 0:FI], src[0:DM, :]).then_inc(done, 16)
                    for part in range(2):
                        sp.dma_start(stage[64 * part:64 * part + 64, u % NST, FI:2 * FI], src[DM:D, :]).then_inc(done, 16)
                else:
                    sp.dma_start(stage[:, u % NST, 0:IC * D].rearrange("p (c d) -> p c d", c=IC),
                                 src.rearrange("(c p) d -> p c d", p=128)).then_inc(done, 16)

            sp.dma_start(row0[0:1, 0:D], pos[0, 0:1, :]).then_inc(pos_in, 16)
            sp.dma_start(row0[0:1, D:2 * D], cls[0, :, :]).then_inc(pos_in, 16)
            sp.dma_start(posb[0:NP, :], pos[0, 1:NP + 1, :]).then_inc(pos_in, 16)
            sp.dma_start(bembb[0:NP, :], b_emb.partition_broadcast(NP)).then_inc(pos_in, 16)
            for f in range(2):
                for b in range(NS // 2):
                    eng = sp
                    eng.dma_start(xin[SIDE * b:SIDE * b + SIDE, f, :, :],
                                  x[f * (NS // 2) + b].rearrange("c (n y) w -> n c (y w)", n=SIDE)
                                  ).then_inc(x_in0 if f == 0 else x_in1, 16)
                if f == 0:
                    sp.dma_start(wemb, w_emb.rearrange("(k p) d -> p k d", p=128)).then_inc(wemb_in, 16)
                    for u in range(NST):
                        load_unit(u)
            sp.dma_start(h[NP + 1:T, :, :], txt.rearrange("b t d -> t b d")).then_inc(txt_in, 16)
            sp.dma_start(wq_m, w_qkv[0:DM, :]).then_inc(wq_in, 16)
            sp.dma_start(wq_t[0:DT, :], w_qkv[DM:D, :]).then_inc(wq_in, 16)
            sp.dma_start(bv[0:T, :], b_qkv[2 * D:3 * D].partition_broadcast(T)).then_inc(wq_in, 16)
            for k in range(2):
                b1 = b_qkv[k * D:(k + 1) * D].rearrange("(p a) -> p a", a=1)
                sp.dma_start(bq[:, 2 * k:2 * k + 1], b1[0:DM, :]).then_inc(wq_in, 16)
                sp.dma_start(bq[0:DT, 2 * k + 1:2 * k + 2], b1[DM:D, :]).then_inc(wq_in, 16)
            sp.dma_start(gw_m, gate_w[0:DM, :]).then_inc(gate_in, 16)
            sp.dma_start(gw_t[0:DT, :], gate_w[DM:D, :]).then_inc(gate_in, 16)
            sp.dma_start(gbias[0:T, :], gate_bias.partition_broadcast(T)).then_inc(gate_in, 16)
            sp.wait_ge(cls_sum, 1)
            sp.dma_start(h[NP:NP + 1, :, :], row0[0:1, 2 * D:3 * D].unsqueeze(1).to_broadcast([1, NS, D])
                         ).then_inc(cls_row, 16)
            sp.wait_ge(const_ready, 3)
            for at in range(NTOK, PS * BW, 128):
                n = min(128, PS * BW - at)
                sp.dma_start(xrows[at:at + n, :], zrow[0:n, :]).then_inc(zero_out, 16)
            sp.dma_start(slot_table.rearrange("(p b) a -> p (b a)", p=128), zrow[:, 0:4 * NSUB].bitcast(I32)
                         ).then_inc(idz_out, 16)
            for u in range(NST, UNITS_EMB + 1):
                load_unit(u)

            def store_rows(g):
                sp.wait_ge(hi_ready, g + 1)
                sp.wait_ge(lo_ready, g + 1)
                at = g * G * T
                sp.dma_start(xrows[at:at + G * T, :].rearrange("(g t) d -> t g d", g=G), rows[0:T, :, :]
                             ).then_inc(rows_out[g % 2], 16)

            for g in range(NG + 2):
                if g < NG:
                    for u in units_at(g):
                        if u + 1 < NU:
                            load_unit(u + 1)
                if g >= 2:
                    store_rows(g - 2)

            for k in range(2):
                sp.wait_ge(rows_out[k], 16 * (NG // 2))
            sp.wait_ge(zero_out, 16 * ZERO_DMAS)

            def load_rows(c, i=0):
                if c >= 2:
                    sp.wait_ge(xt_full, c - 1 + 2 * i)
                at = (c - (PR if c >= PA else 0) + 2 * i) * BW
                sp.dma_start(xrow[:, c % 2, :, :], xrows[ds(at, BW), :].rearrange("(s p) d -> p s d", s=SUB)
                             ).then_inc(xrow_in[c % 2], 16)

            def store_y(c, i=0):
                sp.wait_ge(y_ready, SUB * (c + 1 + 2 * i))
                if PA <= c < PA + PR:
                    rows_of_y = yrouted[ds((c - PA + 2 * i) * BW, BW), :]
                else:
                    rows_of_y = yshared[ds((c - (PR if c >= PA else 0) + 2 * i) * BW, BW), :]
                sp.dma_start(rows_of_y.rearrange("(s p) d -> p s d", s=SUB), ysb[:, c % 2, :, :]
                             ).then_inc(y_out[c % 2], 16)

            def load_y(j):
                last = -(-(j + 1) * G * T // BW) - 1
                last += PR if last >= PA else 0
                sp.wait_ge(y_out[0], 16 * (last // 2 + 1))
                sp.wait_ge(y_out[1], 16 * ((last + 1) // 2))
                if j >= 2:
                    sp.wait_ge(shared_added, j - 1)
                sp.dma_start(yin[0:T, j % 2, :, :], yshared[j * G * T:(j + 1) * G * T, :]
                             .rearrange("(g t) d -> t g d", g=G)).then_inc(yin_in[j % 2], 16)

            def store_out(j):
                sp.wait_ge(second_added[j], 16 * G)
                src = h[:, G * j:G * j + G, :]
                dst = out[G * j:G * j + G, :, :]
                sp.dma_start(dst[:, 1:NP + 1, :].rearrange("b t d -> t b d"), src[0:NP, :, :]).then_inc(out_done, 16)
                sp.dma_start(dst[:, 0:1, :].rearrange("b t d -> t b d"), src[NP:NP + 1, :, :]).then_inc(out_done, 16)
                sp.dma_start(dst[:, NP + 1:T, :].rearrange("b t d -> t b d"), src[NP + 1:T, :, :]).then_inc(out_done, 16)

            for c in range(4):
                load_rows(c)
            with sp.Fori(0, (PA - 4) // 2) as i:
                for s in range(2):
                    load_rows(4 + s, i)
                    store_y(s, i)
            for c in range(PA - 4, PA):
                store_y(c)
            load_y(0)
            load_y(1)
            with sp.Fori(0, (PR - 4) // 2) as i:
                for s in range(2):
                    store_y(PA + s, i)
            store_y(PA + PR - 4)
            load_rows(PA + PR + 1)
            store_y(PA + PR - 3)
            for c in range(PA + PR + 2, NPOS + 4):
                if c < NPOS:
                    load_rows(c)
                store_y(c - 4)
                for j in LOADS_AT.get(c - 4, []):
                    load_y(j)
            for j in range(NG):
                store_out(j)
            sp.wait_ge(out_done, 48 * NG)

        def patches_apart(eng, copy, f, c):
            eng.wait_ge(x_in0 if f == 0 else x_in1, 16 * HALF)
            if f == 1:
                eng.wait_ge(patch_t, NPT // 2)
            P = SIDE * HALF
            copy(xpatch[0:P, c, :, :].rearrange("p w (y v) -> p w y v", v=PATCH),
                 xin[0:P, f, c, :].rearrange("p (y w v) -> p w y v", w=SIDE, v=PATCH)).then_inc(x_patch, 1)

        @block.gpsimd
        def _(pool):
            IO = bass.IndirectOffsetOnAxis
            links = [0]

            def link(ins):
                links[0] += 1
                ins.then_inc(pool_link, 1)
                pool.wait_ge(pool_link, links[0])

            pool.memset(identf[:, :], 0.0).then_inc(pool_link, 1)
            pool.memset(ident16[:, :], 0.0).then_inc(pool_link, 1)
            links[0] = 2
            link(pool.memset(ones16[:, :], 1.0))
            for m in (identf, ident16):
                pool.affine_select(out=m[:, :], in_=m[:, :], compare_op=ALU.not_equal, fill=1.0, base=0,
                                   pattern=[[-1, 128]], channel_multiplier=1).then_inc(const_ready, 1)
            pool.memset(zrow[:, :], 0.0).then_inc(const_ready, 1)
            pool.affine_select(out=before[:, :], in_=ones16[:, :], compare_op=ALU.is_gt, fill=0.0, base=0,
                               pattern=[[1, 128]], channel_multiplier=-1).then_inc(const_ready, 1)
            pool.memset(mhalf[:, :], -0.5).then_inc(const_ready, 1)
            pool.iota(rankof[:, :], pattern=[[-1, NE]], base=NE, channel_multiplier=0,
                      allow_small_or_imprecise_dtypes=True).then_inc(const_ready, 1)
            pool.iota(iotab[:, :], pattern=[[1, PR]], base=0, channel_multiplier=0,
                      allow_small_or_imprecise_dtypes=True).then_inc(const_ready, 1)
            pool.iota(pairs.bitcast(I32)[:, :, :, 0], pattern=[[T, NS], [0, TOPK]], base=0,
                      channel_multiplier=1).then_inc(const_ready, 1)
            pool.iota(btab[:, :], pattern=[[0, NPOS + 2]], base=NE, channel_multiplier=0).then_inc(const_ready, 1)
            pool.wait_ge(const_ready, 9)

            def unit_scale(u):
                e, m = UNITS[u]
                at = slice(3 * e + m, 3 * e + m + 1)
                q = slice(u % 2, u % 2 + 1)
                pool.wait_ge(w_amax, u + 1)
                link(pool.partition_all_reduce(amaxall[:, q], bits[:, q], 128, bass.bass_isa.ReduceOp.max))
                link(pool.tensor_scalar(amaxall.bitcast(I32)[:, q], amaxall.bitcast(I32)[:, q],
                                        float(40 << 23), -1.0, ALU.max, ALU.mult))
                pool.tensor_scalar(wscale[:, at].bitcast(I32), amaxall.bitcast(I32)[:, q], float(268 << 23), None,
                                   ALU.add).then_inc(w_scale, 1)
                pool.tensor_scalar(winv[:, at].bitcast(I32), amaxall.bitcast(I32)[:, q], -1.0,
                                   float((254 - 268) << 23), ALU.mult, ALU.add).then_inc(w_inv, 1)

            def unit_lo(u):
                e, m = UNITS[u]
                if m:
                    return
                at = w_at(e, m)
                src = stage[:, u % NST, 0:2 * FI]
                pool.wait_ge(w_hi, u + 1)
                link(pool.tensor_scalar(src, src, wscale[:, 3 * e + m:3 * e + m + 1], 0.0, ALU.mult, ALU.add))
                link(pool.tensor_tensor(W16[:, at + 2 * FI:at + 3 * FI], src[:, 0:FI], W16[:, at:at + FI], ALU.subtract))
                tail = W16[64:128, at + FI:at + 2 * FI]
                pool.tensor_tensor(tail, src[64:128, FI:2 * FI], tail, ALU.subtract).then_inc(w_lo, 1)
                pool.wait_ge(w_lo, u // 3 + 1)

            def unit(u):
                unit_scale(u)
                if u >= 1:
                    unit_lo(u - 1)

            def rstd(mv, r, ready, done, g):
                pool.wait_ge(ready, g + 1)
                link(pool.tensor_scalar(r[0:T, :], mv[0:T, :].rearrange("p (g k) -> p g k", k=2)[:, :, 1],
                                        1.0, EPS, ALU.mult, ALU.add))
                pool.tensor_tensor(r[0:T, :], r[0:T, :], mhalf[0:T, :], ALU.pow).then_inc(done, 1)

            patches_apart(pool, pool.tensor_copy, 0, 2)
            unit(0)
            unit(1)
            patches_apart(pool, pool.tensor_copy, 1, 2)
            unit(2)
            unit(3)
            for g in range(2):
                rstd(mv1, rstd1, mv1_ready, rstd1_ready, g)
                unit(4 + g)
            for g in range(NG + 2):
                units = list(units_at(g)) if g < NG else []
                if 0 <= g - 2:
                    rstd(mv2, rstd2, mv2_ready, rstd2_ready, g - 2)
                if g + 2 < NG:
                    rstd(mv1, rstd1, mv1_ready, rstd1_ready, g + 2)
                for u in units[:1]:
                    unit(u)
                if g >= 2:
                    pool.wait_ge(hi_ready, g - 1)
                    pool.tensor_tensor(rows[0:T, :, D:2 * D], xs[0:T, g % 2, :, :], rows[0:T, :, 0:D],
                                       ALU.subtract).then_inc(lo_ready, 1)
                for u in units[1:]:
                    unit(u)
            pool.wait_ge(slots_ready, 1)
            pool.wait_ge(idz_out, 16)
            for t in range(NS):
                for k in range(TOPK):
                    pool.indirect_dma_start(out=slot_table, out_offset=IO(pidx.bitcast(U32)[0:T, k, t:t + 1], 0),
                                            in_=pairs.bitcast(I32)[0:T, t, k, :], in_offset=None).then_inc(ids_out, 16)
            pool.wait_ge(ids_out, 16 * NS * TOPK)
            pool.dma_start(ids.bitcast(I32), slot_table.rearrange("(p b) a -> p b a", p=128)).then_inc(ids_in, 16)
            pool.wait_ge(ids_in, 16)
            for k in range(2):
                pool.wait_ge(rows_out[k], 16 * (NG // 2))
            pool.wait_ge(zero_out, 16 * ZERO_DMAS)

            def gather_rows(c, i=0):
                q = c % 2
                pool.wait_ge(xt_full, c - 1 + 2 * i)
                pool.tensor_copy(gidx[:, SUB * q:SUB * (q + 1)],
                                 ids.bitcast(U32)[:, ds(SUB * (c - PA) + 2 * SUB * i, SUB), 0]).then_inc(gidx_ready, 1)
                pool.compute_val(c - PA + 1 + 2 * i)
                pool.wait_ge(ids_in, 16)
                pool.wait_ge(gidx_ready, c - PA + 1 + 2 * i)
                for u in range(SUB):
                    pool.indirect_dma_start(out=xrow[:, q, u, :], out_offset=None, in_=xrows,
                                            in_offset=IO(gidx[:, SUB * q + u:SUB * q + u + 1], 0)
                                            ).then_inc(xrow_got[q], 16)

            with pool.Fori(0, PR // 2) as i:
                for s in range(2):
                    gather_rows(PA + s, i)
            for u in range(SUB):
                pool.wait_ge(xt_full, PA + PR - 1)
                pool.dma_start(xrow[:, (PA + PR) % 2, u, :], xrows[(PA * SUB + u) * 128:(PA * SUB + u + 1) * 128, :]
                               ).then_inc(xrow_got[(PA + PR) % 2], 16)
            pool.wait_ge(y_out[0], 16 * ((PA + PR + 1) // 2))
            pool.wait_ge(y_out[1], 16 * ((PA + PR) // 2))
            for first, last in ((0, 2), (2, 4), (4, 5), (5, 6), (6, 7), (7, 8)):
                pool.wait_ge(shared_added, last)
                for n in range(TOPK):
                    if n == 1:
                        pool.wait_ge(first_added, 16 * G * last)
                    for t in range(G * first, G * last):
                        pool.indirect_dma_start(out=h[0:T, t, :], out_offset=None, in_=yrouted,
                                                in_offset=IO(slots.bitcast(U32)[0:T, n, t:t + 1], 0),
                                                compute_op=ALU.add).then_inc(second_added[t // G] if n else first_added, 16)

        def use_ready(eng, kind, g):
            eng.wait_ge(tr_full, TRNO[kind, g] + 1)
            return 5 + TRNO[kind, g] % 3

        @block.scalar
        def _(act):
            def unit_hi(u):
                e, m = UNITS[u]
                act.wait_ge(w_scale, u + 1)
                n = UCOLS[m]
                at = w_at(e, m)
                act.activation(W16[:, at:at + n], stage[:, u % NST, 0:n], ACT.Copy,
                               scale=wscale[:, 3 * e + m:3 * e + m + 1]).then_inc(w_hi, 1)

            def patch_evac(n):
                f, k, w3 = n // (2 * KC), n % (2 * KC) // 2, n % 2
                act.wait_ge(patch_t, n + 1)
                dst = patchT[:, k, f * HALF * NP:(f + 1) * HALF * NP].rearrange("p (r w) -> p w r", w=SIDE)
                act.activation(dst[:, 3 * w3:3 * w3 + 3, :],
                               banks[:, 0, 0:3 * SIDE * HALF].rearrange("p (w r) -> p w r", w=3),
                               ACT.Copy).then_inc(patch_a, 1)

            def tok_evac(q):
                act.wait_ge(emb_done, 2 * q + 1)
                if q >= 2:
                    act.wait_ge(tok_t, 4 * (q - 1))
                act.activation(tokT[:, q % 2, 0, :], banks[:, 3 + 2 * (q % 2), 0:EQ * NP], ACT.Copy).then_inc(tok_a, 1)

            act.preload_act_table(ACT.Exp)
            patches_apart(act, act.copy, 0, 1)
            for n in range(0, NPT // 2, 2):
                patch_evac(n)
            unit_hi(0)
            unit_hi(1)
            tok_evac(0)
            tok_evac(1)
            patches_apart(act, act.copy, 1, 1)
            for n in range(NPT // 2, NPT, 2):
                patch_evac(n)
            unit_hi(2)
            unit_hi(3)
            tok_evac(2)
            tok_evac(3)
            act.wait_ge(wq_in, 16 * 7)
            act.mul(bqs[:, 0:1], bq[:, 0:1], SCALE).then_inc(act_link, 1)
            act.mul(bqs[0:DT, 1:2], bq[0:DT, 1:2], SCALE).then_inc(act_link, 1)
            act.wait_ge(act_link, 2)
            unit_hi(4)
            unit_hi(5)

            def xn_evac(g):
                if g >= 1:
                    act.wait_ge(vc_full, VCNO["v", g - 1, 1] + 1)
                bank = use_ready(act, "xm", g)
                act.activation(xnT[:, 0, :], banks[:, bank, 0:G * T], ACT.Copy).then_inc(tr_free, 1)
                bank = use_ready(act, "xt", g)
                act.activation(xnT[0:DT, 1, :], banks[0:DT, bank, 0:G * T], ACT.Copy).then_inc(tr_free, 1)

            xn_evac(0)
            for g in range(NG + 3):
                units = list(units_at(g)) if g < NG else []
                if g < NG:
                    if g >= 1:
                        act.wait_ge(s_full, g)
                    for m in range(4):
                        if m == 2 and g >= 1:
                            for u in units_at(g - 1)[2:]:
                                unit_hi(u)
                        act.wait_ge(qk_full, 4 * g + m + 1)
                        n = DT if m % 2 else DM
                        if m < 2:
                            act.activation(qk[0:n, m, :], banks[0:n, m % 2, 0:G * T], ACT.Identity, scale=SCALE,
                                           bias=bqs[0:n, m:m + 1]).then_inc(qk_free, 1)
                        else:
                            act.activation(qk[0:n, m, :], banks[0:n, m % 2, 0:G * T], ACT.Identity,
                                           bias=bq[0:n, m:m + 1]).then_inc(qk_free, 1)
                elif g == NG:
                    for u in units_at(g - 1)[2:]:
                        unit_hi(u)
                if g >= 3:
                    bank = use_ready(act, "gate", g - 3)
                    act.activation(logits[0:T, (g - 3) * G * NE:(g - 2) * G * NE], banks[0:T, bank, 0:G * NE],
                                   ACT.Copy, scale=1.0 / XSC).then_inc(tr_free, 1)
                if 2 <= g < NG + 2:
                    act.wait_ge(xs_ready, g - 1)
                    if g >= 3:
                        act.wait_ge(rows_out[(g - 3) % 2], 16 * ((g - 3) // 2 + 1))
                    act.activation(rows[0:T, :, 0:D], xs[0:T, g % 2, :, :], ACT.Copy).then_inc(hi_ready, 1)
                if units:
                    unit_hi(units[0])
                if g + 1 < NG:
                    xn_evac(g + 1)
                if 1 <= g <= NG:
                    bank = use_ready(act, "p", g - 1)
                    if g >= 2:
                        act.wait_ge(vc_full, VCNO["c", g - 2, 1] + 1)
                    act.activation(probT[0:T, :], banks[0:T, bank, 0:G * T], ACT.Copy).then_inc(tr_free, 1)
                if units[1:2]:
                    unit_hi(units[1])
                if g < NG:
                    act.wait_ge(max_ready, g + 1)
                    for s in range(G):
                        act.activation(prob[0:T, s * T:(s + 1) * T], banks[0:T, 4, s * T:(s + 1) * T], ACT.Exp,
                                       bias=negmax[0:T, s:s + 1],
                                       accum_out=rowsum[0:T, G * (g % 2) + s:G * (g % 2) + s + 1]).then_inc(exp_done, 1)
                if 2 <= g < NG + 2:
                    bank = use_ready(act, "sm", g - 2)
                    act.activation(xsT[:, 0, :], banks[:, bank, 0:G * T], ACT.Copy).then_inc(tr_free, 1)
                    bank = use_ready(act, "st", g - 2)
                    act.activation(xsT[0:DT, 1, :], banks[0:DT, bank, 0:G * T], ACT.Copy).then_inc(tr_free, 1)

            act.wait_ge(e_abs, 1)
            act.activation(rt[1][0:T, :], rt[0][0:T, :], ACT.Exp).then_inc(e_exp, 1)
            act.preload_act_table(ACT.Silu)

            def xt_evac(c, i=0):
                act.wait_ge(xt_full, c + 1 + 2 * i)
                act.activation(xT[:, c % 2, :, :], banks[:, 6 + c % 2, :].bitcast(F16)
                               .rearrange("p (k c) -> p k c", k=4), ACT.Copy).then_inc(xt_ready, 1)

            def y_evac(c, i=0):
                act.wait_ge(y_full, c + 1 + 2 * i)
                if c >= 2:
                    act.wait_ge(y_out[c % 2], 16 * (c // 2 + i))
                for u in range(SUB):
                    act.activation(ysb[:, c % 2, u, :], banks[:, 4 + u, 0:D], ACT.Copy,
                                   scale=yscale[:, ds(c + 2 * i, 1), u]).then_inc(y_ready, 1)

            def step(c, i=0):
                loop = type(i) is not int
                for r in range(ND):
                    n = ND * c + r + 2 * ND * i
                    if r and loop:
                        act.compute_val(n + 1)
                        act.wait_ge(e_exp, 1)
                    act.wait_ge(gu_full, n + 1)
                    act.activation(act_s[:, n_of(c, r) % 2, :], banks[:, n_of(c, r) % 2, 0:HW_], ACT.Silu,
                                   scale=bscale[:, 0, ds(c + 2 * i, 1)]).then_inc(silu_ready, 1)
                    if r == 1 and c + 1 < NPOS:
                        xt_evac(c + 1, i)
                    if r:
                        act.wait_ge(e_exp, 1)
                    act.wait_ge(hid_ready, n + 1)
                    act.activation(hhi[:, r, :], act_h[:, n_of(c, r) % 2, :], ACT.Copy,
                                   scale=bscale[:, 3, ds(c + 2 * i, 1)]).then_inc(hhi_ready, 1)
                    if r == 1 and c >= 1:
                        y_evac(c - 1, i)

            act.wait_ge(btab_shared, 1)
            xt_evac(0)
            for c in range(4):
                step(c)
            with act.Fori(0, (PA - 4) // 2) as i:
                for s in range(2):
                    step(4 + s, i)
            act.wait_ge(btab_ready, 1)
            act.wait_ge(yscale_ready, 1)
            with act.Fori(0, PR // 2) as i:
                for s in range(2):
                    step(PA + s, i)
            with act.Fori(0, (PB - 1) // 2) as i:
                for s in range(2):
                    step(PA + PR + s, i)
            step(NPOS - 1)
            y_evac(NPOS - 1)

        @block.tensor
        def _(pe):
            pe.wait_ge(const_ready, 1)

            def patch_transposes(f):
                pe.wait_ge(x_patch, CH * (f + 1))
                for n in range(f * 2 * KC, (f + 1) * 2 * KC):
                    k, w3 = n % (2 * KC) // 2, n % 2
                    if n >= 2:
                        pe.wait_ge(patch_v if n % 2 else patch_a, n // 2)
                    for w in range(3):
                        mm = pe.transpose(banks[:, n % 2, w * SIDE * HALF:(w + 1) * SIDE * HALF],
                                          xpatch[0:SIDE * HALF, k // 2, 3 * w3 + w, k % 2 * 128:k % 2 * 128 + 128],
                                          identf[0:SIDE * HALF, 0:SIDE * HALF])
                    mm.then_inc(patch_t, 1)

            def embed(q):
                if q >= 2:
                    pe.wait_ge(tok_a, q - 1)
                    pe.wait_ge(tok_v, q - 1)
                f = q // (NQ // 2)
                pe.wait_ge(patch_a, (f + 1) * KC)
                pe.wait_ge(patch_v, (f + 1) * KC)
                for part, (n, at) in enumerate(((DM, 0), (DT, DM))):
                    for k in range(KC):
                        mm = pe.matmul(banks[0:n, 3 + 2 * (q % 2) + part, 0:EQ * NP], wemb[:, k, at:at + n],
                                       patchT[:, k, q * EQ * NP:(q + 1) * EQ * NP], start=(k == 0), stop=(k == KC - 1))
                    mm.then_inc(emb_done, 1)

            def token_transposes(q):
                pe.wait_ge(tok_a, q + 1)
                pe.wait_ge(tok_v, q + 1)
                for m in range(4 * q, 4 * q + 4):
                    if m >= 2:
                        pe.wait_ge(tok_h, m - 1)
                    bank = 2 if m % 2 else 7
                    for s in range(2):
                        col = (2 * (m % 4) + s) * NP
                        pe.transpose(banks[0:NP, bank, s * D:s * D + DM], tokT[:, q % 2, 0, col:col + NP],
                                     identf[:, :])
                        mm = pe.transpose(banks[0:NP, bank, s * D + DM:(s + 1) * D],
                                          tokT[0:DT, q % 2, 1, col:col + NP], identf[0:DT, 0:DT])
                    mm.then_inc(tok_t, 1)

            patch_transposes(0)
            pe.wait_ge(wemb_in, 16)
            embed(0)
            embed(1)
            patch_transposes(1)
            token_transposes(0)
            token_transposes(1)
            embed(2)
            embed(3)
            token_transposes(2)
            token_transposes(3)

            def use_bank(kind, g):
                n = TRNO[kind, g]
                if n >= 3:
                    pe.wait_ge(tr_free, n - 2)
                return 5 + n % 3

            def vc_bank(*use):
                n = VCNO[use]
                if n >= 2:
                    pe.wait_ge(vc_free, n - 1)
                return 2 + n % 2

            def transposes(kind, g, src, n):
                bank = use_bank(kind, g)
                for s in range(G):
                    mm = pe.transpose(banks[0:n, bank, s * T:(s + 1) * T], src(s), identf[0:T, 0:T])
                mm.then_inc(tr_full, 1)

            def xn_transposes(g):
                pe.wait_ge(xn_ready, g + 1)
                transposes("xm", g, lambda s: xn[0:T, s, 0:DM], DM)
                transposes("xt", g, lambda s: xn[0:T, s, DM:D], DT)

            pe.wait_ge(tok_h, 4 * NQ)
            xn_transposes(0)
            pe.wait_ge(wq_in, 16 * 7)
            pe.wait_ge(gate_in, 16 * 3)
            for g in range(NG + 3):
                if g < NG:
                    pe.wait_ge(tr_free, TRNO["xt", g] + 1)
                    for m in range(4):
                        n = DT if m % 2 else DM
                        at = (m // 2) * D + (DM if m % 2 else 0)
                        if 4 * g + m >= 2:
                            pe.wait_ge(qk_free, 4 * g + m - 1)
                        dst = banks[0:n, m % 2, 0:G * T]
                        pe.matmul(dst, wq_m[:, at:at + n], xnT[:, 0, :], start=True, stop=False)
                        pe.matmul(dst, wq_t[0:DT, at:at + n], xnT[0:DT, 1, :], start=False, stop=True
                                  ).then_inc(qk_full, 1)
                if g >= 3:
                    pe.wait_ge(tr_free, TRNO["st", g - 3] + 1)
                    bank = use_bank("gate", g - 3)
                    for s in range(G):
                        cols = slice(s * T, (s + 1) * T)
                        dst = banks[0:T, bank, s * NE:(s + 1) * NE]
                        pe.matmul(dst, xsT[:, 0, cols], gw_m, start=True, stop=False)
                        mm = pe.matmul(dst, xsT[0:DT, 1, cols], gw_t[0:DT, :], start=False, stop=True)
                    mm.then_inc(tr_full, 1)
                if g < NG:
                    for a in range(2):
                        bank = vc_bank("v", g, a)
                        for s in range(2):
                            c0 = (2 * a + s) * T
                            dst = banks[0:T, bank, s * D:(s + 1) * D]
                            pe.matmul(dst, xnT[:, 0, c0:c0 + T], wq_m[:, 2 * D:3 * D], start=True, stop=False)
                            mm = pe.matmul(dst, xnT[0:DT, 1, c0:c0 + T], wq_t[0:DT, 2 * D:3 * D],
                                           start=False, stop=True)
                        mm.then_inc(vc_full, 1)
                if g + 1 < NG:
                    xn_transposes(g + 1)
                if 1 <= g <= NG:
                    pe.wait_ge(exp_done, G * g)
                    transposes("p", g - 1, lambda s: prob[0:T, s * T:(s + 1) * T], T)
                if g < NG:
                    pe.wait_ge(qk_free, 4 * g + 4)
                    if g >= 1:
                        pe.wait_ge(exp_done, G * g)
                    for s in range(G):
                        cols = slice(s * T, (s + 1) * T)
                        pe.matmul(banks[0:T, 4, cols], qk[:, 0, cols], qk[:, 2, cols], start=True, stop=False)
                        mm = pe.matmul(banks[0:T, 4, cols], qk[0:DT, 1, cols], qk[0:DT, 3, cols], start=False, stop=True)
                    mm.then_inc(s_full, 1)
                if 2 <= g < NG + 2:
                    pe.wait_ge(xs_ready, g - 1)
                    transposes("sm", g - 2, lambda s: xs[0:T, g % 2, s, 0:DM], DM)
                    transposes("st", g - 2, lambda s: xs[0:T, g % 2, s, DM:D], DT)
                if 1 <= g <= NG:
                    pe.wait_ge(tr_free, TRNO["p", g - 1] + 1)
                    for a in range(2):
                        bank = vc_bank("c", g - 1, a)
                        for s in range(2):
                            b = 2 * a + s
                            mm = pe.matmul(banks[0:T, bank, s * D:(s + 1) * D], probT[0:T, b * T:(b + 1) * T],
                                           v[0:T, (g - 1) % 2, b, :], start=True, stop=True)
                        mm.then_inc(vc_full, 1)

            pe.wait_ge(mask_ready, 1)
            pe.matmul(banks[0:T, 4, 0:NR], before[0:T, 0:T], mask16[0:T, :], start=True, stop=True)
            pe.matmul(banks[:, 5, 0:NR], ones16[0:T, :], mask16[0:T, :], start=True, stop=True).then_inc(rank_done, 1)

            def row_transposes(c, i=0):
                q = c % 2
                if PA <= c <= PA + PR:
                    pe.wait_ge(xrow_got[q], 16 * SUB * ((c - PA) // 2 + 1 + i))
                else:
                    pe.wait_ge(xrow_in[q], 16 * (len([p for p in range(q, c + 1, 2) if not PA <= p <= PA + PR]) + i))
                if c >= 2:
                    pe.wait_ge(xt_ready, c - 1 + 2 * i)
                dst = banks[:, 6 + q, :].bitcast(F16)
                for u in range(SUB):
                    for k in range(2):
                        pe.transpose(dst[:, k * BW + u * 128:k * BW + (u + 1) * 128],
                                     xrow[:, q, u, k * D:k * D + DM], ident16[:, :])
                        for part in range(2):
                            at = (2 + k) * BW + u * 128
                            mm = pe.transpose(dst[64 * part:64 * part + 64, at:at + 128],
                                              xrow[:, q, u, k * D + DM:(k + 1) * D], ident16[:, :])
                mm.then_inc(xt_full, 1)

            def up_third(c, i, r, base):
                q = c % 2
                n = ND * c + r + 2 * ND * i
                if r == 0:
                    pe.wait_ge(xt_ready, c + 1 + 2 * i)
                if n_of(c, r) >= 2:
                    pe.wait_ge(hid_ready, n - 1)
                for k in range(HC):
                    for m in range(2):
                        dst = banks[:, 2 * m + n_of(c, r) % 2, k * BW:(k + 1) * BW]
                        at = base + m * WU + (HC * r + k) * 128
                        hi = W16[:, ds(at, 128)]
                        tails = W16[:, ds(at + FI, 128)]
                        lo = W16[:, ds(at + 2 * FI, 128)]
                        pe.matmul(dst, hi, xT[:, q, 0, :], start=True, stop=False)
                        pe.matmul(dst, hi, xT[:, q, 1, :], start=False, stop=False)
                        pe.matmul(dst, lo, xT[:, q, 0, :], start=False, stop=False)
                        pe.matmul(dst, tails, xT[:, q, 2, :], start=False, stop=False)
                        mm = pe.matmul(dst, tails, xT[:, q, 3, :], start=False, stop=True)
                mm.then_inc(gu_full, 1)

            def down_third(c, i, r, base):
                pe.wait_ge(hlo_ready, ND * c + r + 1 + 2 * ND * i)
                if r == 0 and c >= 1:
                    pe.wait_ge(y_ready, SUB * (c + 2 * i))
                for k in range(HC):
                    at = base + 2 * WU + (HC * r + k) * D
                    hi = W16[:, ds(at, D)]
                    lo = W16[:, ds(at + IC * D, D)]
                    first, last = r == 0 and k == 0, r == ND - 1 and k == HC - 1
                    for u in range(SUB):
                        dst = banks[:, 4 + u, 0:D]
                        cols = slice(k * BW + u * 128, k * BW + (u + 1) * 128)
                        pe.matmul(dst, hhi[:, r, cols], hi, start=first, stop=False)
                        pe.matmul(dst, hlo[:, r, cols], hi, start=False, stop=False)
                        mm = pe.matmul(dst, hhi[:, r, cols], lo, start=False, stop=last)
                if r == ND - 1:
                    mm.then_inc(y_full, 1)

            def step(c, i, up, down):
                up_third(c, i, 0, up)
                if down is not None:
                    down_third(c - 1, i, 1, down)
                up_third(c, i, 1, up)
                if c + 1 < NPOS:
                    row_transposes(c + 1, i)
                if down is not None:
                    down_third(c - 1, i, 2, down)
                up_third(c, i, 2, up)
                down_third(c, i, 0, up)

            def expert_at(p):
                return pe.value_load(btab[0:1, ds(p, 1)], min_val=0, max_val=NE) * WE

            shared = NE * WE
            pe.wait_ge(w_lo, NE + 1)
            pe.wait_ge(w32_lo, 2 * (NE + 1))
            row_transposes(0)
            step(0, 0, shared, None)
            step(1, 0, shared, shared)
            with pe.Fori(0, (PA - 4) // 2) as i:
                for s in range(2):
                    step(2 + s, i, shared, shared)
            step(PA - 2, 0, shared, shared)
            step(PA - 1, 0, shared, shared)
            pe.wait_ge(btab_ready, 1)
            with pe.Fori(0, PR // 2) as i:
                before_, here, next_ = (expert_at(PA + k + 2 * i) for k in (-1, 0, 1))
                step(PA, i, here, before_)
                step(PA + 1, i, next_, here)
            step(PA + PR, 0, shared, expert_at(PA + PR - 1))
            with pe.Fori(0, (PB - 3) // 2) as i:
                for s in range(2):
                    step(PA + PR + 1 + s, i, shared, shared)
            step(NPOS - 2, 0, shared, shared)
            step(NPOS - 1, 0, shared, shared)
            down_third(NPOS - 1, 0, 1, shared)
            down_third(NPOS - 1, 0, 2, shared)

        @block.vector
        def _(dve):
            links = [0]

            def link(ins):
                links[0] += 1
                ins.then_inc(dve_link, 1)
                dve.wait_ge(dve_link, links[0])

            def unit(u):
                e, m = UNITS[u]
                q = slice(u % 2, u % 2 + 1)
                dve.wait_ge(stage_in[u % NST], stage_full(u))
                link(dve.tensor_reduce(amax[:, q], stage[:, u % NST, 0:UCOLS[m]], axis=AX.X, op=ALU.max,
                                       apply_absolute_value=True))
                if u >= 2:
                    dve.wait_ge(w_scale, u - 1)
                dve.tensor_scalar(bits.bitcast(I32)[:, q], amax.bitcast(I32)[:, q], 0x7F800000, None,
                                  ALU.bitwise_and).then_inc(w_amax, 1)
                if m != 1 and u:
                    unit_lo(u - 1)

            def unit_lo(u):
                e, m = UNITS[u]
                at, n = w_at(e, m), FI if m == 1 else IC * D
                scale = wscale[:, 3 * e + m:3 * e + m + 1]
                dve.wait_ge(w_hi, u + 1)
                last = dve.scalar_tensor_tensor(W16[:, at + 2 * FI:at + 3 * FI] if m == 1 else W16[:, at + n:at + 2 * n],
                                                stage[:, u % NST, 0:n], scale, W16[:, at:at + n],
                                                ALU.mult, ALU.subtract)
                if m == 1:
                    tail = W16[64:128, at + FI:at + 2 * FI]
                    last = dve.scalar_tensor_tensor(tail, stage[64:128, u % NST, FI:2 * FI], scale[64:128, :], tail,
                                                    ALU.mult, ALU.subtract)
                last.then_inc(w32_lo, 1)

            def patch_evac(n):
                f, k, w3 = n // (2 * KC), n % (2 * KC) // 2, n % 2
                dve.wait_ge(patch_t, n + 1)
                dst = patchT[:, k, f * HALF * NP:(f + 1) * HALF * NP].rearrange("p (r w) -> p w r", w=SIDE)
                dve.tensor_copy(dst[:, 3 * w3:3 * w3 + 3, :],
                                banks[:, 1, 0:3 * SIDE * HALF].rearrange("p (w r) -> p w r", w=3)).then_inc(patch_v, 1)

            def tok_evac(q):
                dve.wait_ge(emb_done, 2 * q + 2)
                if q >= 2:
                    dve.wait_ge(tok_t, 4 * (q - 1))
                dve.tensor_copy(tokT[0:DT, q % 2, 1, :], banks[0:DT, 4 + 2 * (q % 2), 0:EQ * NP]).then_inc(tok_v, 1)

            def tok_add(q):
                for m in range(4 * q, 4 * q + 4):
                    dve.wait_ge(tok_t, m + 1)
                    dve.tensor_tensor(h[0:NP, 2 * m:2 * m + 2, :],
                                      banks[0:NP, 2 if m % 2 else 7, 0:2 * D].rearrange("p (s d) -> p s d", s=2),
                                      posb[0:NP, :].unsqueeze(1).to_broadcast([NP, 2, D]), ALU.add).then_inc(tok_h, 1)

            dve.wait_ge(pos_in, 64)
            dve.tensor_tensor(row0[0:1, 2 * D:3 * D], row0[0:1, 0:D], row0[0:1, D:2 * D], ALU.add).then_inc(cls_sum, 1)
            dve.tensor_tensor(posb[0:NP, :], posb[0:NP, :], bembb[0:NP, :], ALU.add).then_inc(pos_sum, 1)
            patches_apart(dve, dve.tensor_copy, 0, 0)
            for n in range(1, NPT // 2, 2):
                patch_evac(n)
            unit(0)
            unit(1)
            tok_evac(0)
            tok_evac(1)
            patches_apart(dve, dve.tensor_copy, 1, 0)
            for n in range(NPT // 2 + 1, NPT, 2):
                patch_evac(n)
            unit(2)
            dve.wait_ge(pos_sum, 1)
            tok_add(0)
            tok_add(1)
            unit(3)
            tok_evac(2)
            tok_evac(3)
            tok_add(2)
            tok_add(3)
            dve.wait_ge(tok_h, 4 * NQ)

            def group_stats(g, mv, ready):
                at = 0 if mv is mv1 else 6 * G
                for s in range(G):
                    dve.bn_stats(stats[0:T, at + 6 * s:at + 6 * s + 6], h[0:T, G * g + s, :]).then_inc(dve_link, 1)
                links[0] += G
                dve.wait_ge(dve_link, links[0])
                for s in range(G):
                    dve.bn_aggr(mv[0:T, 2 * s:2 * s + 2], stats[0:T, at + 6 * s:at + 6 * s + 6]).then_inc(ready, 1) if s == G - 1 \
                        else dve.bn_aggr(mv[0:T, 2 * s:2 * s + 2], stats[0:T, at + 6 * s:at + 6 * s + 6])

            def normalise(g, dst, mv, rstd):
                for s in range(G):
                    last = dve.tensor_scalar(dst(s), h[0:T, G * g + s, :], mv[0:T, 2 * s:2 * s + 1],
                                             rstd[0:T, s:s + 1], ALU.subtract, ALU.mult)
                return last

            def xn_group(g):
                dve.wait_ge(rstd1_ready, g + 1)
                if g >= 1:
                    dve.wait_ge(tr_full, TRNO["xt", g - 1] + 1)
                normalise(g, lambda s: xn[0:T, s, :], mv1, rstd1).then_inc(xn_ready, 1)

            dve.wait_ge(txt_in, 16)
            dve.wait_ge(cls_row, 16)
            group_stats(0, mv1, mv1_ready)
            unit(4)
            xn_group(0)
            group_stats(1, mv1, mv1_ready)
            unit(5)

            dve.wait_ge(wq_in, 16 * 7)
            for g in range(NG + 2):
                units = list(units_at(g)) if g < NG else []
                if g + 1 < NG:
                    xn_group(g + 1)
                if g + 2 < NG:
                    group_stats(g + 2, mv1, mv1_ready)
                if 2 <= g:
                    dve.wait_ge(rstd2_ready, g - 1)
                    link(dve.tensor_scalar(rstdx[0:T, :], rstd2[0:T, :], XSC, None, ALU.mult))
                    if g >= 4:
                        dve.wait_ge(lo_ready, g - 3)
                        dve.wait_ge(tr_full, TRNO["st", g - 4] + 1)
                    normalise(g - 2, lambda s: xs[0:T, g % 2, s, :], mv2, rstdx).then_inc(xs_ready, 1)
                for u in units[:1]:
                    unit(u)
                if g < NG:
                    for a in range(2):
                        n = VCNO["v", g, a]
                        dve.wait_ge(vc_full, n + 1)
                        dve.tensor_tensor(v[0:T, g % 2, 2 * a:2 * a + 2, :],
                                          banks[0:T, 2 + n % 2, 0:2 * D].rearrange("p (s d) -> p s d", s=2),
                                          bv[0:T, :].unsqueeze(1).to_broadcast([T, 2, D]), ALU.add).then_inc(vc_free, 1)
                for u in units[1:2]:
                    unit(u)
                if g < NG:
                    dve.wait_ge(s_full, g + 1)
                    dve.tensor_reduce(negmax[0:T, :], banks[0:T, 4, 0:G * T].rearrange("p (s k) -> p s k", s=G),
                                      axis=AX.X, op=ALU.max, negate=True).then_inc(max_ready, 1)
                for u in units[2:]:
                    unit(u)
                if 1 <= g <= NG:
                    dve.wait_ge(exp_done, G * g)
                    r = G * ((g - 1) % 2)
                    link(dve.reciprocal(rinv[0:T, :], rowsum[0:T, r:r + G]))
                    for a in range(2):
                        n = VCNO["c", g - 1, a]
                        dve.wait_ge(vc_full, n + 1)
                        for s in range(2):
                            b = 2 * a + s
                            row = h[0:T, G * (g - 1) + b, :]
                            last = dve.scalar_tensor_tensor(row, banks[0:T, 2 + n % 2, s * D:(s + 1) * D],
                                                            rinv[0:T, b:b + 1], row, ALU.mult, ALU.add)
                        last.then_inc(vc_free, 1)
                    dve.wait_ge(vc_free, n + 1)
                    group_stats(g - 1, mv2, mv2_ready)

            all_e = [slice(m, 3 * (NE + 1), 3) for m in range(3)]
            d5 = rt[6][:, 0:5 * (NE + 1)].rearrange("p (k e) -> p k e", k=5)
            unit_lo(NU - 1)
            dve.wait_ge(w_inv, NU)
            dve.wait_ge(lo_ready, NG)
            for k in range(2):
                dve.wait_ge(rows_out[k], 16 * (NG // 2))
            dve.tensor_scalar(d5[:, 0, :], winv[:, all_e[0]], 1.0 / XSC, None, ALU.mult)
            dve.tensor_scalar(d5[:, 1, :], wscale[:, all_e[1]], LIMIT * XSC, None, ALU.mult)
            dve.tensor_scalar(d5[:, 2, :], wscale[:, all_e[1]], -LIMIT * XSC, None, ALU.mult)
            dve.tensor_scalar(d5[:, 3, :], winv[:, all_e[1]], HSC / XSC, None, ALU.mult)
            link(dve.tensor_scalar(d5[:, 4, :], winv[:, all_e[2]], 1.0 / HSC, None, ALU.mult))
            link(dve.tensor_copy(bscale[:, :, :], d5[:, :, NE:NE + 1].to_broadcast([128, 5, NPOS + 2])))

            R = slice(0, T)
            dve.wait_ge(tr_free, len(TR))
            link(dve.tensor_scalar(rt[0][R, :], logits[R, :], -1.0, None, ALU.mult))
            dve.tensor_tensor(rt[0][R, :], rt[0][R, :], logits[R, :], ALU.min).then_inc(e_abs, 1)
            dve.wait_ge(e_exp, 1)
            link(dve.tensor_scalar(rt[2][R, :], rt[1][R, :], 2.0, None, ALU.add))
            link(dve.reciprocal(rt[2][R, :], rt[2][R, :]))
            link(dve.tensor_tensor(rt[1][R, :], rt[1][R, :], rt[2][R, :], ALU.mult))
            link(dve.tensor_tensor(rt[2][R, :], rt[1][R, :], rt[1][R, :], ALU.mult))
            link(dve.tensor_scalar(rt[3][R, :], rt[2][R, :], 1.0 / 15, None, ALU.mult))
            for k in range(6, 0, -1):
                link(dve.scalar_tensor_tensor(rt[3][R, :], rt[3][R, :], 1.0 / (2 * k + 1), rt[2][R, :],
                                              ALU.add, ALU.mult))
            link(dve.scalar_tensor_tensor(rt[3][R, :], rt[3][R, :], 1.0, rt[1][R, :], ALU.add, ALU.mult))
            link(dve.tensor_scalar(rt[0][R, :], logits[R, :], 0.0, None, ALU.max))
            link(dve.scalar_tensor_tensor(rt[0][R, :], rt[3][R, :], 2.0, rt[0][R, :], ALU.mult, ALU.add))
            link(dve.tensor_scalar(rt[1][R, :], rt[0][R, :], 1e-30, None, ALU.max))
            link(dve.tensor_scalar(rt[2].bitcast(I32)[R, :], rt[1].bitcast(I32)[R, :], -0.5, float(0x5F3759DF),
                                   ALU.mult, ALU.add))
            for _ in range(4):
                link(dve.tensor_tensor(rt[3][R, :], rt[2][R, :], rt[2][R, :], ALU.mult))
                link(dve.scalar_tensor_tensor(rt[3][R, :], rt[3][R, :], -0.5, rt[1][R, :], ALU.mult, ALU.mult))
                link(dve.scalar_tensor_tensor(rt[2][R, :], rt[3][R, :], 1.5, rt[2][R, :], ALU.add, ALU.mult))
            link(dve.tensor_tensor(rt[0][R, :], rt[0][R, :], rt[2][R, :], ALU.mult))

            def by_tile(a, n=T):
                return a[0:n, :].rearrange("p (t e) -> p t e", e=NE)

            def over_e(a):
                return a[R, :].unsqueeze(2).to_broadcast([T, NS, NE])

            def over_t(a, n=T):
                return a[0:n, :].unsqueeze(1).to_broadcast([n, NS, NE])

            scores = by_tile(rt[0])
            biased, first, second, tmp = by_tile(rt[1]), by_tile(rt[2]), by_tile(rt[3]), by_tile(rt[4])
            dve.wait_ge(gate_in, 48)
            dve.wait_ge(const_ready, 9)
            link(dve.tensor_tensor(biased, scores, over_t(gbias), ALU.add))
            for k, pick in enumerate((first, second)):
                link(dve.tensor_reduce(best[R, 0, :], biased, axis=AX.X, op=ALU.max))
                link(dve.tensor_tensor(tmp, biased, over_e(best[:, 0, :]), ALU.is_equal))
                link(dve.tensor_tensor(tmp, tmp, over_t(rankof), ALU.mult))
                link(dve.tensor_reduce(best[R, 1, :], tmp, axis=AX.X, op=ALU.max))
                link(dve.tensor_tensor(pick, tmp, over_e(best[:, 1, :]), ALU.is_equal))
                link(dve.tensor_tensor(tmp, pick, scores, ALU.mult))
                link(dve.tensor_reduce(best[R, 2 + k, :], tmp, axis=AX.X, op=ALU.add))
                if k == 0:
                    link(dve.scalar_tensor_tensor(biased, pick, -3e38, biased, ALU.mult, ALU.add))
            link(dve.tensor_tensor(best[R, 4, :], best[R, 2, :], best[R, 3, :], ALU.add))
            link(dve.tensor_scalar(best[R, 4, :], best[R, 4, :], 1e-6, None, ALU.max))
            link(dve.reciprocal(best[R, 4, :], best[R, 4, :]))
            for k in range(2):
                dve.tensor_tensor(pairs[R, :, k, 1], best[R, 2 + k, :], best[R, 4, :], ALU.mult)
            dve.tensor_tensor(mask16[R, :], rt[2][R, :], rt[3][R, :], ALU.add).then_inc(mask_ready, 1)
            dve.wait_ge(rank_done, 1)
            a, b = rt[4], rt[5]
            link(dve.tensor_copy(a, banks[:, 5, 0:NR]))
            n = 1
            while n < NS:
                dve.tensor_copy(b[:, 0:n * NE], a[:, 0:n * NE])
                link(dve.tensor_tensor(b[:, n * NE:], a[:, n * NE:], a[:, 0:(NS - n) * NE], ALU.add))
                a, b = b, a
                n *= 2
            total, nblk, end, start = small[:, 0, :], small[:, 1, :], small[:, 2, :], small[:, 3, :]
            link(dve.tensor_tensor(b, a, banks[:, 5, 0:NR], ALU.subtract))
            link(dve.tensor_scalar(total.bitcast(I32), a[:, (NS - 1) * NE:], float(BW - 1), None, ALU.add))
            link(dve.tensor_scalar(total.bitcast(I32), total.bitcast(I32), BW.bit_length() - 1, None,
                                   ALU.logical_shift_right))
            link(dve.tensor_copy(nblk, total.bitcast(I32)))
            c0, c1 = nblk, end
            n = 1
            while n < NE:
                dve.tensor_copy(c1[:, 0:n], c0[:, 0:n])
                link(dve.tensor_tensor(c1[:, n:], c0[:, n:], c0[:, 0:NE - n], ALU.add))
                c0, c1 = c1, (small[:, 4, :] if n == 1 else small[:, 5, :])
                n *= 2
            link(dve.tensor_tensor(start, c0, nblk, ALU.subtract))
            link(dve.tensor_scalar(total, start, float(BW), None, ALU.mult))
            link(dve.tensor_tensor(a[R, :], b[R, :], banks[R, 4, 0:NR], ALU.add))
            link(dve.tensor_tensor(by_tile(a), by_tile(a), over_t(total), ALU.add))
            for k, pick in enumerate((first, second)):
                link(dve.tensor_tensor(by_tile(b), by_tile(a), pick, ALU.mult))
                link(dve.tensor_reduce(best[R, 5 + k, :], by_tile(b), axis=AX.X, op=ALU.add))
            link(dve.tensor_copy(slots[R, :, :], best[R, 5:7, :]))
            link(dve.tensor_scalar(pidx[R, :, :], slots[R, :, :], 127, None, ALU.bitwise_and))
            link(dve.tensor_scalar(tmpi[R, :, :], slots[R, :, :], 7, None, ALU.logical_shift_right))
            dve.scalar_tensor_tensor(pidx[R, :, :], pidx[R, :, :], float(NSUB), tmpi[R, :, :], ALU.mult, ALU.add
                                     ).then_inc(slots_ready, 1)
            link(dve.tensor_scalar(blk[:, 0, :], iotab[:, :], start[:, 1:2], None, ALU.is_ge))
            for e in range(2, NE):
                link(dve.scalar_tensor_tensor(blk[:, 0, :], iotab[:, :], start[:, e:e + 1], blk[:, 0, :],
                                              ALU.is_ge, ALU.add))
            dve.tensor_copy(btab[:, PA:PA + PR], blk[:, 0, :])
            link(dve.memset(bscale[:, :, PA:PA + PR], 0.0))
            for e in range(NE):
                link(dve.tensor_scalar(blk[:, 1, :], blk[:, 0, :], float(e), None, ALU.is_equal))
                for k in range(5):
                    row = bscale[:, k, PA:PA + PR]
                    ins = dve.scalar_tensor_tensor(row, blk[:, 1, :], d5[:, k, e:e + 1], row, ALU.mult, ALU.add)
                    if k == 4:
                        link(ins)
            dve.tensor_copy(yscale[:, :, :], bscale[:, 4, 0:NPOS].unsqueeze(2).to_broadcast([128, NPOS, SUB])
                            ).then_inc(btab_shared, 1)
            dve.memset(best[:, 7, 0:1], 0.0).then_inc(btab_ready, 1)

            def step(c, i=0):
                for r in range(ND):
                    n = ND * c + r + 2 * ND * i
                    q = n_of(c, r) % 2
                    p = ds(c + 2 * i, 1)
                    dve.wait_ge(gu_full, n + 1)
                    dve.tensor_scalar(act_h[:, q, :], banks[:, 2 + q, 0:HW_], bscale[:, 1, p], bscale[:, 2, p],
                                      ALU.min, ALU.max).then_inc(clamp_ready, 1)
                    dve.wait_ge(silu_ready, n + 1)
                    dve.wait_ge(clamp_ready, n + 1)
                    dve.scalar_tensor_tensor(act_h[:, q, :], act_s[:, q, :], SILU_LIMIT, act_h[:, q, :],
                                             ALU.min, ALU.mult).then_inc(hid_ready, 1)
                    dve.wait_ge(hid_ready, n + 1)
                    dve.wait_ge(hhi_ready, n + 1)
                    dve.scalar_tensor_tensor(hlo[:, r, :], act_h[:, q, :], bscale[:, 3, p],
                                             hhi[:, r, :], ALU.mult, ALU.subtract).then_inc(hlo_ready, 1)

            def add_shared(j):
                dve.wait_ge(yin_in[j % 2], 16 * (j // 2 + 1))
                dve.tensor_tensor(h[R, G * j:G * j + G, :], h[R, G * j:G * j + G, :], yin[R, j % 2, :, :], ALU.add
                                  ).then_inc(shared_added, 1)

            step(0)
            step(1)
            with dve.Fori(0, (PA - 2) // 2) as i:
                for s in range(2):
                    step(2 + s, i)
            dve.wait_ge(ids_in, 16)
            dve.tensor_tensor(yscale[:, PA:PA + PR, :], bscale[:, 4, PA:PA + PR].unsqueeze(2)
                              .to_broadcast([128, PR, SUB]), ids[:, :, 1].rearrange("p (b s) -> p b s", s=SUB), ALU.mult
                              ).then_inc(yscale_ready, 1)
            with dve.Fori(0, PR // 2) as i:
                for s in range(2):
                    step(PA + s, i)
            added = 0
            for c in range(PA + PR, NPOS):
                step(c)
                while added < NG and (added < 2 or ADD_AT[added] <= c):
                    add_shared(added)
                    added += 1
            for j in range(added, NG):
                add_shared(j)
    return nc


_INS = ['x', 'txt', 'L0_tok_W_emb', 'L0_tok_b_emb', 'L0_tok_pos_embedding', 'L0_tok_cls_token', 'L0_attn_W_qkv',
        'L0_attn_b_qkv', 'L0_ffn_gate_w', 'L0_ffn_gate_bias', 'L0_ffn_w1', 'L0_ffn_w2', 'L0_ffn_w3',
        'L0_ffn_w1s', 'L0_ffn_w2s', 'L0_ffn_w3s']


def kernel(**inputs):
    import numpy as _np
    import concourse.bacc as _bacc
    from concourse import mybir as _mybir
    from concourse.bass_utils import run_bass_kernel_spmd as _run

    nc = _bacc.Bacc("TRN2", target_bir_lowering=False, num_devices=1)
    arrays, args = {}, []
    for name in _INS:
        a = _np.ascontiguousarray(inputs[name])
        arrays[f"in_{name}"] = a
        args.append(nc.dram_tensor(f"in_{name}", a.shape, _mybir.dt.from_np(a.dtype), kind="ExternalInput").ap())
    b = inputs['x'].shape[0]
    tokens = inputs['L0_tok_pos_embedding'].shape[1] + inputs['txt'].shape[1]
    d = inputs['txt'].shape[2]
    args.append(nc.dram_tensor("out", (b, tokens, d), _mybir.dt.float32, kind="ExternalOutput").ap())
    early_fusion_layer(nc, *args)
    r = _run(nc, [arrays], core_ids=[0])
    return r.results[0]["out"]
```

```python
import numpy as np
import concourse.bass as bass
from concourse import mybir
from concourse.bass import ds
from contextlib import ExitStack

F32 = mybir.dt.float32
F16 = mybir.dt.float16
I32 = mybir.dt.int32
U32 = mybir.dt.uint32
ALU = mybir.AluOpType
ACT = mybir.ActivationFunctionType
AX = mybir.AxisListType


def early_fusion_layer(nc: bass.Bass, x, txt, w_emb, b_emb, pos, cls, w_qkv, b_qkv, gate_w, gate_bias,
                       w1, w2, w3, w1s, w2s, w3s, out):
    NS, CH, IMG, _ = x.shape
    NW, D = txt.shape[1], txt.shape[2]
    PATCH = 16
    SIDE = IMG // PATCH
    NP = SIDE * SIDE
    T = NP + 1 + NW
    NE, _, FI = w1.shape
    TOPK = 2
    DM, DT = 128, D - 128
    KC = CH * PATCH * PATCH // 128
    IC = FI // 128
    EPS = 1e-5
    SCALE = float(D) ** -0.5
    LIMIT = 10.0
    SILU_LIMIT = float(LIMIT / (1.0 + np.exp(-LIMIT)))
    G = 4
    NG = NS // G
    XSC = 2.0 ** 11
    HSC = 2.0 ** 9

    BW, SUB = 256, 2
    HALF = NS // 2
    NTOK = NS * T
    PS = -(-NTOK // BW)
    PA = 13
    PB = PS - PA
    PR = (NTOK * TOPK + NE * (BW - 1)) // BW
    NPOS = PS + PR
    NSUB = PR * SUB
    ODD = PA % 2
    HEAD = 4
    RANK_STEP = 2

    xrows = nc.dram_tensor("xrows", [PS * BW, 2 * D], F16).ap()
    acc = nc.dram_tensor("acc", [PS * BW, D], F32).ap()
    JUNK = NTOK
    assert PS * BW - NTOK >= 128
    slot_table = nc.dram_tensor("slot_table", [128 * NSUB, 2], I32).ap()

    ctx = ExitStack()
    with ctx:
        def sb(name, shape, dt=F32):
            return ctx.enter_context(nc.sbuf_tensor(name, shape, dt))

        def sem(name):
            return ctx.enter_context(nc.semaphore(name))

        WU = 3 * FI
        WE = 2 * WU + 2 * IC * D
        W16 = sb("W16", [128, (NE + 1) * WE], F16)
        h = sb("h", [128, NS, D])
        identf = sb("identf", [128, 128])
        ident16 = sb("ident16", [128, 128], F16)
        before = sb("before", [128, 128], F16)
        ones16 = sb("ones16", [128, 128], F16)
        wscale = sb("wscale", [128, 3 * (NE + 1)])
        winv = sb("winv", [128, 3 * (NE + 1)])
        logits = sb("logits", [128, NS * NE])
        mhalf = sb("mhalf", [128, G])
        gbias = sb("gbias", [128, NE])
        btab = sb("btab", [128, NPOS + 2], I32)
        bscale = sb("bscale", [128, 5, NPOS + 2])
        yscale = sb("yscale", [128, NPOS, SUB])
        pairs = sb("pairs", [128, NS, TOPK, 2])

        ARENA = 13600
        arena = sb("arena", [128, ARENA])

        def carve(at, cols, dt=F32):
            words = cols if dt != F16 else (cols + 1) // 2
            ap = arena[:, at:at + words]
            assert at + words <= ARENA, (at, words, ARENA)
            return (ap if dt == F32 else ap.bitcast(dt)), at + words

        o = 0
        wq_m, o = carve(o, 3 * D)
        wq_t, o = carve(o, 3 * D)
        bv, o = carve(o, D)
        gw_m, o = carve(o, NE)
        gw_t, o = carve(o, NE)
        bq, o = carve(o, 4)
        bqs, o = carve(o, 2)
        stats, o = carve(o, 2 * 6 * G)
        mv1, o = carve(o, 2 * G)
        rstd1, o = carve(o, G)
        mv2, o = carve(o, 2 * G)
        rstd2, o = carve(o, G)
        negmax, o = carve(o, G)
        rowsum, o = carve(o, 2 * G)
        rinv, o = carve(o, G)
        rstdx, o = carve(o, G)
        amax, o = carve(o, 4)
        amaxall, o = carve(o, 4)
        bits, o = carve(o, 4)
        xnT, o = carve(o, 2 * G * T)
        qk, o = carve(o, 4 * G * T)
        v, o = carve(o, 2 * G * D)
        prob, o = carve(o, G * T)
        probT, o = carve(o, G * T)
        xs, o = carve(o, 2 * G * D)
        rows, o = carve(o, G * 2 * D, F16)
        NST = 3
        stage, o = carve(o, NST * 2 * FI)
        xnT = xnT.rearrange("p (m c) -> p m c", m=2)
        qk = qk.rearrange("p (m c) -> p m c", m=4)
        v = v.rearrange("p (r g d) -> p r g d", r=2, g=G)
        xs = xs.rearrange("p (r g d) -> p r g d", r=2, g=G)
        rows = rows.rearrange("p (g d) -> p g d", g=G)
        stage = stage.rearrange("p (r c) -> p r c", r=NST)
        xsT = sb("xsT", [128, 2, G * T])

        EMB = WE
        emb = W16[:, EMB:NE * WE].bitcast(F32)
        xin = emb[:, 0:2 * CH * PATCH * IMG].rearrange("p (f c w) -> p f c w", f=2, c=CH)
        e0 = 2 * CH * PATCH * IMG
        patchT = emb[:, e0:e0 + KC * NS * NP].rearrange("p (k c) -> p k c", k=KC)
        e0 += KC * NS * NP
        wemb = emb[:, e0:e0 + KC * D].rearrange("p (k d) -> p k d", k=KC)
        e0 += KC * D
        EQ = 8
        NQ = NS // EQ
        tokT = emb[:, e0:e0 + 2 * 2 * EQ * NP].rearrange("p (r m c) -> p r m c", r=2, m=2)
        e0 += 2 * 2 * EQ * NP
        posb = emb[:, e0:e0 + D]
        bembb = emb[:, e0 + D:e0 + 2 * D]
        row0 = emb[:, e0 + 2 * D:e0 + 5 * D]
        zrow = emb[:, e0 + 5 * D:e0 + 6 * D].bitcast(F16)
        e0 += 6 * D
        xpatch = emb[:, e0:e0 + CH * PATCH * IMG].rearrange("p (c w v) -> p c w v", c=CH, w=SIDE)
        assert e0 + CH * PATCH * IMG <= (NE * WE - EMB) // 2
        xn = emb[:, (NE * WE - EMB) // 2 - G * D:(NE * WE - EMB) // 2].rearrange("p (g d) -> p g d", g=G)

        o = 0
        NR = NS * NE
        rt = []
        for _ in range(6):
            a, o = carve(o, NR)
            rt.append(a)
        best, o = carve(o, 8 * NS)
        best = best.rearrange("p (k t) -> p k t", k=8)
        xrow, o = carve(o, 2 * SUB * 2 * D, F16)
        xT, o = carve(o, 2 * 4 * BW, F16)
        ND = 3
        HC = IC // ND
        HW_ = HC * BW
        act_s, o = carve(o, 2 * HW_)
        act_h, o = carve(o, 2 * HW_)
        hhi, o = carve(o, ND * HW_, F16)
        hlo, o = carve(o, ND * HW_, F16)
        ysb, o = carve(o, 2 * SUB * D)
        gidx, o = carve(o, 2 * SUB)
        sidx, o = carve(o, 2 * SUB)
        xrow = xrow.rearrange("p (r s c) -> p r s c", r=2, s=SUB)
        xT = xT.rearrange("p (r k c) -> p r k c", r=2, k=4)
        act_s = act_s.rearrange("p (r c) -> p r c", r=2)
        act_h = act_h.rearrange("p (r c) -> p r c", r=2)
        hhi = hhi.rearrange("p (r c) -> p r c", r=ND)
        hlo = hlo.rearrange("p (r c) -> p r c", r=ND)
        ysb = ysb.rearrange("p (r s d) -> p r s d", r=2, s=SUB)
        gidx, sidx = gidx.bitcast(U32), sidx.bitcast(U32)
        empty = bscale[:, :, :].rearrange("p k b -> p (k b)").bitcast(I32)[:, 0:2 * NSUB]
        mask16, o = carve(o, NR, F16)
        small, o = carve(o, 6 * NE)
        small = small.rearrange("p (k e) -> p k e", k=6)
        blk, o = carve(o, 2 * PR)
        blk = blk.rearrange("p (k b) -> p k b", k=2)
        ids, o = carve(o, 2 * NSUB)
        ids = ids.rearrange("p (b k) -> p b k", k=2)
        slots, o = carve(o, 2 * NS)
        slots = slots.bitcast(I32).rearrange("p (k t) -> p k t", k=2)
        pidx, o = carve(o, 2 * NS)
        pidx = pidx.bitcast(I32).rearrange("p (k t) -> p k t", k=2)
        tmpi, o = carve(o, 2 * NS)
        tmpi = tmpi.bitcast(I32).rearrange("p (k t) -> p k t", k=2)
        d5 = sb("d5", [128, 5, NE + 1])
        rankof = sb("rankof", [128, NE])
        iotab = sb("iotab", [128, PR])
        perm = sb("perm", [128, 1])

        banks = ctx.enter_context(nc.psum_tensor("banks", [128, 8, 512], F32))

        const_ready = sem("const_ready")
        wemb_in, pos_in, txt_in, wq_in, gate_in = map(sem, ("wemb_in", "pos_in", "txt_in", "wq_in", "gate_in"))
        x_in = [[sem(f"x_in{f}{c}") for c in range(CH)] for f in range(2)]
        cls_sum, cls_row, pos_sum = sem("cls_sum"), sem("cls_row"), sem("pos_sum")
        x_patch = sem("x_patch")
        patch_t, patch_a, patch_v = sem("patch_t"), sem("patch_a"), sem("patch_v")
        emb_done, tok_a, tok_v = sem("emb_done"), sem("tok_a"), sem("tok_v")
        tok_t, tok_h = sem("tok_t"), sem("tok_h")
        stage_in = [sem(f"stage_in{k}") for k in range(NST)]
        w_amax, w_scale, w_inv, w_hi, w_lo, w32_lo = map(sem, ("w_amax", "w_scale", "w_inv", "w_hi", "w_lo", "w32_lo"))
        dve_link, act_link = sem("dve_link"), sem("act_link")
        mv1_ready, rstd1_ready, xn_ready = sem("mv1_ready"), sem("rstd1_ready"), sem("xn_ready")
        mv2_ready, rstd2_ready, xs_ready = sem("mv2_ready"), sem("rstd2_ready"), sem("xs_ready")
        pool_link = sem("pool_link")
        tr_full, tr_free = sem("tr_full"), sem("tr_free")
        qk_full, qk_free = sem("qk_full"), sem("qk_free")
        vc_full, vc_free = sem("vc_full"), sem("vc_free")
        s_full, max_ready, exp_done = sem("s_full"), sem("max_ready"), sem("exp_done")
        hi_ready, lo_ready, rows_out = sem("hi_ready"), sem("lo_ready"), [sem("rows_out0"), sem("rows_out1")]
        zero_out, idz_out = sem("zero_out"), sem("idz_out")
        e_abs, e_exp, mask_ready, rank_done, slots_ready, btab_ready = map(
            sem, ("e_abs", "e_exp", "mask_ready", "rank_done", "slots_ready", "btab_ready"))
        btab_shared, rank_copied = sem("btab_shared"), sem("rank_copied")
        ids_out, ids_in = sem("ids_out"), sem("ids_in")
        xrow_in = [sem("xrow_in0"), sem("xrow_in1")]
        xrow_got = [sem("xrow_got0"), sem("xrow_got1")]
        xt_full, xt_ready = sem("xt_full"), sem("xt_ready")
        gu_full = sem("gu_full")
        silu_ready, clamp_ready, hid_ready = sem("silu_ready"), sem("clamp_ready"), sem("hid_ready")
        hhi_ready, hlo_ready = sem("hhi_ready"), sem("hlo_ready")
        y_full, y_ready = sem("y_full"), sem("y_ready")
        acc_in, y_done = [sem("acc_in0"), sem("acc_in1")], sem("y_done")
        gidx_ready, sidx_ready, yscale_ready = sem("gidx_ready"), sem("sidx_ready"), sem("yscale_ready")
        out_done = sem("out_done")

        UNITS = [(e, m) for e in [NE] + list(range(NE)) for m in range(3)]
        NU = len(UNITS)
        UCOLS = [2 * FI, 2 * FI, IC * D]
        SHARED_W = [w1s, w3s, w2s]
        ROUTED_W = [w1, w3, w2]
        UNITS_EMB = 6

        def units_at(g):
            left, groups = NU - UNITS_EMB, NG - 1
            at = [UNITS_EMB + left * min(k, groups) // groups for k in (g, g + 1)]
            return range(*at)

        def w_at(e, m):
            return e * WE + m * WU

        def stage_full(u):
            return sum(16 if UNITS[k][1] == 2 else 48 for k in range(u % NST, u + 1, NST))

        TR = [("xm", 0), ("xt", 0)]
        for g in range(NG + 3):
            if 0 <= g - 3 < NG:
                TR += [("gate", g - 3)]
            if g + 1 < NG:
                TR += [("xm", g + 1), ("xt", g + 1)]
            if 0 <= g - 1 < NG:
                TR += [("p", g - 1)]
            if 0 <= g - 2 < NG:
                TR += [("sm", g - 2), ("st", g - 2)]
        TRNO = {u: n for n, u in enumerate(TR)}

        def n_of(c, r):
            return ND * c + r

        VC = []
        for g in range(NG + 1):
            if g < NG:
                VC += [("v", g, 0), ("v", g, 1)]
            if g >= 1:
                VC += [("c", g - 1, 0), ("c", g - 1, 1)]
        VCNO = {u: n for n, u in enumerate(VC)}

        RANK_BANK = 6 + RANK_STEP % 2
        UNROLL = 6
        ZERO_DMAS = 2 * -(-(PS * BW - NTOK) // 128)
        NPT = 2 * KC * 2
        block = ctx.enter_context(nc.Block())

        @block.sync
        def _(sp):
            def load_unit(u):
                e, m = UNITS[u]
                if u >= NST:
                    sp.wait_ge(w32_lo if m else w_lo, 2 * (u // 3) - 2 + m if m else u // 3)
                src = SHARED_W[m] if e == NE else ROUTED_W[m][e]
                done = stage_in[u % NST]
                if m < 2:
                    sp.dma_start(stage[:, u % NST, 0:FI], src[0:DM, :]).then_inc(done, 16)
                    for part in range(2):
                        sp.dma_start(stage[64 * part:64 * part + 64, u % NST, FI:2 * FI], src[DM:D, :]).then_inc(done, 16)
                else:
                    sp.dma_start(stage[:, u % NST, 0:IC * D].rearrange("p (c d) -> p c d", c=IC),
                                 src.rearrange("(c p) d -> p c d", p=128)).then_inc(done, 16)

            for f in range(2):
                for c in range(CH):
                    sp.dma_start(xin[0:SIDE * HALF, f, c, :],
                                 x[f * HALF:(f + 1) * HALF, c].rearrange("b (n y) w -> b n (y w)", n=SIDE)
                                 ).then_inc(x_in[f][c], 16)
                if f == 0:
                    sp.dma_start(row0[0:1, 0:D], pos[0, 0:1, :]).then_inc(pos_in, 16)
                    sp.dma_start(row0[0:1, D:2 * D], cls[0, :, :]).then_inc(pos_in, 16)
                    sp.dma_start(posb[0:NP, :], pos[0, 1:NP + 1, :]).then_inc(pos_in, 16)
                    sp.dma_start(bembb[0:NP, :], b_emb.partition_broadcast(NP)).then_inc(pos_in, 16)
                    sp.dma_start(wemb, w_emb.rearrange("(k p) d -> p k d", p=128)).then_inc(wemb_in, 16)
                    for u in range(NST):
                        load_unit(u)
            sp.dma_start(h[NP + 1:T, :, :], txt.rearrange("b t d -> t b d")).then_inc(txt_in, 16)
            sp.dma_start(wq_m, w_qkv[0:DM, :]).then_inc(wq_in, 16)
            sp.dma_start(wq_t[0:DT, :], w_qkv[DM:D, :]).then_inc(wq_in, 16)
            sp.dma_start(bv[0:T, :], b_qkv[2 * D:3 * D].partition_broadcast(T)).then_inc(wq_in, 16)
            for k in range(2):
                b1 = b_qkv[k * D:(k + 1) * D].rearrange("(p a) -> p a", a=1)
                sp.dma_start(bq[:, 2 * k:2 * k + 1], b1[0:DM, :]).then_inc(wq_in, 16)
                sp.dma_start(bq[0:DT, 2 * k + 1:2 * k + 2], b1[DM:D, :]).then_inc(wq_in, 16)
            sp.dma_start(gw_m, gate_w[0:DM, :]).then_inc(gate_in, 16)
            sp.dma_start(gw_t[0:DT, :], gate_w[DM:D, :]).then_inc(gate_in, 16)
            sp.dma_start(gbias[0:T, :], gate_bias.partition_broadcast(T)).then_inc(gate_in, 16)
            sp.wait_ge(cls_sum, 1)
            sp.dma_start(h[NP:NP + 1, :, :], row0[0:1, 2 * D:3 * D].unsqueeze(1).to_broadcast([1, NS, D])
                         ).then_inc(cls_row, 16)
            sp.wait_ge(const_ready, 3)
            for at in range(NTOK, PS * BW, 128):
                n = min(128, PS * BW - at)
                sp.dma_start(xrows[at:at + n, :], zrow[0:n, :]).then_inc(zero_out, 16)
                sp.dma_start(acc[at:at + n, :], zrow[0:n, :].bitcast(F32)).then_inc(zero_out, 16)
            sp.wait_ge(const_ready, 11)
            sp.dma_start(slot_table.rearrange("(p b) a -> p (b a)", p=128), empty[:, :]).then_inc(idz_out, 16)
            for u in range(NST, UNITS_EMB + 1):
                load_unit(u)

            def store_rows(g):
                sp.wait_ge(hi_ready, g + 1)
                sp.wait_ge(lo_ready, g + 1)
                for tile, rows_of, done in ((rows, xrows, rows_out[g % 2]), (h[:, G * g:G * g + G, :], acc, acc_in[g % 2])):
                    dst = rows_of[G * g * T:G * (g + 1) * T, :].rearrange("(g t) d -> t g d", g=G)
                    sp.dma_start(dst[1:NP + 1], tile[0:NP, :, :]).then_inc(done, 16)
                    sp.dma_start(dst[0:1], tile[NP:NP + 1, :, :]).then_inc(done, 16)
                    sp.dma_start(dst[NP + 1:T], tile[NP + 1:T, :, :]).then_inc(done, 16)

            for g in range(NG + 2):
                if g < NG:
                    for u in units_at(g):
                        if u + 1 < NU:
                            load_unit(u + 1)
                if g >= 2:
                    store_rows(g - 2)

            for k in range(2):
                sp.wait_ge(rows_out[k], 48 * (NG // 2))
            sp.wait_ge(zero_out, 16 * ZERO_DMAS)

            def load_rows(c, i=0):
                if c >= 2:
                    sp.wait_ge(xt_full, c - 1 + 2 * i)
                at = (c - (PR if c >= PA else 0) + 2 * i) * BW
                sp.dma_start(xrow[:, c % 2, :, :], xrows[ds(at, BW), :].rearrange("(s p) d -> p s d", s=SUB)
                             ).then_inc(xrow_in[c % 2], 16)

            for c in range(4 + ODD):
                load_rows(c)
            with sp.Fori(0, (PA - 4) // 2) as i:
                for s in range(2):
                    load_rows(4 + ODD + s, i)
            for c in range(PA + PR + 1, NPOS):
                load_rows(c)
            rows_of_out = out.rearrange("b t d -> (b t) d")
            sp.wait_ge(y_done, 32 * (PA + PR))
            n = min(NTOK, PA * BW)
            sp.dma_start(rows_of_out[0:n, :], acc[0:n, :]).then_inc(out_done, 16)
            for c in range(PA + PR, NPOS):
                sp.wait_ge(y_done, 32 * (c + 1))
                first, last = (c - PR) * BW, min((c - PR + 1) * BW, NTOK)
                sp.dma_start(rows_of_out[first:last, :], acc[first:last, :]).then_inc(out_done, 16)
            sp.wait_ge(out_done, 16 * (PB + 1))

        def patches_apart(eng, copy, f, c):
            eng.wait_ge(x_in[f][c], 16)
            if f == 1:
                eng.wait_ge(patch_t, NPT // 2)
            P = SIDE * HALF
            copy(xpatch[0:P, c, :, :].rearrange("p w (y v) -> p w y v", v=PATCH),
                 xin[0:P, f, c, :].rearrange("p (y w v) -> p w y v", w=SIDE, v=PATCH)).then_inc(x_patch, 1)

        @block.gpsimd
        def _(pool):
            IO = bass.IndirectOffsetOnAxis
            links = [0]

            def link(ins):
                links[0] += 1
                ins.then_inc(pool_link, 1)
                pool.wait_ge(pool_link, links[0])

            pool.memset(identf[:, :], 0.0).then_inc(pool_link, 1)
            pool.memset(ident16[:, :], 0.0).then_inc(pool_link, 1)
            links[0] = 2
            link(pool.memset(ones16[:, :], 1.0))
            for m in (identf, ident16):
                pool.affine_select(out=m[:, :], in_=m[:, :], compare_op=ALU.not_equal, fill=1.0, base=0,
                                   pattern=[[-1, 128]], channel_multiplier=1).then_inc(const_ready, 1)
            pool.memset(zrow[:, :], 0.0).then_inc(const_ready, 1)
            pool.affine_select(out=before[:, :], in_=ones16[:, :], compare_op=ALU.is_gt, fill=0.0, base=0,
                               pattern=[[1, 128]], channel_multiplier=-1).then_inc(const_ready, 1)
            pool.memset(mhalf[:, :], -0.5).then_inc(const_ready, 1)
            pool.iota(rankof[:, :], pattern=[[-1, NE]], base=NE, channel_multiplier=0,
                      allow_small_or_imprecise_dtypes=True).then_inc(const_ready, 1)
            pool.iota(iotab[:, :], pattern=[[1, PR]], base=0, channel_multiplier=0,
                      allow_small_or_imprecise_dtypes=True).then_inc(const_ready, 1)
            pool.iota(pairs.bitcast(I32)[:, :, :, 0], pattern=[[T, NS], [0, TOPK]], base=0,
                      channel_multiplier=1).then_inc(const_ready, 1)
            link(pool.memset(perm[:, :], 0.0))
            link(pool.affine_select(out=perm[:, :], in_=perm[:, :], compare_op=ALU.is_ge, fill=1.0, base=-NP,
                                    pattern=[[0, 1]], channel_multiplier=1))
            pool.affine_select(out=perm[:, :], in_=perm[:, :], compare_op=ALU.not_equal, fill=-float(NP), base=-NP,
                               pattern=[[0, 1]], channel_multiplier=1).then_inc(const_ready, 1)
            link(pool.memset(empty[:, :], 0))
            pool.iota(empty.rearrange("p (b a) -> p b a", a=2)[:, :, 0], pattern=[[0, NSUB]], base=JUNK,
                      channel_multiplier=1).then_inc(const_ready, 1)
            pool.iota(btab[:, :], pattern=[[0, NPOS + 2]], base=NE, channel_multiplier=0).then_inc(const_ready, 1)
            pool.wait_ge(const_ready, 11)
            numbers = pairs.bitcast(I32)[:, :, :, 0]
            pool.tensor_scalar(numbers, numbers, perm[:, 0:1], 0.0, ALU.add, ALU.add).then_inc(const_ready, 1)
            pool.wait_ge(const_ready, 12)

            def unit_scale(u):
                e, m = UNITS[u]
                at = slice(3 * e + m, 3 * e + m + 1)
                q = slice(u % 2, u % 2 + 1)
                pool.wait_ge(w_amax, u + 1)
                link(pool.partition_all_reduce(amaxall[:, q], bits[:, q], 128, bass.bass_isa.ReduceOp.max))
                link(pool.tensor_scalar(amaxall.bitcast(I32)[:, q], amaxall.bitcast(I32)[:, q],
                                        float(40 << 23), -1.0, ALU.max, ALU.mult))
                pool.tensor_scalar(wscale[:, at].bitcast(I32), amaxall.bitcast(I32)[:, q], float(268 << 23), None,
                                   ALU.add).then_inc(w_scale, 1)
                pool.tensor_scalar(winv[:, at].bitcast(I32), amaxall.bitcast(I32)[:, q], -1.0,
                                   float((254 - 268) << 23), ALU.mult, ALU.add).then_inc(w_inv, 1)

            def unit_lo(u):
                e, m = UNITS[u]
                if m:
                    return
                at = w_at(e, m)
                src = stage[:, u % NST, 0:2 * FI]
                pool.wait_ge(w_hi, u + 1)
                link(pool.tensor_scalar(src, src, wscale[:, 3 * e + m:3 * e + m + 1], 0.0, ALU.mult, ALU.add))
                link(pool.tensor_tensor(W16[:, at + 2 * FI:at + 3 * FI], src[:, 0:FI], W16[:, at:at + FI], ALU.subtract))
                tail = W16[64:128, at + FI:at + 2 * FI]
                pool.tensor_tensor(tail, src[64:128, FI:2 * FI], tail, ALU.subtract).then_inc(w_lo, 1)
                pool.wait_ge(w_lo, u // 3 + 1)

            def unit(u):
                unit_scale(u)
                if u >= 1:
                    unit_lo(u - 1)

            def rstd(mv, r, ready, done, g):
                pool.wait_ge(ready, g + 1)
                link(pool.tensor_scalar(r[0:T, :], mv[0:T, :].rearrange("p (g k) -> p g k", k=2)[:, :, 1],
                                        1.0, EPS, ALU.mult, ALU.add))
                pool.tensor_tensor(r[0:T, :], r[0:T, :], mhalf[0:T, :], ALU.pow).then_inc(done, 1)

            patches_apart(pool, pool.tensor_copy, 0, 2)
            unit(0)
            unit(1)
            patches_apart(pool, pool.tensor_copy, 1, 2)
            for g in range(2):
                unit(2 + g)
                rstd(mv1, rstd1, mv1_ready, rstd1_ready, g)
            unit(4)
            unit(5)
            for g in range(NG + 2):
                units = list(units_at(g)) if g < NG else []
                if 0 <= g - 2:
                    rstd(mv2, rstd2, mv2_ready, rstd2_ready, g - 2)
                if g + 2 < NG:
                    rstd(mv1, rstd1, mv1_ready, rstd1_ready, g + 2)
                for u in units[:2]:
                    unit(u)
                if g >= 2:
                    pool.wait_ge(hi_ready, g - 1)
                    pool.tensor_tensor(rows[0:T, :, D:2 * D], xs[0:T, g % 2, :, :], rows[0:T, :, 0:D],
                                       ALU.subtract).then_inc(lo_ready, 1)
                for u in units[2:]:
                    unit(u)
            for k in range(2):
                pool.wait_ge(acc_in[k], 48 * (NG // 2))
                pool.wait_ge(rows_out[k], 48 * (NG // 2))
            pool.wait_ge(zero_out, 16 * ZERO_DMAS)

            def low_third(c, r):
                n = ND * c + r
                pool.wait_ge(hhi_ready, n + 1)
                link(pool.tensor_scalar(act_h[:, n % 2, :], act_h[:, n % 2, :], bscale[:, 3, 0:1], 0.0, ALU.mult, ALU.add))
                pool.tensor_tensor(hlo[:, r, :], act_h[:, n % 2, :], hhi[:, r, :], ALU.subtract).then_inc(hlo_ready, 1)

            def add_shared(c):
                pool.wait_ge(y_ready, SUB * (c + 1))
                if c >= 1:
                    pool.wait_ge(y_done, 32 * c)
                at = (c - (PR if c >= PA else 0)) * BW
                pool.dma_start(acc[at:at + BW, :].rearrange("(s p) d -> p s d", s=SUB), ysb[:, c % 2, :, :],
                               accum_op=ALU.add).then_inc(y_done, 32)

            def add_routed(c, i=0):
                q = c % 2
                pool.wait_ge(y_ready, SUB * (c + 1 + 2 * i))
                pool.tensor_copy(sidx[:, SUB * q:SUB * (q + 1)],
                                 ids.bitcast(U32)[:, ds(SUB * (c - PA) + 2 * SUB * i, SUB), 0]).then_inc(sidx_ready, 1)
                for u in range(SUB):
                    if u == 0:
                        pool.compute_val(c - PA + 1 + 2 * i)
                    pool.compute_val(32 * c + 16 * u + 64 * i)
                    pool.wait_ge(ids_in, 16)
                    if u == 0:
                        pool.wait_ge(sidx_ready, c - PA + 1 + 2 * i)
                    pool.wait_ge(y_done, 32 * c + 16 * u + 64 * i)
                    pool.indirect_dma_start(out=acc, out_offset=IO(sidx[:, SUB * q + u:SUB * q + u + 1], 0),
                                            in_=ysb[:, q, u, :], in_offset=None, compute_op=ALU.add
                                            ).then_inc(y_done, 16)

            def gather_rows(c, i=0):
                q = c % 2
                pool.wait_ge(xt_full, c - 1 + 2 * i)
                pool.tensor_copy(gidx[:, SUB * q:SUB * (q + 1)],
                                 ids.bitcast(U32)[:, ds(SUB * (c - PA) + 2 * SUB * i, SUB), 0]).then_inc(gidx_ready, 1)
                pool.compute_val(c - PA + 1 + 2 * i)
                pool.wait_ge(ids_in, 16)
                pool.wait_ge(gidx_ready, c - PA + 1 + 2 * i)
                for u in range(SUB):
                    pool.indirect_dma_start(out=xrow[:, q, u, :], out_offset=None, in_=xrows,
                                            in_offset=IO(gidx[:, SUB * q + u:SUB * q + u + 1], 0)
                                            ).then_inc(xrow_got[q], 16)

            pool.wait_ge(btab_shared, 1)
            for c in range(HEAD):
                for r in range(ND):
                    low_third(c, r)
                if c >= 1:
                    add_shared(c - 1)
            pool.wait_ge(slots_ready, 1)
            pool.wait_ge(idz_out, 16)
            c = HEAD - 1
            for t in range(NS):
                for k in range(TOPK):
                    pool.indirect_dma_start(out=slot_table, out_offset=IO(pidx.bitcast(U32)[0:T, k, t:t + 1], 0),
                                            in_=pairs.bitcast(I32)[0:T, t, k, :], in_offset=None).then_inc(ids_out, 16)
                if t % 4 == 3 and c < PA - 2:
                    add_shared(c)
                    c += 1
            assert c == PA - 2, c
            pool.wait_ge(ids_out, 16 * NS * TOPK)
            pool.dma_start(ids.bitcast(I32), slot_table.rearrange("(p b) a -> p b a", p=128)).then_inc(ids_in, 16)
            pool.wait_ge(ids_in, 16)
            gather_rows(PA)
            gather_rows(PA + 1)
            add_shared(PA - 2)
            gather_rows(PA + 2)
            add_shared(PA - 1)
            with pool.Fori(0, (PR - 3) // 2) as i:
                for s in range(2):
                    gather_rows(PA + 3 + s, i)
                    add_routed(PA + s, i)
            gather_rows(PA + PR - 1)
            add_routed(PA + PR - 4)
            for u in range(SUB):
                pool.wait_ge(xt_full, PA + PR - 1)
                pool.dma_start(xrow[:, (PA + PR) % 2, u, :], xrows[(PA * SUB + u) * 128:(PA * SUB + u + 1) * 128, :]
                               ).then_inc(xrow_got[(PA + PR) % 2], 16)
            for c in range(PA + PR - 3, PA + PR):
                add_routed(c)
            for c in range(PA + PR, NPOS):
                add_shared(c)

        def use_ready(eng, kind, g):
            eng.wait_ge(tr_full, TRNO[kind, g] + 1)
            return 5 + TRNO[kind, g] % 3

        @block.scalar
        def _(act):
            def unit_hi(u):
                e, m = UNITS[u]
                act.wait_ge(w_scale, u + 1)
                n = UCOLS[m]
                at = w_at(e, m)
                act.activation(W16[:, at:at + n], stage[:, u % NST, 0:n], ACT.Copy,
                               scale=wscale[:, 3 * e + m:3 * e + m + 1]).then_inc(w_hi, 1)

            def patch_evac(n):
                f, k, w3 = n // (2 * KC), n % (2 * KC) // 2, n % 2
                act.wait_ge(patch_t, n + 1)
                dst = patchT[:, k, f * HALF * NP:(f + 1) * HALF * NP].rearrange("p (r w) -> p w r", w=SIDE)
                act.activation(dst[:, 3 * w3:3 * w3 + 3, :],
                               banks[:, 0, 0:3 * SIDE * HALF].rearrange("p (w r) -> p w r", w=3),
                               ACT.Copy).then_inc(patch_a, 1)

            def tok_evac(q):
                act.wait_ge(emb_done, 2 * q + 1)
                if q >= 2:
                    act.wait_ge(tok_t, 4 * (q - 1))
                act.activation(tokT[:, q % 2, 0, :], banks[:, 3 + 2 * (q % 2), 0:EQ * NP], ACT.Copy).then_inc(tok_a, 1)

            act.preload_act_table(ACT.Exp)
            patches_apart(act, act.copy, 0, 1)
            for n in range(0, NPT // 2, 2):
                patch_evac(n)
            unit_hi(0)
            unit_hi(1)
            tok_evac(0)
            tok_evac(1)
            patches_apart(act, act.copy, 1, 1)
            for n in range(NPT // 2, NPT, 2):
                patch_evac(n)
            unit_hi(2)
            unit_hi(3)
            tok_evac(2)
            tok_evac(3)
            act.wait_ge(wq_in, 16 * 7)
            act.mul(bqs[:, 0:1], bq[:, 0:1], SCALE).then_inc(act_link, 1)
            act.mul(bqs[0:DT, 1:2], bq[0:DT, 1:2], SCALE).then_inc(act_link, 1)
            act.wait_ge(act_link, 2)

            def xn_evac(g):
                if g >= 1:
                    act.wait_ge(vc_full, VCNO["v", g - 1, 1] + 1)
                bank = use_ready(act, "xm", g)
                act.activation(xnT[:, 0, :], banks[:, bank, 0:G * T], ACT.Copy).then_inc(tr_free, 1)
                bank = use_ready(act, "xt", g)
                act.activation(xnT[0:DT, 1, :], banks[0:DT, bank, 0:G * T], ACT.Copy).then_inc(tr_free, 1)

            xn_evac(0)
            unit_hi(4)
            for g in range(NG + 3):
                units = list(units_at(g)) if g < NG else []
                if g < NG:
                    if g >= 1:
                        act.wait_ge(s_full, g)
                    for m in range(4):
                        if m == 2:
                            for u in units_at(g - 1)[2:] if g else [UNITS_EMB - 1]:
                                unit_hi(u)
                        act.wait_ge(qk_full, 4 * g + m + 1)
                        n = DT if m % 2 else DM
                        if m < 2:
                            act.activation(qk[0:n, m, :], banks[0:n, m % 2, 0:G * T], ACT.Identity, scale=SCALE,
                                           bias=bqs[0:n, m:m + 1]).then_inc(qk_free, 1)
                        else:
                            act.activation(qk[0:n, m, :], banks[0:n, m % 2, 0:G * T], ACT.Identity,
                                           bias=bq[0:n, m:m + 1]).then_inc(qk_free, 1)
                elif g == NG:
                    for u in units_at(g - 1)[2:]:
                        unit_hi(u)
                if g >= 3:
                    bank = use_ready(act, "gate", g - 3)
                    act.activation(logits[0:T, (g - 3) * G * NE:(g - 2) * G * NE], banks[0:T, bank, 0:G * NE],
                                   ACT.Copy, scale=1.0 / XSC).then_inc(tr_free, 1)
                if 2 <= g < NG + 2:
                    act.wait_ge(xs_ready, g - 1)
                    if g >= 3:
                        act.wait_ge(rows_out[(g - 3) % 2], 48 * ((g - 3) // 2 + 1))
                    act.activation(rows[0:T, :, 0:D], xs[0:T, g % 2, :, :], ACT.Copy).then_inc(hi_ready, 1)
                if units:
                    unit_hi(units[0])
                if g + 1 < NG:
                    xn_evac(g + 1)
                if 1 <= g <= NG:
                    bank = use_ready(act, "p", g - 1)
                    if g >= 2:
                        act.wait_ge(vc_full, VCNO["c", g - 2, 1] + 1)
                    act.activation(probT[0:T, :], banks[0:T, bank, 0:G * T], ACT.Copy).then_inc(tr_free, 1)
                if g < NG:
                    act.wait_ge(max_ready, g + 1)
                    for s in range(G):
                        act.activation(prob[0:T, s * T:(s + 1) * T], banks[0:T, 4, s * T:(s + 1) * T], ACT.Exp,
                                       bias=negmax[0:T, s:s + 1],
                                       accum_out=rowsum[0:T, G * (g % 2) + s:G * (g % 2) + s + 1]).then_inc(exp_done, 1)
                if units[1:2]:
                    unit_hi(units[1])
                if 2 <= g < NG + 2:
                    bank = use_ready(act, "sm", g - 2)
                    act.activation(xsT[:, 0, :], banks[:, bank, 0:G * T], ACT.Copy).then_inc(tr_free, 1)
                    bank = use_ready(act, "st", g - 2)
                    act.activation(xsT[0:DT, 1, :], banks[0:DT, bank, 0:G * T], ACT.Copy).then_inc(tr_free, 1)

            act.wait_ge(e_abs, 1)
            act.activation(rt[1][0:T, :], rt[0][0:T, :], ACT.Exp).then_inc(e_exp, 1)

            def xt_evac(c, i=0):
                act.wait_ge(xt_full, c + 1 + 2 * i)
                act.activation(xT[:, c % 2, :, :], banks[:, 6 + c % 2, :].bitcast(F16)
                               .rearrange("p (k c) -> p k c", k=4), ACT.Copy).then_inc(xt_ready, 1)

            def y_evac(c, i=0):
                act.wait_ge(y_full, c + 1 + 2 * i)
                if c >= 2:
                    act.wait_ge(y_done, 32 * (c - 1) + 64 * i)
                for u in range(SUB):
                    act.activation(ysb[:, c % 2, u, :], banks[:, 4 + u, 0:D], ACT.Copy,
                                   scale=yscale[:, ds(c + 2 * i, 1), u]).then_inc(y_ready, 1)

            def step(c, i=0):
                loop = type(i) is not int
                for r in range(ND):
                    n = ND * c + r + 2 * ND * i
                    if r and loop:
                        act.compute_val(n + 1)
                        act.wait_ge(e_exp, 1)
                    act.wait_ge(gu_full, n + 1)
                    act.activation(act_s[:, n_of(c, r) % 2, :], banks[:, n_of(c, r) % 2, 0:HW_], ACT.Silu,
                                   scale=bscale[:, 0, ds(c + 2 * i, 1)]).then_inc(silu_ready, 1)
                    if r == 1 and c + 1 < NPOS:
                        xt_evac(c + 1, i)
                    if r == 1 and c >= 1:
                        y_evac(c - 1, i)
                    if r:
                        act.wait_ge(e_exp, 1)
                    act.wait_ge(hid_ready, n + 1)
                    act.activation(hhi[:, r, :], act_h[:, n_of(c, r) % 2, :], ACT.Copy,
                                   scale=bscale[:, 3, ds(c + 2 * i, 1)]).then_inc(hhi_ready, 1)

            act.wait_ge(btab_shared, 1)
            xt_evac(0)
            act.preload_act_table(ACT.Silu)
            for c in range(4 + ODD):
                step(c)
            with act.Fori(0, (PA - 4) // 2) as i:
                for s in range(2):
                    step(4 + ODD + s, i)
            act.wait_ge(btab_ready, 1)
            act.wait_ge(yscale_ready, 1)
            with act.Fori(0, PR // 2) as i:
                for s in range(2):
                    step(PA + s, i)
            for c in range(PA + PR, NPOS):
                step(c)
            y_evac(NPOS - 1)

        @block.tensor
        def _(pe):
            pe.wait_ge(const_ready, 1)

            def patch_transposes(f):
                pe.wait_ge(x_patch, CH * (f + 1))
                for n in range(f * 2 * KC, (f + 1) * 2 * KC):
                    k, w3 = n % (2 * KC) // 2, n % 2
                    if n >= 2:
                        pe.wait_ge(patch_v if n % 2 else patch_a, n // 2)
                    for w in range(3):
                        mm = pe.transpose(banks[:, n % 2, w * SIDE * HALF:(w + 1) * SIDE * HALF],
                                          xpatch[0:SIDE * HALF, k // 2, 3 * w3 + w, k % 2 * 128:k % 2 * 128 + 128],
                                          identf[0:SIDE * HALF, 0:SIDE * HALF])
                    mm.then_inc(patch_t, 1)

            def embed(q):
                if q >= 2:
                    pe.wait_ge(tok_a, q - 1)
                    pe.wait_ge(tok_v, q - 1)
                f = q // (NQ // 2)
                pe.wait_ge(patch_a, (f + 1) * KC)
                pe.wait_ge(patch_v, (f + 1) * KC)
                for part, (n, at) in enumerate(((DM, 0), (DT, DM))):
                    for k in range(KC):
                        mm = pe.matmul(banks[0:n, 3 + 2 * (q % 2) + part, 0:EQ * NP], wemb[:, k, at:at + n],
                                       patchT[:, k, q * EQ * NP:(q + 1) * EQ * NP], start=(k == 0), stop=(k == KC - 1))
                    mm.then_inc(emb_done, 1)

            def token_transposes(q):
                pe.wait_ge(tok_a, q + 1)
                pe.wait_ge(tok_v, q + 1)
                for m in range(4 * q, 4 * q + 4):
                    if m >= 2:
                        pe.wait_ge(tok_h, m - 1)
                    bank = 2 if m % 2 else 7
                    for s in range(2):
                        col = (2 * (m % 4) + s) * NP
                        pe.transpose(banks[0:NP, bank, s * D:s * D + DM], tokT[:, q % 2, 0, col:col + NP],
                                     identf[:, :])
                        mm = pe.transpose(banks[0:NP, bank, s * D + DM:(s + 1) * D],
                                          tokT[0:DT, q % 2, 1, col:col + NP], identf[0:DT, 0:DT])
                    mm.then_inc(tok_t, 1)

            patch_transposes(0)
            pe.wait_ge(wemb_in, 16)
            embed(0)
            embed(1)
            patch_transposes(1)
            token_transposes(0)
            token_transposes(1)
            embed(2)
            embed(3)
            token_transposes(2)
            token_transposes(3)

            def use_bank(kind, g):
                n = TRNO[kind, g]
                if n >= 3:
                    pe.wait_ge(tr_free, n - 2)
                return 5 + n % 3

            def vc_bank(*use):
                n = VCNO[use]
                if n >= 2:
                    pe.wait_ge(vc_free, n - 1)
                return 2 + n % 2

            def transposes(kind, g, src, n):
                bank = use_bank(kind, g)
                for s in range(G):
                    mm = pe.transpose(banks[0:n, bank, s * T:(s + 1) * T], src(s), identf[0:T, 0:T])
                mm.then_inc(tr_full, 1)

            def xn_transposes(g):
                pe.wait_ge(xn_ready, g + 1)
                transposes("xm", g, lambda s: xn[0:T, s, 0:DM], DM)
                transposes("xt", g, lambda s: xn[0:T, s, DM:D], DT)

            pe.wait_ge(tok_h, 4 * NQ)
            xn_transposes(0)
            pe.wait_ge(wq_in, 16 * 7)
            pe.wait_ge(gate_in, 16 * 3)
            for g in range(NG + 3):
                if g < NG:
                    pe.wait_ge(tr_free, TRNO["xt", g] + 1)
                    for m in range(4):
                        n = DT if m % 2 else DM
                        at = (m // 2) * D + (DM if m % 2 else 0)
                        if 4 * g + m >= 2:
                            pe.wait_ge(qk_free, 4 * g + m - 1)
                        dst = banks[0:n, m % 2, 0:G * T]
                        pe.matmul(dst, wq_m[:, at:at + n], xnT[:, 0, :], start=True, stop=False)
                        pe.matmul(dst, wq_t[0:DT, at:at + n], xnT[0:DT, 1, :], start=False, stop=True
                                  ).then_inc(qk_full, 1)
                if g >= 3:
                    pe.wait_ge(tr_free, TRNO["st", g - 3] + 1)
                    bank = use_bank("gate", g - 3)
                    for s in range(G):
                        cols = slice(s * T, (s + 1) * T)
                        dst = banks[0:T, bank, s * NE:(s + 1) * NE]
                        pe.matmul(dst, xsT[:, 0, cols], gw_m, start=True, stop=False)
                        mm = pe.matmul(dst, xsT[0:DT, 1, cols], gw_t[0:DT, :], start=False, stop=True)
                    mm.then_inc(tr_full, 1)
                if g < NG:
                    for a in range(2):
                        bank = vc_bank("v", g, a)
                        for s in range(2):
                            c0 = (2 * a + s) * T
                            dst = banks[0:T, bank, s * D:(s + 1) * D]
                            pe.matmul(dst, xnT[:, 0, c0:c0 + T], wq_m[:, 2 * D:3 * D], start=True, stop=False)
                            mm = pe.matmul(dst, xnT[0:DT, 1, c0:c0 + T], wq_t[0:DT, 2 * D:3 * D],
                                           start=False, stop=True)
                        mm.then_inc(vc_full, 1)
                if g + 1 < NG:
                    xn_transposes(g + 1)
                if 1 <= g <= NG:
                    pe.wait_ge(exp_done, G * g)
                    transposes("p", g - 1, lambda s: prob[0:T, s * T:(s + 1) * T], T)
                if g < NG:
                    pe.wait_ge(qk_free, 4 * g + 4)
                    if g >= 1:
                        pe.wait_ge(exp_done, G * g)
                    for s in range(G):
                        cols = slice(s * T, (s + 1) * T)
                        pe.matmul(banks[0:T, 4, cols], qk[:, 0, cols], qk[:, 2, cols], start=True, stop=False)
                        mm = pe.matmul(banks[0:T, 4, cols], qk[0:DT, 1, cols], qk[0:DT, 3, cols], start=False, stop=True)
                    mm.then_inc(s_full, 1)
                if 2 <= g < NG + 2:
                    pe.wait_ge(xs_ready, g - 1)
                    transposes("sm", g - 2, lambda s: xs[0:T, g % 2, s, 0:DM], DM)
                    transposes("st", g - 2, lambda s: xs[0:T, g % 2, s, DM:D], DT)
                if 1 <= g <= NG:
                    pe.wait_ge(tr_free, TRNO["p", g - 1] + 1)
                    for a in range(2):
                        bank = vc_bank("c", g - 1, a)
                        for s in range(2):
                            b = 2 * a + s
                            mm = pe.matmul(banks[0:T, bank, s * D:(s + 1) * D], probT[0:T, b * T:(b + 1) * T],
                                           v[0:T, (g - 1) % 2, b, :], start=True, stop=True)
                        mm.then_inc(vc_full, 1)

            def row_transposes(c, i=0):
                q = c % 2
                if PA <= c <= PA + PR:
                    pe.wait_ge(xrow_got[q], 16 * SUB * ((c - PA) // 2 + 1 + i))
                else:
                    pe.wait_ge(xrow_in[q], 16 * (len([p for p in range(q, c + 1, 2) if not PA <= p <= PA + PR]) + i))
                if c >= 2:
                    pe.wait_ge(xt_ready, c - 1 + 2 * i)
                dst = banks[:, 6 + q, :].bitcast(F16)
                for u in range(SUB):
                    for k in range(2):
                        pe.transpose(dst[:, k * BW + u * 128:k * BW + (u + 1) * 128],
                                     xrow[:, q, u, k * D:k * D + DM], ident16[:, :])
                        for part in range(2):
                            at = (2 + k) * BW + u * 128
                            mm = pe.transpose(dst[64 * part:64 * part + 64, at:at + 128],
                                              xrow[:, q, u, k * D + DM:(k + 1) * D], ident16[:, :])
                mm.then_inc(xt_full, 1)

            def up_third(c, i, r, base):
                q = c % 2
                n = ND * c + r + 2 * ND * i
                if r == 0:
                    pe.wait_ge(xt_ready, c + 1 + 2 * i)
                if n_of(c, r) >= 2:
                    pe.wait_ge(hid_ready, n - 1)
                for k in range(HC):
                    for m in range(2):
                        dst = banks[:, 2 * m + n_of(c, r) % 2, k * BW:(k + 1) * BW]
                        at = base + m * WU + (HC * r + k) * 128
                        hi = W16[:, ds(at, 128)]
                        tails = W16[:, ds(at + FI, 128)]
                        lo = W16[:, ds(at + 2 * FI, 128)]
                        pe.matmul(dst, hi, xT[:, q, 0, :], start=True, stop=False)
                        pe.matmul(dst, hi, xT[:, q, 1, :], start=False, stop=False)
                        pe.matmul(dst, lo, xT[:, q, 0, :], start=False, stop=False)
                        pe.matmul(dst, tails, xT[:, q, 2, :], start=False, stop=False)
                        mm = pe.matmul(dst, tails, xT[:, q, 3, :], start=False, stop=True)
                mm.then_inc(gu_full, 1)

            def down_third(c, i, r, base):
                pe.wait_ge(hlo_ready, ND * c + r + 1 + 2 * ND * i)
                if r == 0 and c >= 1:
                    pe.wait_ge(y_ready, SUB * (c + 2 * i))
                for k in range(HC):
                    at = base + 2 * WU + (HC * r + k) * D
                    hi = W16[:, ds(at, D)]
                    lo = W16[:, ds(at + IC * D, D)]
                    first, last = r == 0 and k == 0, r == ND - 1 and k == HC - 1
                    for u in range(SUB):
                        dst = banks[:, 4 + u, 0:D]
                        cols = slice(k * BW + u * 128, k * BW + (u + 1) * 128)
                        pe.matmul(dst, hhi[:, r, cols], hi, start=first, stop=False)
                        pe.matmul(dst, hlo[:, r, cols], hi, start=False, stop=False)
                        mm = pe.matmul(dst, hhi[:, r, cols], lo, start=False, stop=last)
                if r == ND - 1:
                    mm.then_inc(y_full, 1)

            def step(c, i, up, down):
                up_third(c, i, 0, up)
                if down is not None:
                    down_third(c - 1, i, 1, down)
                up_third(c, i, 1, up)
                if c + 1 < NPOS:
                    row_transposes(c + 1, i)
                if c == RANK_STEP:
                    pe.wait_ge(mask_ready, 1)
                    pe.matmul(banks[0:T, RANK_BANK, 0:NR], before[0:T, 0:T], mask16[0:T, :], start=True, stop=True)
                    pe.matmul(banks[:, RANK_BANK, NR:2 * NR], ones16[0:T, :], mask16[0:T, :], start=True, stop=True
                              ).then_inc(rank_done, 1)
                if down is not None:
                    down_third(c - 1, i, 2, down)
                up_third(c, i, 2, up)
                down_third(c, i, 0, up)

            def expert_at(p):
                return pe.value_load(btab[0:1, ds(p, 1)], min_val=0, max_val=NE) * WE

            shared = NE * WE
            pe.wait_ge(w_lo, NE + 1)
            pe.wait_ge(w32_lo, 2 * (NE + 1))
            row_transposes(0)
            for c in range(HEAD + ODD):
                if c == RANK_STEP + 1:
                    pe.wait_ge(rank_copied, 1)
                step(c, 0, shared, shared if c else None)
            with pe.Fori(0, (PA - HEAD - 2) // 2) as i:
                for s in range(2):
                    step(HEAD + ODD + s, i, shared, shared)
            for c in range(PA - 2, PA):
                step(c, 0, shared, shared)
            pe.wait_ge(btab_ready, 1)
            with pe.Fori(0, PR // UNROLL) as j:
                i = (UNROLL // 2) * j
                down = expert_at(PA - 1 + UNROLL * j)
                for s in range(UNROLL):
                    up = expert_at(PA + s + UNROLL * j)
                    step(PA + s, i, up, down)
                    down = up
            step(PA + PR, 0, shared, expert_at(PA + PR - 1))
            for c in range(PA + PR + 1, NPOS):
                step(c, 0, shared, shared)
            down_third(NPOS - 1, 0, 1, shared)
            down_third(NPOS - 1, 0, 2, shared)

        @block.vector
        def _(dve):
            links = [0]

            def link(ins):
                links[0] += 1
                ins.then_inc(dve_link, 1)
                dve.wait_ge(dve_link, links[0])

            def unit(u):
                e, m = UNITS[u]
                q = slice(u % 2, u % 2 + 1)
                dve.wait_ge(stage_in[u % NST], stage_full(u))
                link(dve.tensor_reduce(amax[:, q], stage[:, u % NST, 0:UCOLS[m]], axis=AX.X, op=ALU.max,
                                       apply_absolute_value=True))
                if u >= 2:
                    dve.wait_ge(w_scale, u - 1)
                dve.tensor_scalar(bits.bitcast(I32)[:, q], amax.bitcast(I32)[:, q], 0x7F800000, None,
                                  ALU.bitwise_and).then_inc(w_amax, 1)
                if m != 1 and u:
                    unit_lo(u - 1)

            def unit_lo(u):
                e, m = UNITS[u]
                at, n = w_at(e, m), FI if m == 1 else IC * D
                scale = wscale[:, 3 * e + m:3 * e + m + 1]
                dve.wait_ge(w_hi, u + 1)
                last = dve.scalar_tensor_tensor(W16[:, at + 2 * FI:at + 3 * FI] if m == 1 else W16[:, at + n:at + 2 * n],
                                                stage[:, u % NST, 0:n], scale, W16[:, at:at + n],
                                                ALU.mult, ALU.subtract)
                if m == 1:
                    tail = W16[64:128, at + FI:at + 2 * FI]
                    last = dve.scalar_tensor_tensor(tail, stage[64:128, u % NST, FI:2 * FI], scale[64:128, :], tail,
                                                    ALU.mult, ALU.subtract)
                last.then_inc(w32_lo, 1)

            def group_stats(g, mv, ready):
                at = 0 if mv is mv1 else 6 * G
                for s in range(G):
                    dve.bn_stats(stats[0:T, at + 6 * s:at + 6 * s + 6], h[0:T, G * g + s, :]).then_inc(dve_link, 1)
                links[0] += G
                dve.wait_ge(dve_link, links[0])
                for s in range(G):
                    last = dve.bn_aggr(mv[0:T, 2 * s:2 * s + 2], stats[0:T, at + 6 * s:at + 6 * s + 6])
                last.then_inc(ready, 1)

            def normalise(g, dst, mv, rstd):
                for s in range(G):
                    last = dve.tensor_scalar(dst(s), h[0:T, G * g + s, :], mv[0:T, 2 * s:2 * s + 1],
                                             rstd[0:T, s:s + 1], ALU.subtract, ALU.mult)
                return last

            def xn_group(g):
                dve.wait_ge(rstd1_ready, g + 1)
                if g >= 1:
                    dve.wait_ge(tr_full, TRNO["xt", g - 1] + 1)
                normalise(g, lambda s: xn[0:T, s, :], mv1, rstd1).then_inc(xn_ready, 1)

            def patch_evac(n):
                f, k, w3 = n // (2 * KC), n % (2 * KC) // 2, n % 2
                dve.wait_ge(patch_t, n + 1)
                dst = patchT[:, k, f * HALF * NP:(f + 1) * HALF * NP].rearrange("p (r w) -> p w r", w=SIDE)
                dve.tensor_copy(dst[:, 3 * w3:3 * w3 + 3, :],
                                banks[:, 1, 0:3 * SIDE * HALF].rearrange("p (w r) -> p w r", w=3)).then_inc(patch_v, 1)

            def tok_evac(q):
                dve.wait_ge(emb_done, 2 * q + 2)
                if q >= 2:
                    dve.wait_ge(tok_t, 4 * (q - 1))
                dve.tensor_copy(tokT[0:DT, q % 2, 1, :], banks[0:DT, 4 + 2 * (q % 2), 0:EQ * NP]).then_inc(tok_v, 1)

            def tok_add(q):
                for m in range(4 * q, 4 * q + 4):
                    dve.wait_ge(tok_t, m + 1)
                    dve.tensor_tensor(h[0:NP, 2 * m:2 * m + 2, :],
                                      banks[0:NP, 2 if m % 2 else 7, 0:2 * D].rearrange("p (s d) -> p s d", s=2),
                                      posb[0:NP, :].unsqueeze(1).to_broadcast([NP, 2, D]), ALU.add).then_inc(tok_h, 1)

            dve.wait_ge(pos_in, 64)
            dve.tensor_tensor(row0[0:1, 2 * D:3 * D], row0[0:1, 0:D], row0[0:1, D:2 * D], ALU.add).then_inc(cls_sum, 1)
            dve.tensor_tensor(posb[0:NP, :], posb[0:NP, :], bembb[0:NP, :], ALU.add).then_inc(pos_sum, 1)
            patches_apart(dve, dve.tensor_copy, 0, 0)
            for n in range(1, NPT // 2, 2):
                patch_evac(n)
            unit(0)
            unit(1)
            tok_evac(0)
            tok_evac(1)
            patches_apart(dve, dve.tensor_copy, 1, 0)
            for n in range(NPT // 2 + 1, NPT, 2):
                patch_evac(n)
            unit(2)
            dve.wait_ge(pos_sum, 1)
            tok_add(0)
            dve.wait_ge(txt_in, 16)
            dve.wait_ge(cls_row, 16)
            dve.wait_ge(tok_h, 4)
            group_stats(0, mv1, mv1_ready)
            tok_add(1)
            unit(3)
            xn_group(0)
            group_stats(1, mv1, mv1_ready)
            tok_evac(2)
            tok_evac(3)
            tok_add(2)
            tok_add(3)
            dve.wait_ge(tok_h, 4 * NQ)
            unit(4)
            unit(5)
            dve.wait_ge(wq_in, 16 * 7)

            for g in range(NG + 2):
                units = list(units_at(g)) if g < NG else []
                if g + 1 < NG:
                    xn_group(g + 1)
                if g + 2 < NG:
                    group_stats(g + 2, mv1, mv1_ready)
                if 2 <= g:
                    dve.wait_ge(rstd2_ready, g - 1)
                    link(dve.tensor_scalar(rstdx[0:T, :], rstd2[0:T, :], XSC, None, ALU.mult))
                    if g >= 4:
                        dve.wait_ge(lo_ready, g - 3)
                        dve.wait_ge(tr_full, TRNO["st", g - 4] + 1)
                    normalise(g - 2, lambda s: xs[0:T, g % 2, s, :], mv2, rstdx).then_inc(xs_ready, 1)
                for u in units[:1]:
                    unit(u)
                if g < NG:
                    for a in range(2):
                        n = VCNO["v", g, a]
                        dve.wait_ge(vc_full, n + 1)
                        dve.tensor_tensor(v[0:T, g % 2, 2 * a:2 * a + 2, :],
                                          banks[0:T, 2 + n % 2, 0:2 * D].rearrange("p (s d) -> p s d", s=2),
                                          bv[0:T, :].unsqueeze(1).to_broadcast([T, 2, D]), ALU.add).then_inc(vc_free, 1)
                for u in units[1:2]:
                    unit(u)
                if g < NG:
                    dve.wait_ge(s_full, g + 1)
                    dve.tensor_reduce(negmax[0:T, :], banks[0:T, 4, 0:G * T].rearrange("p (s k) -> p s k", s=G),
                                      axis=AX.X, op=ALU.max, negate=True).then_inc(max_ready, 1)
                if 1 <= g <= NG:
                    dve.wait_ge(exp_done, G * g)
                    r = G * ((g - 1) % 2)
                    link(dve.reciprocal(rinv[0:T, :], rowsum[0:T, r:r + G]))
                    for a in range(2):
                        n = VCNO["c", g - 1, a]
                        dve.wait_ge(vc_full, n + 1)
                        for s in range(2):
                            b = 2 * a + s
                            row = h[0:T, G * (g - 1) + b, :]
                            last = dve.scalar_tensor_tensor(row, banks[0:T, 2 + n % 2, s * D:(s + 1) * D],
                                                            rinv[0:T, b:b + 1], row, ALU.mult, ALU.add)
                        last.then_inc(vc_free, 1)
                    dve.wait_ge(vc_free, n + 1)
                    group_stats(g - 1, mv2, mv2_ready)
                for u in units[2:]:
                    unit(u)
                if g == NG - 1:
                    unit_lo(NU - 1)

            dve.wait_ge(w_inv, NU)
            dve.wait_ge(idz_out, 16)
            all_e = [slice(m, 3 * (NE + 1), 3) for m in range(3)]
            dve.tensor_scalar(d5[:, 0, :], winv[:, all_e[0]], 1.0 / XSC, None, ALU.mult)
            dve.tensor_scalar(d5[:, 1, :], wscale[:, all_e[1]], LIMIT * XSC, None, ALU.mult)
            dve.tensor_scalar(d5[:, 2, :], wscale[:, all_e[1]], -LIMIT * XSC, None, ALU.mult)
            dve.tensor_scalar(d5[:, 3, :], winv[:, all_e[1]], HSC / XSC, None, ALU.mult)
            link(dve.tensor_scalar(d5[:, 4, :], winv[:, all_e[2]], 1.0 / HSC, None, ALU.mult))
            link(dve.tensor_copy(bscale[:, :, :], d5[:, :, NE:NE + 1].to_broadcast([128, 5, NPOS + 2])))
            dve.tensor_copy(yscale[:, :, :], bscale[:, 4, 0:NPOS].unsqueeze(2).to_broadcast([128, NPOS, SUB])
                            ).then_inc(btab_shared, 1)
            dve.wait_ge(tr_free, len(TR))
            R = slice(0, T)

            def by_tile(a, n=T):
                return a[0:n, :].rearrange("p (t e) -> p t e", e=NE)

            def over_e(a):
                return a[R, :].unsqueeze(2).to_broadcast([T, NS, NE])

            def over_t(a, n=T):
                return a[0:n, :].unsqueeze(1).to_broadcast([n, NS, NE])

            scores = by_tile(rt[0])
            biased, first, second, tmp = by_tile(rt[1]), by_tile(rt[2]), by_tile(rt[3]), by_tile(rt[4])
            link(dve.tensor_scalar(rt[0][R, :], logits[R, :], -1.0, None, ALU.mult))
            dve.tensor_tensor(rt[0][R, :], rt[0][R, :], logits[R, :], ALU.min).then_inc(e_abs, 1)

            def softplus_ratio():
                link(dve.tensor_scalar(rt[2][R, :], rt[1][R, :], 2.0, None, ALU.add))
                link(dve.reciprocal(rt[2][R, :], rt[2][R, :]))

            def softplus_square():
                link(dve.tensor_tensor(rt[1][R, :], rt[1][R, :], rt[2][R, :], ALU.mult))
                link(dve.tensor_tensor(rt[2][R, :], rt[1][R, :], rt[1][R, :], ALU.mult))
                link(dve.tensor_scalar(rt[3][R, :], rt[2][R, :], 1.0 / 15, None, ALU.mult))

            def softplus_series(high, low):
                for k in range(high, low - 1, -1):
                    link(dve.scalar_tensor_tensor(rt[3][R, :], rt[3][R, :], 1.0 / (2 * k + 1), rt[2][R, :],
                                                  ALU.add, ALU.mult))

            def softplus_sum():
                link(dve.scalar_tensor_tensor(rt[3][R, :], rt[3][R, :], 1.0, rt[1][R, :], ALU.add, ALU.mult))
                link(dve.tensor_scalar(rt[0][R, :], logits[R, :], 0.0, None, ALU.max))
                link(dve.scalar_tensor_tensor(rt[0][R, :], rt[3][R, :], 2.0, rt[0][R, :], ALU.mult, ALU.add))

            def root_guess():
                link(dve.tensor_scalar(rt[1][R, :], rt[0][R, :], 1e-30, None, ALU.max))
                link(dve.tensor_scalar(rt[2].bitcast(I32)[R, :], rt[1].bitcast(I32)[R, :], -0.5, float(0x5F3759DF),
                                       ALU.mult, ALU.add))

            def root_step():
                link(dve.tensor_tensor(rt[3][R, :], rt[2][R, :], rt[2][R, :], ALU.mult))
                link(dve.scalar_tensor_tensor(rt[3][R, :], rt[3][R, :], -0.5, rt[1][R, :], ALU.mult, ALU.mult))
                link(dve.scalar_tensor_tensor(rt[2][R, :], rt[3][R, :], 1.5, rt[2][R, :], ALU.add, ALU.mult))

            def root_end():
                link(dve.tensor_tensor(rt[0][R, :], rt[0][R, :], rt[2][R, :], ALU.mult))
                link(dve.tensor_tensor(biased, scores, over_t(gbias), ALU.add))

            def best_at():
                link(dve.tensor_reduce(best[R, 0, :], biased, axis=AX.X, op=ALU.max))
                link(dve.tensor_tensor(tmp, biased, over_e(best[:, 0, :]), ALU.is_equal))
                link(dve.tensor_tensor(tmp, tmp, over_t(rankof), ALU.mult))

            def best_one(pick):
                link(dve.tensor_reduce(best[R, 1, :], tmp, axis=AX.X, op=ALU.max))
                link(dve.tensor_tensor(pick, tmp, over_e(best[:, 1, :]), ALU.is_equal))

            def best_score(k, pick):
                link(dve.tensor_tensor(tmp, pick, scores, ALU.mult))
                link(dve.tensor_reduce(best[R, 2 + k, :], tmp, axis=AX.X, op=ALU.add))
                if k == 0:
                    link(dve.scalar_tensor_tensor(biased, pick, -3e38, biased, ALU.mult, ALU.add))

            def mask():
                dve.tensor_tensor(mask16[R, :], rt[2][R, :], rt[3][R, :], ALU.add).then_inc(mask_ready, 1)

            def weights():
                link(dve.tensor_tensor(best[R, 4, :], best[R, 2, :], best[R, 3, :], ALU.add))
                link(dve.tensor_scalar(best[R, 4, :], best[R, 4, :], 1e-6, None, ALU.max))
                link(dve.reciprocal(best[R, 4, :], best[R, 4, :]))
                for k in range(2):
                    ins = dve.tensor_tensor(pairs[R, :, k, 1], best[R, 2 + k, :], best[R, 4, :], ALU.mult)
                link(ins)

            def ranks():
                dve.wait_ge(rank_done, 1)
                dve.tensor_copy(rt[1][R, :], banks[R, RANK_BANK, 0:NR])
                dve.tensor_copy(rt[0], banks[:, RANK_BANK, NR:2 * NR]).then_inc(rank_copied, 1)
                dve.wait_ge(rank_copied, 1)

            sums = [rt[4], rt[5]]

            def tiles_before(first_n, last_n):
                n = first_n
                while n <= last_n:
                    a, b = (rt[0] if n == 1 else sums[0]), sums[1]
                    dve.tensor_copy(b[:, 0:n * NE], a[:, 0:n * NE])
                    link(dve.tensor_tensor(b[:, n * NE:], a[:, n * NE:], a[:, 0:(NS - n) * NE], ALU.add))
                    sums.reverse()
                    n *= 2

            total, nblk, end, start = small[:, 0, :], small[:, 1, :], small[:, 2, :], small[:, 3, :]

            def expert_blocks():
                a, b = sums
                link(dve.tensor_tensor(b, a, rt[0], ALU.subtract))
                link(dve.tensor_scalar(total.bitcast(I32), a[:, (NS - 1) * NE:], float(BW - 1), None, ALU.add))
                link(dve.tensor_scalar(total.bitcast(I32), total.bitcast(I32), BW.bit_length() - 1, None,
                                       ALU.logical_shift_right))
                link(dve.tensor_copy(nblk, total.bitcast(I32)))

            def expert_starts():
                c0, c1 = nblk, end
                n = 1
                while n < NE:
                    dve.tensor_copy(c1[:, 0:n], c0[:, 0:n])
                    link(dve.tensor_tensor(c1[:, n:], c0[:, n:], c0[:, 0:NE - n], ALU.add))
                    c0, c1 = c1, (small[:, 4, :] if n == 1 else small[:, 5, :])
                    n *= 2
                link(dve.tensor_tensor(start, c0, nblk, ALU.subtract))
                link(dve.tensor_scalar(total, start, float(BW), None, ALU.mult))

            def slots_of_experts():
                a, b = sums
                link(dve.tensor_tensor(a[R, :], b[R, :], rt[1][R, :], ALU.add))
                link(dve.tensor_tensor(by_tile(a), by_tile(a), over_t(total), ALU.add))

            def slots_of_tokens(k, pick):
                a, b = sums
                link(dve.tensor_tensor(by_tile(b), by_tile(a), pick, ALU.mult))
                link(dve.tensor_reduce(best[R, 5 + k, :], by_tile(b), axis=AX.X, op=ALU.add))

            def table_places():
                link(dve.tensor_copy(slots[R, :, :], best[R, 5:7, :]))
                link(dve.tensor_scalar(pidx[R, :, :], slots[R, :, :], 127, None, ALU.bitwise_and))
                link(dve.tensor_scalar(tmpi[R, :, :], slots[R, :, :], 7, None, ALU.logical_shift_right))
                dve.scalar_tensor_tensor(pidx[R, :, :], pidx[R, :, :], float(NSUB), tmpi[R, :, :], ALU.mult, ALU.add
                                         ).then_inc(slots_ready, 1)

            def block_experts():
                link(dve.tensor_scalar(blk[:, 0, :], iotab[:, :], start[:, 1:2], None, ALU.is_ge))
                for e in range(2, NE):
                    link(dve.scalar_tensor_tensor(blk[:, 0, :], iotab[:, :], start[:, e:e + 1], blk[:, 0, :],
                                                  ALU.is_ge, ALU.add))
                dve.tensor_copy(btab[:, PA:PA + PR], blk[:, 0, :])
                link(dve.memset(bscale[:, :, PA:PA + PR], 0.0))

            def block_scales(e):
                link(dve.tensor_scalar(blk[:, 1, :], blk[:, 0, :], float(e), None, ALU.is_equal))
                for k in range(5):
                    row = bscale[:, k, PA:PA + PR]
                    ins = dve.scalar_tensor_tensor(row, blk[:, 1, :], d5[:, k, e:e + 1], row, ALU.mult, ALU.add)
                link(ins)
                if e == NE - 1:
                    dve.memset(best[:, 7, 0:1], 0.0).then_inc(btab_ready, 1)

            def third(c, r, i=0, beside=None):
                n = ND * c + r + 2 * ND * i
                q = n_of(c, r) % 2
                p = ds(c + 2 * i, 1)
                dve.wait_ge(gu_full, n + 1)
                by_pool = ND * HEAD
                if type(n) is int and 2 <= n < by_pool + 2:
                    dve.wait_ge(hlo_ready, n - 1)
                dve.tensor_scalar(act_h[:, q, :], banks[:, 2 + q, 0:HW_], bscale[:, 1, p], bscale[:, 2, p],
                                  ALU.min, ALU.max).then_inc(clamp_ready, 1)
                dve.wait_ge(silu_ready, n + 1)
                dve.wait_ge(clamp_ready, n + 1)
                dve.scalar_tensor_tensor(act_h[:, q, :], act_s[:, q, :], SILU_LIMIT, act_h[:, q, :],
                                         ALU.min, ALU.mult).then_inc(hid_ready, 1)
                if type(n) is int and n < by_pool:
                    return
                if beside:
                    beside()
                if type(n) is int and n == by_pool:
                    dve.wait_ge(hlo_ready, n)
                dve.wait_ge(hid_ready, n + 1)
                dve.wait_ge(hhi_ready, n + 1)
                dve.scalar_tensor_tensor(hlo[:, r, :], act_h[:, q, :], bscale[:, 3, p],
                                         hhi[:, r, :], ALU.mult, ALU.subtract).then_inc(hlo_ready, 1)

            def step(c, i=0):
                for r in range(ND):
                    third(c, r, i)

            dve.wait_ge(e_exp, 1)
            dve.wait_ge(gate_in, 48)
            softplus_ratio()
            softplus_square()
            softplus_series(6, 1)
            softplus_sum()
            dve.wait_ge(lo_ready, NG)
            for k in range(2):
                dve.wait_ge(rows_out[k], 48 * (NG // 2))
                dve.wait_ge(acc_in[k], 48 * (NG // 2))
            third(0, 0)
            root_guess()
            root_step()
            third(0, 1)
            root_step()
            root_step()
            third(0, 2)
            root_end()
            best_at()
            third(1, 0)
            best_one(first)
            best_score(0, first)
            third(1, 1)
            best_at()
            best_one(second)
            third(1, 2)
            mask()
            best_score(1, second)
            third(2, 0)
            weights()
            third(2, 1)
            ranks()
            tiles_before(1, 2)
            third(2, 2)
            tiles_before(4, 16)
            expert_blocks()
            third(3, 0)
            expert_starts()
            slots_of_experts()
            third(3, 1)
            slots_of_tokens(0, first)
            slots_of_tokens(1, second)
            table_places()
            third(3, 2)
            third(HEAD, 0, beside=block_experts)
            for e in range(NE):
                third(HEAD + (e + 1) // ND, (e + 1) % ND, beside=lambda: block_scales(e))
            assert (NE + 1) % ND == 0
            for c in range(HEAD + (NE + 1) // ND, HEAD + 4 + ODD):
                step(c)
            with dve.Fori(0, (PA - HEAD - 4) // 2) as i:
                for s in range(2):
                    step(HEAD + 4 + ODD + s, i)
            dve.wait_ge(ids_in, 16)
            dve.tensor_tensor(yscale[:, PA:PA + PR, :], bscale[:, 4, PA:PA + PR].unsqueeze(2)
                              .to_broadcast([128, PR, SUB]), ids[:, :, 1].rearrange("p (b s) -> p b s", s=SUB), ALU.mult
                              ).then_inc(yscale_ready, 1)
            with dve.Fori(0, PR // 2) as i:
                for s in range(2):
                    step(PA + s, i)
            for c in range(PA + PR, NPOS):
                step(c)
    return nc


_INS = ['x', 'txt', 'L0_tok_W_emb', 'L0_tok_b_emb', 'L0_tok_pos_embedding', 'L0_tok_cls_token', 'L0_attn_W_qkv',
        'L0_attn_b_qkv', 'L0_ffn_gate_w', 'L0_ffn_gate_bias', 'L0_ffn_w1', 'L0_ffn_w2', 'L0_ffn_w3',
        'L0_ffn_w1s', 'L0_ffn_w2s', 'L0_ffn_w3s']


def kernel(**inputs):
    import numpy as _np
    import concourse.bacc as _bacc
    from concourse import mybir as _mybir
    from concourse.bass_utils import run_bass_kernel_spmd as _run

    nc = _bacc.Bacc("TRN2", target_bir_lowering=False, num_devices=1)
    arrays, args = {}, []
    for name in _INS:
        a = _np.ascontiguousarray(inputs[name])
        arrays[f"in_{name}"] = a
        args.append(nc.dram_tensor(f"in_{name}", a.shape, _mybir.dt.from_np(a.dtype), kind="ExternalInput").ap())
    b = inputs['x'].shape[0]
    tokens = inputs['L0_tok_pos_embedding'].shape[1] + inputs['txt'].shape[1]
    d = inputs['txt'].shape[2]
    args.append(nc.dram_tensor("out", (b, tokens, d), _mybir.dt.float32, kind="ExternalOutput").ap())
    early_fusion_layer(nc, *args)
    r = _run(nc, [arrays], core_ids=[0])
    return r.results[0]["out"]
```
